# Optimizing a Trainium2 kernel written in Bass

```python
import numpy as np
import jax
import jax.numpy as jnp

def _softmax(x, axis=-1):
    return jax.nn.softmax(x, axis=axis)

def _gelu(x):
    return jax.nn.gelu(x, approximate=True)

def _silu(x):
    return jax.nn.silu(x)

def _sigmoid(x):
    return jax.nn.sigmoid(x)

def _layernorm(x, axis=-1, eps=1e-05):
    m = jnp.mean(x, axis=axis, keepdims=True)
    v = jnp.var(x, axis=axis, keepdims=True)
    return (x - m) / jnp.sqrt(v + eps)

def _scatter_add(tgt, idx, src, axis=0):
    return tgt.at[idx].add(src)

def _segment_sum(src, seg, n):
    return jax.ops.segment_sum(src, seg, n)
kernel_name = 'mk_decoder_preln_d1_seqx_r4_e38f59'

def setup_inputs(seed: int=0):
    np.random.seed(seed)
    _w = jnp.asarray

    def _rec_inputs():
        import jax
        import jax.numpy as jnp
        _rk = jax.random.key(seed)
        x = 7.22e-05 + 1 * jax.random.normal(jax.random.fold_in(_rk, 1), (2, 1024, 256), jnp.float32)
        _lenS = 1024 - jax.random.randint(jax.random.fold_in(_rk, 7), (2,), 0, max(1, 1024 // 4) + 1, jnp.int32)
        _lenS2 = 154 - jax.random.randint(jax.random.fold_in(_rk, 8), (2,), 0, max(1, 154 // 4) + 1, jnp.int32)
        _ctx_1024P = jax.random.normal(jax.random.fold_in(_rk, 11), (2, 16, 256), jnp.float32)
        _ctx_1024c = jax.random.dirichlet(jax.random.fold_in(_rk, 511), 0.3 * jnp.ones((16,), jnp.float32), (2, 154))
        _ctx_1024t = jnp.einsum('bsk,bkd->bsd', _ctx_1024c, _ctx_1024P)
        _ctx_1024t = _ctx_1024t * jax.lax.rsqrt(jnp.mean(jnp.square(_ctx_1024t)) + 1e-12) * 0.953939
        ctx_1024 = 4.13588e-05 + 0.999923 * (_ctx_1024t + 0.3 * jax.random.normal(jax.random.fold_in(_rk, 611), (2, 154, 256), jnp.float32))
        _validS = jnp.arange(1024)[None, :] < _lenS[:, None]
        _validS2 = jnp.arange(154)[None, :] < _lenS2[:, None]
        _causal = jnp.tril(jnp.ones((1024, 1024), dtype=bool))
        mask_BxS2_ik0 = jnp.where(jnp.broadcast_to(_validS2[:, :], (2, 154)), 0, 1).astype(jnp.int32)
        return (x, ctx_1024, mask_BxS2_ik0)
    x, ctx_1024, mask_BxS2_ik0 = _rec_inputs()

    def _L0_attn_setup():
        import jax, jax.numpy as jnp
        import numpy as np
        D_MODEL = 256
        D_STATE = 128
        D_CONV = 4
        EXPAND = 2
        HEADDIM = 64
        D_INNER = D_MODEL * EXPAND
        NHEADS = D_INNER // HEADDIM
        CONV_DIM = D_INNER + 2 * D_STATE
        D_IN_PROJ = 2 * D_INNER + 2 * D_STATE + NHEADS
        POOL = 50
        SDIM = 64
        HEAD_DIM_RET = SDIM // 4
        TAU1 = 0.5
        TAU2 = 0.3
        HID = D_MODEL // 4
        B = 4
        T = 512
        EPS = 1e-05

        def _rmsnorm(x, w):
            return x * jax.lax.rsqrt(jnp.mean(x * x, axis=-1, keepdims=True) + EPS) * w

        def _mamba2(x, in_w, conv_w, conv_b, dt_bias, A_log, D_param, gnorm_w, out_w):
            Bn, Tn, _ = x.shape
            zxbcdt = x @ in_w.T
            z = zxbcdt[..., :D_INNER]
            xBC = zxbcdt[..., D_INNER:D_INNER + CONV_DIM]
            dt = zxbcdt[..., D_INNER + CONV_DIM:]
            xp = jnp.pad(jnp.transpose(xBC, (0, 2, 1)), ((0, 0), (0, 0), (D_CONV - 1, 0)))
            conv = jax.lax.conv_general_dilated(xp, conv_w[:, None, :], (1,), 'VALID', dimension_numbers=('NCH', 'OIH', 'NCH'), feature_group_count=CONV_DIM)
            xBC = jax.nn.silu(jnp.transpose(conv, (0, 2, 1)) + conv_b)
            xs = xBC[..., :D_INNER].reshape(Bn, Tn, NHEADS, HEADDIM)
            Bm = xBC[..., D_INNER:D_INNER + D_STATE]
            Cm = xBC[..., D_INNER + D_STATE:]
            dt = jax.nn.softplus(dt + dt_bias)
            A = -jnp.exp(A_log)
            dA = jnp.exp(dt * A)
            dtx = dt[..., None] * xs

            def step(h, inp):
                dA_t, dtx_t, B_t, C_t = inp
                h = h * dA_t[:, :, None, None] + dtx_t[..., None] * B_t[:, None, None, :]
                y = jnp.einsum('bhpn,bn->bhp', h, C_t)
                return (h, y)
            tm = lambda a: jnp.moveaxis(a, 1, 0)
            h0 = jnp.zeros((Bn, NHEADS, HEADDIM, D_STATE), x.dtype)
            _, ys = jax.lax.scan(step, h0, (tm(dA), tm(dtx), tm(Bm), tm(Cm)))
            y = jnp.moveaxis(ys, 0, 1) + D_param[None, None, :, None] * xs
            y = y.reshape(Bn, Tn, D_INNER)
            y = _rmsnorm(y * jax.nn.silu(z), gnorm_w)
            return y @ out_w.T

        def _update_memory(tokens, imp, summ_w, pool, prio, counts):
            Bn, Tn, Dm = tokens.shape
            S = min(Tn, POOL)
            order = jnp.argsort(-imp, axis=1)[:, :S]
            s_imp = jnp.take_along_axis(imp, order, axis=1)
            s_tok = jnp.take_along_axis(tokens, order[..., None], axis=1)
            s_sum = s_tok @ summ_w.T
            s_mask = s_imp > TAU1
            ar = jnp.arange(Bn)

            def body(carry, inp):
                pool, prio, counts = carry
                hi, si, ss = inp
                add = hi & (counts < POOL)
                idx = jnp.minimum(counts, POOL - 1)
                pool = pool.at[ar, idx].set(jnp.where(add[:, None], ss, pool[ar, idx]))
                prio = prio.at[ar, idx].set(jnp.where(add, si, prio[ar, idx]))
                counts = counts + add.astype(counts.dtype)
                repl = hi & (counts >= POOL)
                mi = jnp.argmin(prio, axis=1)
                should = repl & (si > prio[ar, mi])
                pool = pool.at[ar, mi].set(jnp.where(should[:, None], ss, pool[ar, mi]))
                prio = prio.at[ar, mi].set(jnp.where(should, si, prio[ar, mi]))
                return ((pool, prio, counts), None)
            xs = (jnp.moveaxis(s_mask, 1, 0), jnp.moveaxis(s_imp, 1, 0), jnp.moveaxis(s_sum, 1, 0))
            (pool, prio, counts), _ = jax.lax.scan(body, (pool, prio, counts), xs)
            return (pool, prio, counts)
        key = jax.random.key(seed)
        ks = jax.random.split(key, 16)

        def w(k, shape, fan_in):
            return jax.random.normal(k, shape, dtype=jnp.float32) / np.float32(np.sqrt(fan_in))
        inp = {}
        inp['x'] = jax.random.normal(ks[0], (B, T, D_MODEL), dtype=jnp.float32)
        inp['norm_w'] = jnp.ones((D_MODEL,), jnp.float32)
        inp['in_w'] = w(ks[1], (D_IN_PROJ, D_MODEL), D_MODEL)
        inp['conv_w'] = w(ks[2], (CONV_DIM, D_CONV), D_CONV)
        inp['conv_b'] = jnp.zeros((CONV_DIM,), jnp.float32)
        inp['dt_bias'] = jnp.log(jnp.expm1(jax.random.uniform(ks[3], (NHEADS,), minval=0.001, maxval=0.1))).astype(jnp.float32)
        inp['A_log'] = jnp.log(jax.random.uniform(ks[4], (NHEADS,), minval=1.0, maxval=16.0)).astype(jnp.float32)
        inp['D_param'] = jnp.ones((NHEADS,), jnp.float32)
        inp['gnorm_w'] = jnp.ones((D_INNER,), jnp.float32)
        inp['out_w'] = w(ks[5], (D_MODEL, D_INNER), D_INNER)
        inp['scorer_w1'] = w(ks[6], (HID, D_MODEL), D_MODEL)
        inp['scorer_w2'] = w(ks[7], (1, HID), HID)
        inp['summ_w'] = w(ks[8], (SDIM, D_MODEL), D_MODEL)
        inp['q_w'] = w(ks[9], (SDIM, D_MODEL), D_MODEL)
        inp['k_w'] = w(ks[10], (SDIM, SDIM), SDIM)
        inp['v_w'] = w(ks[11], (D_MODEL, SDIM), SDIM)
        inp['gate_w'] = w(ks[12], (D_MODEL, 2 * D_MODEL), 2 * D_MODEL)
        return inp
    _L0_attn_all = _L0_attn_setup()
    _L0_attn_in = {k: v for k, v in _L0_attn_all.items() if k in ('norm_w', 'in_w', 'conv_w', 'conv_b', 'dt_bias', 'A_log', 'D_param', 'gnorm_w', 'out_w', 'scorer_w1', 'scorer_w2', 'summ_w', 'q_w', 'k_w', 'v_w', 'gate_w')}
    del _L0_attn_all

    def _L0_xattn_setup():
        import jax, jax.numpy as jnp
        import numpy as np
        B, LQ, LK, D = (4, 512, 512, 256)
        H = 16
        HD = D // H

        def _split_heads(x):
            b, l, _ = x.shape
            return x.reshape(b, l, H, HD).transpose(0, 2, 1, 3)
        key = jax.random.key(seed)
        ks = jax.random.split(key, 10)
        s = 0.02
        return {'hidden_states': jax.random.normal(ks[0], (B, LQ, D), jnp.float32), 'context': jax.random.normal(ks[1], (B, LK, D), jnp.float32), 'attention_mask': jax.random.randint(ks[2], (B, LK), 0, 2, jnp.int32), 'q_w': jax.random.normal(ks[3], (D, D), jnp.float32) * s, 'q_b': jnp.zeros((D,), jnp.float32), 'k_w': jax.random.normal(ks[4], (D, D), jnp.float32) * s, 'k_b': jnp.zeros((D,), jnp.float32), 'v_w': jax.random.normal(ks[5], (D, D), jnp.float32) * s, 'v_b': jnp.zeros((D,), jnp.float32)}
    _L0_xattn_all = _L0_xattn_setup()
    _L0_xattn_in = {k: v for k, v in _L0_xattn_all.items() if k in ('q_w', 'q_b', 'k_w', 'k_b', 'v_w', 'v_b')}
    del _L0_xattn_all

    def _L0_ffn_setup():
        import jax, jax.numpy as jnp
        import numpy as np
        D_MODEL, D_FF, N_EXP = (256, 1024, 8)
        key = jax.random.key(seed)
        ks = jax.random.split(key, 8)
        s = lambda fan_in: 1.0 / np.sqrt(fan_in)
        x = jax.random.normal(ks[0], (4, 512, D_MODEL), dtype=jnp.float32)
        Wr = jax.random.uniform(ks[1], (N_EXP, D_MODEL), jnp.float32, -s(D_MODEL), s(D_MODEL))
        br = jax.random.uniform(ks[2], (N_EXP,), jnp.float32, -s(D_MODEL), s(D_MODEL))
        W1 = jax.random.uniform(ks[3], (N_EXP, D_FF, D_MODEL), jnp.float32, -s(D_MODEL), s(D_MODEL))
        b1 = jax.random.uniform(ks[4], (N_EXP, D_FF), jnp.float32, -s(D_MODEL), s(D_MODEL))
        W2 = jax.random.uniform(ks[5], (N_EXP, D_MODEL, D_FF), jnp.float32, -s(D_FF), s(D_FF))
        b2 = jax.random.uniform(ks[6], (N_EXP, D_MODEL), jnp.float32, -s(D_FF), s(D_FF))
        return {'x': x, 'Wr': Wr, 'br': br, 'W1': W1, 'b1': b1, 'W2': W2, 'b2': b2}
    _L0_ffn_all = _L0_ffn_setup()
    _L0_ffn_in = {k: v for k, v in _L0_ffn_all.items() if k in ('Wr', 'br', 'W1', 'b1', 'W2', 'b2')}
    del _L0_ffn_all
    return {'x': x, 'ctx_1024': ctx_1024, 'mask_BxS2_ik0': mask_BxS2_ik0, 'L0_attn_norm_w': _L0_attn_in['norm_w'], 'L0_attn_in_w': _L0_attn_in['in_w'], 'L0_attn_conv_w': _L0_attn_in['conv_w'], 'L0_attn_conv_b': _L0_attn_in['conv_b'], 'L0_attn_dt_bias': _L0_attn_in['dt_bias'], 'L0_attn_A_log': _L0_attn_in['A_log'], 'L0_attn_D_param': _L0_attn_in['D_param'], 'L0_attn_gnorm_w': _L0_attn_in['gnorm_w'], 'L0_attn_out_w': _L0_attn_in['out_w'], 'L0_attn_scorer_w1': _L0_attn_in['scorer_w1'], 'L0_attn_scorer_w2': _L0_attn_in['scorer_w2'], 'L0_attn_summ_w': _L0_attn_in['summ_w'], 'L0_attn_q_w': _L0_attn_in['q_w'], 'L0_attn_k_w': _L0_attn_in['k_w'], 'L0_attn_v_w': _L0_attn_in['v_w'], 'L0_attn_gate_w': _L0_attn_in['gate_w'], 'L0_xattn_q_w': _L0_xattn_in['q_w'], 'L0_xattn_q_b': _L0_xattn_in['q_b'], 'L0_xattn_k_w': _L0_xattn_in['k_w'], 'L0_xattn_k_b': _L0_xattn_in['k_b'], 'L0_xattn_v_w': _L0_xattn_in['v_w'], 'L0_xattn_v_b': _L0_xattn_in['v_b'], 'L0_ffn_Wr': _L0_ffn_in['Wr'], 'L0_ffn_br': _L0_ffn_in['br'], 'L0_ffn_W1': _L0_ffn_in['W1'], 'L0_ffn_b1': _L0_ffn_in['b1'], 'L0_ffn_W2': _L0_ffn_in['W2'], 'L0_ffn_b2': _L0_ffn_in['b2']}

def reference(x, ctx_1024, mask_BxS2_ik0, L0_attn_norm_w, L0_attn_in_w, L0_attn_conv_w, L0_attn_conv_b, L0_attn_dt_bias, L0_attn_A_log, L0_attn_D_param, L0_attn_gnorm_w, L0_attn_out_w, L0_attn_scorer_w1, L0_attn_scorer_w2, L0_attn_summ_w, L0_attn_q_w, L0_attn_k_w, L0_attn_v_w, L0_attn_gate_w, L0_xattn_q_w, L0_xattn_q_b, L0_xattn_k_w, L0_xattn_k_b, L0_xattn_v_w, L0_xattn_v_b, L0_ffn_Wr, L0_ffn_br, L0_ffn_W1, L0_ffn_b1, L0_ffn_W2, L0_ffn_b2):
    import jax
    import jax.numpy as jnp

    def _L0_attn_ref(x, norm_w, in_w, conv_w, conv_b, dt_bias, A_log, D_param, gnorm_w, out_w, scorer_w1, scorer_w2, summ_w, q_w, k_w, v_w, gate_w):
        import jax, jax.numpy as jnp
        import numpy as np
        D_MODEL = 256
        D_STATE = 128
        D_CONV = 4
        EXPAND = 2
        HEADDIM = 64
        D_INNER = D_MODEL * EXPAND
        NHEADS = D_INNER // HEADDIM
        CONV_DIM = D_INNER + 2 * D_STATE
        D_IN_PROJ = 2 * D_INNER + 2 * D_STATE + NHEADS
        POOL = 50
        SDIM = 64
        HEAD_DIM_RET = SDIM // 4
        TAU1 = 0.5
        TAU2 = 0.3
        HID = D_MODEL // 4
        B = 4
        T = 512
        EPS = 1e-05

        def _rmsnorm(x, w):
            return x * jax.lax.rsqrt(jnp.mean(x * x, axis=-1, keepdims=True) + EPS) * w

        def _mamba2(x, in_w, conv_w, conv_b, dt_bias, A_log, D_param, gnorm_w, out_w):
            Bn, Tn, _ = x.shape
            zxbcdt = x @ in_w.T
            z = zxbcdt[..., :D_INNER]
            xBC = zxbcdt[..., D_INNER:D_INNER + CONV_DIM]
            dt = zxbcdt[..., D_INNER + CONV_DIM:]
            xp = jnp.pad(jnp.transpose(xBC, (0, 2, 1)), ((0, 0), (0, 0), (D_CONV - 1, 0)))
            conv = jax.lax.conv_general_dilated(xp, conv_w[:, None, :], (1,), 'VALID', dimension_numbers=('NCH', 'OIH', 'NCH'), feature_group_count=CONV_DIM)
            xBC = jax.nn.silu(jnp.transpose(conv, (0, 2, 1)) + conv_b)
            xs = xBC[..., :D_INNER].reshape(Bn, Tn, NHEADS, HEADDIM)
            Bm = xBC[..., D_INNER:D_INNER + D_STATE]
            Cm = xBC[..., D_INNER + D_STATE:]
            dt = jax.nn.softplus(dt + dt_bias)
            A = -jnp.exp(A_log)
            dA = jnp.exp(dt * A)
            dtx = dt[..., None] * xs

            def step(h, inp):
                dA_t, dtx_t, B_t, C_t = inp
                h = h * dA_t[:, :, None, None] + dtx_t[..., None] * B_t[:, None, None, :]
                y = jnp.einsum('bhpn,bn->bhp', h, C_t)
                return (h, y)
            tm = lambda a: jnp.moveaxis(a, 1, 0)
            h0 = jnp.zeros((Bn, NHEADS, HEADDIM, D_STATE), x.dtype)
            _, ys = jax.lax.scan(step, h0, (tm(dA), tm(dtx), tm(Bm), tm(Cm)))
            y = jnp.moveaxis(ys, 0, 1) + D_param[None, None, :, None] * xs
            y = y.reshape(Bn, Tn, D_INNER)
            y = _rmsnorm(y * jax.nn.silu(z), gnorm_w)
            return y @ out_w.T

        def _update_memory(tokens, imp, summ_w, pool, prio, counts):
            Bn, Tn, Dm = tokens.shape
            S = min(Tn, POOL)
            order = jnp.argsort(-imp, axis=1)[:, :S]
            s_imp = jnp.take_along_axis(imp, order, axis=1)
            s_tok = jnp.take_along_axis(tokens, order[..., None], axis=1)
            s_sum = s_tok @ summ_w.T
            s_mask = s_imp > TAU1
            ar = jnp.arange(Bn)

            def body(carry, inp):
                pool, prio, counts = carry
                hi, si, ss = inp
                add = hi & (counts < POOL)
                idx = jnp.minimum(counts, POOL - 1)
                pool = pool.at[ar, idx].set(jnp.where(add[:, None], ss, pool[ar, idx]))
                prio = prio.at[ar, idx].set(jnp.where(add, si, prio[ar, idx]))
                counts = counts + add.astype(counts.dtype)
                repl = hi & (counts >= POOL)
                mi = jnp.argmin(prio, axis=1)
                should = repl & (si > prio[ar, mi])
                pool = pool.at[ar, mi].set(jnp.where(should[:, None], ss, pool[ar, mi]))
                prio = prio.at[ar, mi].set(jnp.where(should, si, prio[ar, mi]))
                return ((pool, prio, counts), None)
            xs = (jnp.moveaxis(s_mask, 1, 0), jnp.moveaxis(s_imp, 1, 0), jnp.moveaxis(s_sum, 1, 0))
            (pool, prio, counts), _ = jax.lax.scan(body, (pool, prio, counts), xs)
            return (pool, prio, counts)
        residual = x
        xn = _rmsnorm(x, norm_w)
        y = _mamba2(xn, in_w, conv_w, conv_b, dt_bias, A_log, D_param, gnorm_w, out_w)
        h = jax.nn.relu(y @ scorer_w1.T)
        scores = jax.nn.sigmoid((h @ scorer_w2.T)[..., 0])
        Bn = x.shape[0]
        pool = jnp.zeros((Bn, POOL, SDIM), x.dtype)
        prio = jnp.zeros((Bn, POOL), x.dtype)
        counts = jnp.zeros((Bn,), jnp.int32)
        pool, prio, counts = _update_memory(y, scores, summ_w, pool, prio, counts)
        mean_score = jnp.mean(scores, axis=1)
        retrieve_mask = (mean_score > TAU2) & (counts > 0)
        memory_mask = jnp.arange(POOL)[None, :] < counts[:, None]
        q = y @ q_w.T
        k = pool @ k_w.T
        v = pool @ v_w.T
        scale = np.float32(1.0 / np.sqrt(HEAD_DIM_RET))
        logits = jnp.einsum('btd,bpd->btp', q, k) * scale
        logits = jnp.where(memory_mask[:, None, :], logits, jnp.float32(-1000000000.0))
        attn = jax.nn.softmax(logits, axis=-1)
        retrieved = jnp.einsum('btp,bpd->btd', attn, v)
        gate = jax.nn.sigmoid(jnp.concatenate([y, retrieved], axis=-1) @ gate_w.T)
        y = y + gate * retrieved * retrieve_mask[:, None, None].astype(y.dtype)
        return residual + y

    def _L0_xattn_ref(hidden_states, context, attention_mask, q_w, q_b, k_w, k_b, v_w, v_b):
        import jax, jax.numpy as jnp
        import numpy as np
        B, LQ, LK, D = (4, 512, 512, 256)
        H = 16
        HD = D // H

        def _split_heads(x):
            b, l, _ = x.shape
            return x.reshape(b, l, H, HD).transpose(0, 2, 1, 3)
        q = _split_heads(hidden_states @ q_w.T + q_b)
        k = _split_heads(context @ k_w.T + k_b)
        v = _split_heads(context @ v_w.T + v_b)
        scores = jnp.einsum('bhqd,bhkd->bhqk', q, k) / jnp.sqrt(jnp.float32(HD))
        mask = (attention_mask > 0)[:, None, None, :]
        scores = jnp.where(mask, -jnp.inf, scores)
        probs = jax.nn.softmax(scores, axis=-1)
        ctx = jnp.einsum('bhqk,bhkd->bhqd', probs, v)
        ctx = ctx.transpose(0, 2, 1, 3).reshape(ctx.shape[0], ctx.shape[2], H * HD)
        return ctx

    def _L0_ffn_ref(x, Wr, br, W1, b1, W2, b2):
        import jax, jax.numpy as jnp
        import numpy as np
        D_MODEL, D_FF, N_EXP = (256, 1024, 8)
        B, S, D = x.shape
        xf = x.reshape(-1, D)
        logits = xf @ Wr.T + br
        expert_idx = jnp.argmax(logits, axis=-1)
        h = jax.nn.relu(jnp.einsum('td,efd->etf', xf, W1) + b1[:, None, :])
        y = jnp.einsum('etf,edf->etd', h, W2) + b2[:, None, :]
        out = y[expert_idx, jnp.arange(xf.shape[0])]
        return out.reshape(B, S, D)
    x = x + _L0_attn_ref(_layernorm(x, axis=-1), L0_attn_norm_w, L0_attn_in_w, L0_attn_conv_w, L0_attn_conv_b, L0_attn_dt_bias, L0_attn_A_log, L0_attn_D_param, L0_attn_gnorm_w, L0_attn_out_w, L0_attn_scorer_w1, L0_attn_scorer_w2, L0_attn_summ_w, L0_attn_q_w, L0_attn_k_w, L0_attn_v_w, L0_attn_gate_w)
    x = x + _L0_xattn_ref(_layernorm(x, axis=-1), ctx_1024, mask_BxS2_ik0, L0_xattn_q_w, L0_xattn_q_b, L0_xattn_k_w, L0_xattn_k_b, L0_xattn_v_w, L0_xattn_v_b)
    x = x + _L0_ffn_ref(_layernorm(x, axis=-1), L0_ffn_Wr, L0_ffn_br, L0_ffn_W1, L0_ffn_b1, L0_ffn_W2, L0_ffn_b2)
    return x

_drawn_inputs = setup_inputs


def setup_inputs(seed=0):
    import zlib

    import numpy as np

    out = dict(_drawn_inputs(seed))
    spreads = {'L0_attn_norm_w': (1.0, 0.2),
     'L0_attn_conv_b': (0.0, 0.1),
     'L0_attn_D_param': (1.0, 0.2),
     'L0_attn_gnorm_w': (1.0, 0.2),
     'L0_xattn_q_b': (0.0, 0.8),
     'L0_xattn_k_b': (0.0, 0.8),
     'L0_xattn_v_b': (0.0, 0.1)}
    factors = {'L0_xattn_q_w': 8.0, 'L0_xattn_k_w': 8.0, 'L0_ffn_b1': 8.0, 'L0_ffn_b2': 7.068}
    for name, (base, spread) in spreads.items():
        noise = np.random.default_rng([zlib.crc32(name.encode()), seed]).standard_normal(out[name].shape)
        drawn = base * np.exp(spread * noise) if base else spread * noise
        out[name] = jnp.asarray(drawn.astype(out[name].dtype))
    for name, factor in factors.items():
        out[name] = (out[name] * factor).astype(out[name].dtype)
    return out
```

```python
from contextlib import ExitStack

import numpy as np

import concourse.bass as bass
from concourse import mybir

F32 = mybir.dt.float32
I32 = mybir.dt.int32
ALU = mybir.AluOpType
ACT = mybir.ActivationFunctionType
AX = mybir.AxisListType.X
ds = bass.ds

P = 128
EPS = 1e-5
NEG = -1e30

B, T, D = 2, 1024, 256
NT = B * T // P
TB = T // P
KD = D // P
DI, NS, H, HP = 512, 128, 8, 64
TAPS = 4
NZ, NX = DI // P, (DI + 2 * NS) // P
BLK = 512
NBLK = B * T // BLK
POOL, SD = 50, 64
LK, XH, HD = 154, 16, 16
KT = 32
KM = LK - KT
GH, NG = 4, 4
NE, FF = 8, 1024
NFF = FF // P
NB = NT + NE - 1
ROW = 2 * D + 1

DVE_EVENTS = (
    "eps_set", "ln_var", "rstd_1", "rstd_2", "rms_var", "rstd_3", "rstd_4", "dt_steps_1", 
    "dt_steps_2", "dt_abs", "dt_sum", "dt_ready", "tot_kept", "wend_diff", "first_cleared_1", 
    "first_cleared_2", "decay_ready", "gn_rstd", "w2b_ready", "pos_ready", "cols_cleared", 
    "valid_ready", "rank_sum_1", "rank_sum_2", "mean_ready_1", "mean_ready_2", "ln2_var", "ln2_rstd", 
    "mask_row_ready", "bias_cols_ready", "ln3_var", "ln3_rstd", "iotas_ready", "block_expert_ready",
)
ACT_EVENTS = (
    "ln_sd", "rms_sd", "dt_e", "a_exp", "dt_ln", "ecum_exp", "dec_exp", "wend_exp", "gn_sd", "ln2_sd", 
    "ln3_sd",
)
POOL_EVENTS = (
    "ones_set", "mask_init", "masks_set_1", "masks_set_2", "masks_set_3", "state_set", "pos_set", 
    "bias_rows_zero_1", "bias_rows_cleared_1", "bias_rows_zero_2", "bias_rows_cleared_2", 
    "pads_zero_1", "pads_zero_2", "pads_zero_3", "pads_zero_4", "pads_zero_5", "empty_ready_1", 
    "empty_ready_2", "counters_set",
)


def events_of(name):
    return next(events for events in (DVE_EVENTS, ACT_EVENTS, POOL_EVENTS) if name in events)


def at(name):
    return events_of(name).index(name) + 1


def build(nc, a, out):
    x_flat = a["x"].rearrange("b t d -> (b t) d")
    out_flat = out.rearrange("b t d -> (b t) d")

    with ExitStack() as ctx:
        def sb(name, shape, dt=F32):
            return ctx.enter_context(nc.sbuf_tensor(name, shape, dt))

        names = {}

        def sem(name):
            if name not in names:
                names[name] = ctx.enter_context(nc.semaphore(name))
            return names[name]

        dve_once, act_once, pool_once = sem("dve_once"), sem("act_once"), sem("pool_once")
        met = []

        def reached(name):
            met.append(name)
            events = events_of(name)
            assert [m for m in met if m in events] == list(events[:at(name)])
            return 1

        bank = [ctx.enter_context(nc.psum_tensor(f"bank{i}", [P, 512], F32)) for i in range(8)]

        xres = sb("xres", [P, NT, D])
        featT = sb("featT", [P, KD, B * T])
        ybuf = sb("ybuf", [P, NT * D])
        arena = sb("arena", [P, 2 * NE * KD * FF])
        y_tok = ybuf[:, :].rearrange("p (t d) -> p t d", t=NT)
        IN_W = 2 * DI + 2 * NS + H
        w_in = ybuf[:, 0:KD * IN_W].rearrange("p (k n) -> p k n", k=KD)

        place = [0]

        def cut(shape):
            n = int(np.prod(shape))
            v = arena[:, place[0]:place[0] + n]
            place[0] += n
            if len(shape) == 2:
                v = v.rearrange("p (a b) -> p a b", a=shape[0])
            if len(shape) == 3:
                v = v.rearrange("p (a b c) -> p a b c", a=shape[0], b=shape[1])
            return v

        xbcT = cut([NX, B * T])
        zsT = cut([NZ, B * T])
        work0 = place[0]
        raw = cut([NX, TAPS - 1 + BLK])
        conv = cut([2, BLK])
        tanh_c = cut([2, BLK])
        tanh_z = cut([2, BLK])
        place[0] = work0
        x0 = cut([2, D])
        xn = cut([2, D])
        xn_tile = cut([2, KD, P])
        place[0] = work0
        xbc = cut([2, NX, P])
        seg = cut([2, H, P])
        lmat = cut([2, H, P])
        gmat = cut([2, P])
        b_tok = cut([2, P])
        xdt = cut([2, DI])
        xend = cut([2, DI])
        xskip = cut([2, DI])
        state = cut([DI])
        y_in = cut([2, DI])
        gated = cut([2, NZ, P])
        sq = featT[:, 0, 0:2 * NZ * P].rearrange("p (a b c) -> p a b c", a=2, b=NZ)
        assert place[0] <= 2 * NE * KD * FF

        ident = sb("ident", [P, P])
        ones = sb("ones", [P, P])
        tri_le = sb("tri_le", [P, P])
        tri_gt = sb("tri_gt", [P, P])
        w_out = sb("w_out", [P, NZ, D])
        norm_w = sb("norm_w", [P, KD])
        gnorm_w = sb("gnorm_w", [P, NZ])
        conv_w = sb("conv_w", [P, NX, TAPS])
        conv_b = sb("conv_b", [P, NX])
        dt_bias = sb("dt_bias", [P, H])
        a_log = sb("a_log", [P, H])
        d_skip = sb("d_skip", [P, H])
        stats = sb("stats", [P, NT, 6])
        mv = sb("mv", [P, NT, 2])
        nrm = sb("nrm", [P, 6, NT])
        dts = sb("dts", [P, 8, NT * H])
        ssq = sb("ssq", [P, 4, NT])
        eps_col = sb("eps_col", [P, 1])
        dt_raw, dt_neg, dt_pos, dt_exp = (dts[:, i, :] for i in range(4))
        dt_v, dta, ecum, dec = (dts[:, i, :] for i in range(4, 8))
        wend = dt_raw
        tot = dt_neg

        def th(v):
            return v.rearrange("p (t h) -> p t h", h=H)

        def heads(v, n):
            return v.unsqueeze(2).broadcast_to([P, H, n])

        w1 = arena[:, 0:NE * KD * FF].rearrange("p (e k f) -> p e k f", e=NE, k=KD)
        UP = NE * KD * FF
        place[0] = UP
        wq_dense = cut([KD, D])
        wk_dense = cut([KD, D])
        wv = cut([KD, D])
        ctxT = cut([B, KD, LK])
        after_loads = place[0]
        sig = cut([B * T])
        y_st = cut([2, D])
        hid = cut([2, BLK])
        junk = cut([T])
        onehot = cut([TB, POOL])
        pool_tok = cut([D])
        pool_tokT = cut([KD, POOL])
        poolT = cut([POOL])
        keyT = cut([POOL])
        val = cut([D])
        q_mem = cut([BLK])
        logit = cut([4, POOL])
        attnT = cut([BLK])
        retT = cut([KD, BLK])
        gate_t = cut([KD, BLK])
        upd = cut([KD, BLK])
        assert place[0] <= 2 * NE * KD * FF
        scorer_w1 = sb("scorer_w1", [P, KD, SD])
        scorer_w2 = sb("scorer_w2", [SD, 1])
        scorer_w2b = sb("scorer_w2b", [SD, P])
        summ_w = sb("summ_w", [P, KD, SD])
        mem_q_w = sb("mem_q_w", [P, KD, SD])
        mem_k_w = sb("mem_k_w", [SD, SD])
        mem_v_w = sb("mem_v_w", [SD, D])
        gate_w = sb("gate_w", [P, 2 * KD, D])
        pos_i = sb("pos_i", [P, POOL], I32)
        pos = sb("pos", [P, POOL])
        cols = sb("cols", [P, 8, NT])
        s_col, n_ge, n_gt, n_eq, rank, valid = (cols[:, i, :] for i in range(6))
        mean_s = sb("mean_s", [P, B])
        vbias = sb("vbias", [P, POOL])
        red = sb("red", [P, 3, 4])

        place[0] = after_loads
        wq_pad = cut([KD, NG * P])
        wk_pad = cut([KD, NG * P])
        tail_ctx = cut([B, KD, P])
        keys = cut([B, NG, GH * LK])
        v_main = cut([B, XH, HD + 1])
        v_tail = cut([B, NG, GH * (HD + 1)])
        qT = cut([NG, BLK])
        assert place[0] + XH * LK <= 2 * NE * KD * FF
        prob_a = cut([XH * LK])
        prob_b = sb("prob_b", [P, XH * LK])
        prob = (prob_a, prob_b[:, :])
        prob_m = [v[:, 0:XH * KM].rearrange("p (h n) -> p h n", h=XH) for v in prob]
        prob_t = [v[:, XH * KM:].rearrange("p (h n) -> p h n", h=XH) for v in prob]
        probT = ybuf[:, 0:(XH + NG) * P].rearrange("p (h n) -> p h n", h=XH + NG)
        ln_st = ybuf[:, (XH + NG) * P:(XH + NG) * P + 2 * D].rearrange("p (a d) -> p a d", a=2)
        head_o = ybuf[:, (XH + NG) * P + 2 * D:(XH + NG) * P + 4 * D].rearrange("p (a d) -> p a d", a=2)
        bias_rows = sb("bias_rows", [NG, 2, GH, 32])
        bias_cols = sb("bias_cols", [P, 2, NG])
        rows1 = w_out[0:1, :, :].rearrange("p k n -> p (k n)")
        mask_i = rows1[:, 0:B * LK].bitcast(I32)
        mask_row = rows1[:, B * LK:2 * B * LK]
        vb_row = rows1[:, 2 * B * LK:2 * B * LK + D]
        mask_sel = rows1[:, 2 * B * LK + D:2 * B * LK + D + P]
        xmax = sb("xmax", [P, 2, XH])
        xinv = sb("xinv", [P, 2, XH])
        QW, HW_ = HD, 32

        w2 = arena[:, NE * KD * FF:].rearrange("p (e f d) -> p e f d", e=NE, f=NFF)
        sorted_rows = nc.dram_tensor("sorted_rows", [NB * P, ROW], F32, kind="Internal").ap()
        NOWHERE = 2 * B * T

        def parts(v, *shapes):
            at_, out_ = 0, []
            for shape in shapes:
                n = int(np.prod(shape))
                w = v[:, at_:at_ + n]
                if len(shape) == 2:
                    w = w.rearrange("p (a b) -> p a b", a=shape[0])
                if len(shape) == 3:
                    w = w.rearrange("p (a b c) -> p a b c", a=shape[0], b=shape[1])
                out_.append(w)
                at_ += n
            return out_
        g_flat = gate_w[:, :, :].rearrange("p k n -> p (k n)")
        b1_cols, w_route, br_row, empty = parts(g_flat, [NE * NFF], [KD, NE], [NE], [ROW])
        ints = g_flat[:, 640:].bitcast(I32)
        token_i, slot_i, slot_now, expert_i, desc_i, thr_i, blk_i = parts(ints, [NT], [NT], [2], [NB], [NE], [NT], [NB])
        logits, hot, slot_t, before, blocks_c, expert_c, desc, thr, blk_n, first_blk, best, slot_f, expert_f = parts(
            w_out[:, :, :].rearrange("p k n -> p (k n)"), [NT, NE], [NT, NE], [NT, NE], [NT + 1, NE], [NE, NT], [NB, NE],
            [NE], [NT], [NB], [NE + 1], [NT], [NT], [NB])
        rows, xsT, x3T = parts(ybuf[:, 0:(XH + NG) * P], [2, ROW], [2, KD, P], [2, KD, P])
        hid_e, hidT = parts(prob_b[:, :], [FF], [NFF, P])
        b2_rows, xs, rest, yo = parts(featT[:, :, :].rearrange("p k n -> p (k n)"), [NE, D], [2, D], [2, D + 1], [2, D])

        block = ctx.enter_context(nc.Block())
        S = sem
        N_SMALL = 8

        @block.sync
        def _(sp):
            for q in range(4):
                sp.dma_start(xres[:, 4 * q:4 * q + 4, :],
                             x_flat[q * BLK:(q + 1) * BLK, :].rearrange("(t p) d -> p t d", p=P)
                             ).then_inc(S(f"x_loaded{q}"), 16)
            sp.dma_start(w_in, a["attn_in_wT"].rearrange("(k p) n -> p k n", p=P)).then_inc(S("w_loaded"), 16)
            sp.dma_start(w_out[:, :, :], a["attn_out_wT"].rearrange("(k p) n -> p k n", p=P)
                         ).then_inc(S("w_loaded"), 16)

            sp.wait_ge(S("conv_done"), NX * NBLK)

            def load_chunk(t, p, wait):
                first, used = (sp.snap(t * P), sp.snap(t - 1)) if wait else (t * P, 0)
                if wait:
                    sp.wait_ge(S("state_mm"), used)
                sp.dma_start(xbc[:, p, :, :], xbcT[:, :, ds(first, P)]).then_inc(S(f"chunk_loaded{p}"), 16)
            load_chunk(0, 0, False)
            load_chunk(1, 1, False)
            with sp.Fori(1, NT // 2) as i:
                for p in range(2):
                    load_chunk(2 * i + p, p, True)

            for dst, src in ((scorer_w1[:, :, :], a["scorer_w1T"].rearrange("(k p) n -> p k n", p=P)),
                             (scorer_w2[:, :], a["scorer_w2T"]),
                             (summ_w[:, :, :], a["summ_wT"].rearrange("(k p) n -> p k n", p=P)),
                             (mem_q_w[:, :, :], a["mem_q_wT"].rearrange("(k p) n -> p k n", p=P)),
                             (mem_k_w[:, :], a["mem_k_wT"]),
                             (mem_v_w[:, :], a["mem_v_wT"]),
                             (gate_w[:, :, :], a["gate_wT"].rearrange("(k p) n -> p k n", p=P))):
                sp.dma_start(dst, src).then_inc(S("mem_w_loaded"), 16)
            sp.wait_ge(S("out_kept"), NT)
            sp.wait_ge(S("y_part"), 2 * NT)
            sp.wait_ge(S("state_added"), NT)

            for dst, src in ((wq_dense, a["q_w"].rearrange("(k p) n -> p k n", p=P)),
                             (wk_dense, a["k_w"].rearrange("(k p) n -> p k n", p=P)),
                             (wv, a["v_w"].rearrange("(k p) n -> p k n", p=P)),
                             (mask_i[:, :], a["mask"].rearrange("b k -> (b k)").unsqueeze(0)),
                             (vb_row[:, :], a["v_b"].unsqueeze(0))):
                sp.dma_start(dst, src).then_inc(S("x_w_loaded"), 16)
            for b in range(B):
                sp.dma_start(ctxT[:, b, :, :], a["ctxT"][b].rearrange("(k p) n -> p k n", p=P)).then_inc(S("x_w_loaded"), 16)
            sp.wait_ge(pool_once, at("bias_rows_cleared_2"))
            for n, name in enumerate(("q_b", "k_b")):
                sp.dma_start(bias_rows[:, n, :, 0:HD], a[name].rearrange("(g h d) -> g h d", g=NG, h=GH)).then_inc(S("x_w_loaded"), 16)
            for e in range(NE):
                sp.dma_start(w1[:, e, :, :], a["W1T"][e].rearrange("(k p) f -> p k f", p=P)).then_inc(S("w1_loaded"), 16)

            sp.wait_ge(S("gate_tanh"), 2 * NBLK)
            for dst, src in ((b1_cols, a["b1"]), (w_route, a["WrT"].rearrange("(k p) n -> p k n", p=P)),
                             (br_row, a["br"].partition_broadcast(P))):
                sp.dma_start(dst, src).then_inc(S("route_w_loaded"), 16)
            sp.wait_ge(pool_once, at("empty_ready_2"))
            sp.dma_start(sorted_rows.rearrange("(n p) r -> p n r", p=P), empty.unsqueeze(1).broadcast_to([P, NB, ROW])
                         ).then_inc(S("rows_emptied"), 16)
            sp.wait_ge(S("x2_ready"), NT)
            sp.wait_ge(S("prob_turned"), (NG + 1) * NT)
            for e in range(NE):
                sp.dma_start(w2[:, e, :, :], a["W2T"][e].rearrange("(f p) d -> p f d", p=P)).then_inc(S("w2_loaded"), 16)
            for e in range(NE):
                sp.dma_start(b2_rows[:, e, :], a["b2"][e].partition_broadcast(P)).then_inc(S("w2_loaded"), 16)
            sp.wait_ge(S("scattered0"), 16 * NT // 2)
            sp.wait_ge(S("scattered1"), 16 * NT // 2)

            def load_rows(n, p, wait):
                first, used, stored = (sp.snap(n * P), sp.snap(n - 1), sp.snap(8 * (n - p))) if wait else (n * P, 0, 0)
                if wait:
                    sp.wait_ge(S("xs_turned"), used)
                sp.dma_start(xs[:, p, :], sorted_rows[ds(first, P), 0:D]).then_inc(S(f"xs_loaded{p}"), 16)
                if wait:
                    sp.wait_ge(S(f"out_stored{p}"), stored)
                sp.dma_start(rest[:, p, :], sorted_rows[ds(first, P), D:ROW]).then_inc(S(f"rest_loaded{p}"), 16)
            load_rows(0, 0, False)
            load_rows(1, 1, False)
            with sp.Fori(1, NB // 2) as i:
                load_rows(2 * i, 0, True)
                load_rows(2 * i + 1, 1, True)
            load_rows(NB - 1, 0, True)

        @block.gpsimd
        def _(pool):
            pool.memset(ones[:, :], 1.0).then_inc(pool_once, reached("ones_set"))
            pool.memset(ident[:, :], 0.0).then_inc(pool_once, reached("mask_init"))
            pool.wait_ge(pool_once, at("ones_set"))
            pool.wait_ge(pool_once, at("mask_init"))
            pool.affine_select(out=ident[:, :], in_=ident[:, :], compare_op=ALU.not_equal, fill=1.0, base=0,
                               pattern=[[-1, P]], channel_multiplier=1).then_inc(pool_once, reached("masks_set_1"))
            pool.affine_select(out=tri_le[:, :], in_=ones[:, :], compare_op=ALU.is_ge, fill=0.0, base=0,
                               pattern=[[1, P]], channel_multiplier=-1).then_inc(pool_once, reached("masks_set_2"))
            pool.affine_select(out=tri_gt[:, :], in_=ones[:, :], compare_op=ALU.is_gt, fill=0.0, base=0,
                               pattern=[[-1, P]], channel_multiplier=1).then_inc(pool_once, reached("masks_set_3"))
            with pool.Fori(0, NT // 2) as i:
                for p in range(2):
                    t = 2 * i + p
                    pool.wait_ge(S("x0_ready"), t + 1)
                    pool.tensor_tensor(xres[:, ds(t, 1), :].rearrange("p a d -> p (a d)"), xres[:, ds(t, 1), :].rearrange("p a d -> p (a d)"), x0[:, p, :], ALU.add
                                       ).then_inc(S("res_added"), 1)
                    pool.wait_ge(S("xn_tile_ready"), t + 1)
                    pool.tensor_copy(featT[:, :, ds(t * P, P)], xn_tile[:, p, :, :]).then_inc(S("xnT_ready"), 1)
            pool.wait_ge(dve_once, at("dt_ready"))
            pool.wait_ge(dve_once, at("decay_ready"))
            pool.wait_ge(S("conv_done"), NX * NBLK)
            pool.memset(state, 0.0).then_inc(pool_once, reached("state_set"))

            def make_seg(t, p, wait):
                if wait:
                    pool.wait_ge(S("seg_mm"), t - 1)
                pool.tensor_tensor(seg[:, p, :, :], tri_le[:, :].unsqueeze(1).broadcast_to([P, H, P]),
                                   heads(dta[:, ds(t * H, H)], P), ALU.mult).then_inc(S("seg_ready"), 1)

            def make_m(t, p):
                pool.wait_ge(S("decay_mat"), t + 1)
                pool.wait_ge(S("g_ready"), t + 1)
                pool.tensor_tensor(lmat[:, p, :, :], lmat[:, p, :, :],
                                   gmat[:, p, :].unsqueeze(1).broadcast_to([P, H, P]), ALU.mult
                                   ).then_inc(S("m_ready"), 1)

            def decay_state(t):
                pool.wait_ge(S("inter_mm"), t + 1)
                pool.wait_ge(S("state_added"), t)
                sv = state.rearrange("p (h n) -> p h n", h=H)
                pool.tensor_tensor(sv, sv, heads(dec[:, ds(t * H, H)], HP), ALU.mult).then_inc(S("state_decayed"), 1)

            pool.wait_ge(pool_once, at("state_set"))
            make_seg(0, 0, False)
            make_seg(1, 1, False)
            make_m(0, 0)

            def step(t, p):
                make_seg(t + 2, p, True)
                make_m(t + 1, 1 - p)
                decay_state(t)
            with pool.Fori(0, NT // 2 - 1) as i:
                step(2 * i, 0)
                step(2 * i + 1, 1)
            make_m(NT - 1, 1)
            decay_state(NT - 2)
            decay_state(NT - 1)

            pool.iota(pos_i[:, :], pattern=[[1, POOL]], base=0, channel_multiplier=0).then_inc(pool_once, reached("pos_set"))
            with pool.Fori(0, NT // 2) as i:
                for p in range(2):
                    t = 2 * i + p
                    pool.wait_ge(S("y_st_ready"), t + 1)
                    pool.tensor_tensor(xres[:, ds(t, 1), :].rearrange("p a d -> p (a d)"),
                                       xres[:, ds(t, 1), :].rearrange("p a d -> p (a d)"), y_st[:, p, :], ALU.add
                                       ).then_inc(S("res_y_added"), 1)

            pool.memset(bias_rows[:, :, :, :], 0.0).then_inc(pool_once, reached("bias_rows_zero_1"))
            pool.wait_ge(pool_once, at("bias_rows_zero_1"))
            pool.memset(bias_rows[:, 0, :, HD:HD + 1], 1.0).then_inc(pool_once, reached("bias_rows_cleared_1"))
            pool.memset(mask_sel[:, :], 0.0).then_inc(pool_once, reached("bias_rows_zero_2"))
            pool.wait_ge(pool_once, at("bias_rows_zero_2"))
            pool.memset(mask_sel[:, :].rearrange("o (h c) -> o h c", c=32)[:, :, HD:HD + 1], 1.0).then_inc(pool_once, reached("bias_rows_cleared_2"))
            pool.wait_ge(S("x1_ready"), 2 * NBLK)
            pool.wait_ge(S("gate_tanh"), 2 * NBLK)
            pool.memset(wq_pad, 0.0).then_inc(pool_once, reached("pads_zero_1"))
            pool.memset(wk_pad, 0.0).then_inc(pool_once, reached("pads_zero_2"))
            pool.memset(keys, 0.0).then_inc(pool_once, reached("pads_zero_3"))
            pool.memset(v_tail, 0.0).then_inc(pool_once, reached("pads_zero_4"))
            pool.memset(v_main, 1.0).then_inc(pool_once, reached("pads_zero_5"))
            pool.wait_ge(S("x_w_loaded"), 16 * 9)
            pool.wait_ge(pool_once, at("pads_zero_5"))
            for pad, dense in ((wk_pad, wk_dense), (wq_pad, wq_dense)):
                pool.tensor_copy(pad.rearrange("p k (h c) -> p (k h) c", c=32)[:, :, 0:HD],
                                 dense.rearrange("p k (h d) -> p (k h) d", d=HD)).then_inc(S("pads_ready"), 1)
            for b in range(B):
                pool.tensor_copy(tail_ctx[:, b, :, :].rearrange("p k (r c) -> p k r c", c=KT),
                                 ctxT[:, b, :, KM:LK].unsqueeze(2).broadcast_to([P, KD, GH, KT])).then_inc(S("pads_ready"), 1)
            pool.wait_ge(S("x_w_loaded"), 16 * 9)
            pool.memset(empty, 0.0).then_inc(pool_once, reached("empty_ready_1"))
            pool.wait_ge(pool_once, at("empty_ready_1"))
            pool.memset(empty[:, ROW - 1:ROW].bitcast(I32), NOWHERE).then_inc(pool_once, reached("empty_ready_2"))
            pool.iota(token_i, pattern=[[P, NT]], base=0, channel_multiplier=1)
            pool.iota(desc_i, pattern=[[-1, NE]], base=NE, channel_multiplier=0)
            pool.iota(thr_i, pattern=[[P, NT]], base=0, channel_multiplier=0)
            pool.iota(blk_i, pattern=[[1, NB]], base=0, channel_multiplier=0).then_inc(pool_once, reached("counters_set"))
            with pool.Fori(0, NT // 2) as i:
                for p in range(2):
                    t = 2 * i + p
                    pool.wait_ge(S("head_o_ready"), t + 1)
                    pool.tensor_tensor(xres[:, ds(t, 1), :].rearrange("p a d -> p (a d)"),
                                       xres[:, ds(t, 1), :].rearrange("p a d -> p (a d)"), head_o[:, p, :], ALU.add
                                       ).then_inc(S("x2_ready"), 1)
            pool.wait_ge(S("rows_emptied"), 16)
            last_row, last_token = pool.to_reg(NB * P - 1), pool.to_reg(B * T - 1)
            with pool.Fori(0, NT // 2) as i:
                for p in range(2):
                    pool.wait_ge(S("row_ready"), 2 * i + p + 1)
                    pool.sem_inc(S("pool_turn"), 1)
                    pool.indirect_dma_start(out=sorted_rows, out_offset=bass.IndirectOffsetOnAxis(ap=slot_now[:, p:p + 1], axis=0),
                                            in_=rows[:, p, :], in_offset=None, bounds_check=last_row, oob_is_err=False
                                            ).then_inc(S(f"scattered{p}"), 16)

            def store(n, p):
                pool.wait_ge(S("yo_ready"), n + 1)
                pool.sem_inc(S("pool_turn"), 1)
                pool.indirect_dma_start(out=out_flat, out_offset=bass.IndirectOffsetOnAxis(ap=rest[:, p, D:D + 1].bitcast(I32), axis=0),
                                        in_=yo[:, p, :], in_offset=None, bounds_check=last_token, oob_is_err=False
                                        ).then_inc(S(f"out_stored{p}"), 16)
            with pool.Fori(0, NB // 2) as i:
                store(2 * i, 0)
                store(2 * i + 1, 1)
            store(NB - 1, 0)
            pool.wait_ge(S("out_stored0"), 16 * (NB // 2 + 1))
            pool.wait_ge(S("out_stored1"), 16 * (NB // 2))

        @block.scalar
        def _(act):
            for dst, src in ((norm_w[:, :], a["attn_norm_w"]),
                             (gnorm_w[:, :], a["attn_gnorm_w"]),
                             (conv_w[:, :, :], a["attn_conv_w"]),
                             (conv_b[:, :], a["attn_conv_b"]),
                             (dt_bias[:, :], a["attn_dt_bias"].partition_broadcast(P)),
                             (a_log[:, :], a["attn_A_log"].partition_broadcast(P)),
                             (d_skip[:, :], a["attn_D_param"].partition_broadcast(P))):
                act.dma_start(dst, src).then_inc(S("small_loaded"), 16)
            act.wait_ge(dve_once, at("eps_set"))
            act.wait_ge(dve_once, at("ln_var"))
            act.activation(nrm[:, 0, :], mv[:, :, 1], ACT.Sqrt, bias=eps_col[:, :]).then_inc(act_once, reached("ln_sd"))
            act.wait_ge(dve_once, at("rms_var"))
            act.activation(nrm[:, 2, :], nrm[:, 1, :], ACT.Sqrt, bias=eps_col[:, :]).then_inc(act_once, reached("rms_sd"))
            with act.Fori(0, NT // 2) as i:
                for p in range(2):
                    t = 2 * i + p
                    act.wait_ge(S("xn_transposed"), t + 1)
                    if p == 0:
                        act.wait_ge(S("xnT_ready"), 2 * i)
                        act.wait_ge(S("dt_mm"), 2 * i)
                    act.activation(xn_tile[:, p, :, :], bank[p][:, 0:D].rearrange("p (k n) -> p k n", k=KD), ACT.Copy
                                   ).then_inc(S("xn_tile_ready"), 1)
            act.wait_ge(S("xnT_ready"), NT)

            def tanh_conv(blk, f):
                act.wait_ge(S("conv_sum"), NX * blk + f + 1)
                act.activation(tanh_c[:, f % 2, :], conv[:, f % 2, :], ACT.Tanh).then_inc(S("tanh_c_ready"), 1)

            with act.Fori(0, NBLK) as blk:
                for f in range(NZ):
                    act.wait_ge(S("proj_mm"), (NZ + NX) * blk + f + 1)
                    if f < 2:
                        act.wait_ge(S("zs_ready"), NZ * blk)
                    else:
                        act.wait_ge(S("zs_ready"), NZ * blk + f - 1)
                    act.activation(tanh_z[:, f % 2, :], bank[f % 5][:, :], ACT.Tanh).then_inc(S("tanh_z_ready"), 1)
                for f in range(NX):
                    act.wait_ge(S("proj_mm"), (NZ + NX) * blk + NZ + f + 1)
                    if f == 0:
                        act.wait_ge(S("raw_used"), NX * blk)
                    act.activation(raw[:, f, TAPS - 1:], bank[(NZ + f) % 5][:, :], ACT.Copy).then_inc(S("raw_ready"), 1)
                    if f >= 1:
                        tanh_conv(blk, f - 1)
                tanh_conv(blk, NX - 1)
            act.wait_ge(dve_once, at("dt_abs"))
            act.activation(dt_exp, dt_neg, ACT.Exp).then_inc(act_once, reached("dt_e"))
            act.activation(a_log[:, :], a_log[:, :], ACT.Exp).then_inc(act_once, reached("a_exp"))
            act.wait_ge(act_once, at("dt_e"))
            act.activation(dt_exp, dt_exp, ACT.Ln, bias=1.0).then_inc(act_once, reached("dt_ln"))
            act.wait_ge(S("cum_mm"), 1)
            act.activation(ecum, bank[0][:, 0:NT * H], ACT.Exp).then_inc(act_once, reached("ecum_exp"))
            act.wait_ge(S("cum_mm"), 2)
            act.activation(dec, bank[1][:, 0:NT * H], ACT.Exp).then_inc(act_once, reached("dec_exp"))
            act.wait_ge(dve_once, at("wend_diff"))
            act.activation(wend, wend, ACT.Exp).then_inc(act_once, reached("wend_exp"))

            def decay_matrix(t, p, wait):
                act.wait_ge(S("seg_mm"), t + 1)
                if wait:
                    act.wait_ge(S("intra_mm"), t - 1)
                for q in range(2):
                    i = act.activation(lmat[:, p, 4 * q:4 * q + 4, :], bank[2 + q][:, :].rearrange("p (h n) -> p h n", h=4), ACT.Exp)
                i.then_inc(S("decay_mat"), 1)

            def square(t, p):
                act.wait_ge(S("gated_ready"), t + 1)
                act.activation(sq[:, p, :, :], gated[:, p, :, :], ACT.Square).then_inc(S("sq_ready"), 1)

            def keep_out(t):
                act.wait_ge(S("out_mm"), t + 1)
                act.activation(y_tok[:, ds(t, 1), :].rearrange("p a d -> p (a d)"), bank[7][:, 0:D], ACT.Copy)
                act.activation(ssq[:, 0, ds(t, 1)], bank[7][:, D:D + 1], ACT.Copy).then_inc(S("out_kept"), 1)

            act.wait_ge(S("conv_done"), NX * NBLK)
            decay_matrix(0, 0, False)
            decay_matrix(1, 1, False)

            def act_step(t, p):
                square(t - 1, 1 - p)
                decay_matrix(t + 1, 1 - p, True)
                keep_out(t - 1)
            with act.Fori(0, NT // 2 - 1) as i:
                act_step(2 * i + 1, 1)
                act_step(2 * i + 2, 0)
            square(NT - 2, 0)
            keep_out(NT - 2)
            square(NT - 1, 1)
            keep_out(NT - 1)

            act.wait_ge(S("out_kept"), NT)
            act.activation(ssq[:, 1, :], ssq[:, 0, :], ACT.Sqrt, bias=eps_col[:, :], scale=1.0 / DI).then_inc(act_once, reached("gn_sd"))
            with act.Fori(0, NT // 2) as i:
                for p in range(2):
                    t = 2 * i + p
                    act.wait_ge(S("y_st_transposed"), t + 1)
                    act.activation(featT[:, :, ds(t * P, P)], bank[p][:, 0:D].rearrange("p (k n) -> p k n", k=KD), ACT.Copy
                                   ).then_inc(S("yT_ready"), 1)
            with act.Fori(0, NBLK) as blk:
                act.wait_ge(S("score_mm"), blk + 1)
                act.activation(sig[:, ds(blk * BLK, BLK)], bank[3][:, :], ACT.Tanh, scale=0.5).then_inc(S("score_tanh"), 1)
            with act.Fori(0, B) as b:
                act.wait_ge(S("pool_tok_turned"), b + 1)
                act.activation(pool_tokT, bank[4][:, 0:KD * POOL].rearrange("p (k n) -> p k n", k=KD), ACT.Copy).then_inc(S("pool_tokT_ready"), 1)
                act.wait_ge(S("pool_mm"), b + 1)
                act.activation(poolT[0:SD, :], bank[5][0:SD, 0:POOL], ACT.Copy).then_inc(S("poolT_ready"), 1)
                act.wait_ge(S("key_mm"), b + 1)
                act.activation(keyT[0:SD, :], bank[4][0:SD, 0:POOL], ACT.Copy, scale=0.25).then_inc(S("keyT_ready"), 1)
                for j in range(T // BLK):
                    n = (T // BLK) * b + j
                    act.wait_ge(S("q_mem_mm"), n + 1)
                    act.activation(q_mem[0:SD, :], bank[0][0:SD, :], ACT.Copy).then_inc(S("q_mem_ready"), 1)
                    act.wait_ge(S("logit_shifted"), n + 1)
                    act.activation(logit, logit, ACT.Exp).then_inc(S("logit_exp"), 1)
                    act.wait_ge(S("attn_turned"), n + 1)
                    act.activation(attnT[0:POOL, :], bank[2][0:POOL, :], ACT.Copy).then_inc(S("attnT_ready"), 1)
                    for m in range(KD):
                        act.wait_ge(S("ret_mm"), KD * n + m + 1)
                        act.activation(retT[:, m, :], bank[3 + m][:, :], ACT.Copy).then_inc(S("retT_ready"), 1)
                    for m in range(KD):
                        act.wait_ge(S("gate_mm"), KD * n + m + 1)
                        act.activation(gate_t[:, m, :], bank[5 + m][:, :], ACT.Tanh, scale=0.5).then_inc(S("gate_tanh"), 1)

            act.wait_ge(dve_once, at("ln2_var"))
            act.activation(nrm[:, 0, :], mv[:, :, 1], ACT.Sqrt, bias=eps_col[:, :]).then_inc(act_once, reached("ln2_sd"))
            with act.Fori(0, NT // 2) as i:
                for p in range(2):
                    t = 2 * i + p
                    act.wait_ge(S("ln2_transposed"), t + 1)
                    act.activation(featT[:, :, ds(t * P, P)], bank[p][:, 0:D].rearrange("p (k n) -> p k n", k=KD), ACT.Copy
                                   ).then_inc(S("hT_ready"), 1)

            def keep_q(blk, g):
                act.wait_ge(S("q_mm"), NG * blk + g + 1)
                act.activation(qT[:, g, :], bank[7 - g % 2][:, :], ACT.Identity, bias=bias_cols[:, 0, g:g + 1]).then_inc(S("qT_ready"), 1)

            def exp_scores(blk, i, g):
                n = 4 * blk + i
                act.wait_ge(S("shifted"), 2 * (NG * n + g) + 2)
                mv_, tv = prob_m[i % 2][:, GH * g:GH * (g + 1), :], prob_t[i % 2][:, GH * g:GH * (g + 1), :]
                act.activation(mv_, mv_, ACT.Exp)
                act.activation(tv, tv, ACT.Exp).then_inc(S("prob_ready"), 1)

            def keep_probT(blk, i, g):
                n = 4 * blk + i
                act.wait_ge(S("prob_turned"), (NG + 1) * n + g + 1)
                if g == 0:
                    act.wait_ge(S("pv_mm"), n)
                rows = KM if g < NG else P
                act.activation(probT[0:rows, GH * g:GH * (g + 1), :], bank[4 + g % 2][0:rows, :].rearrange("p (h n) -> p h n", h=GH),
                               ACT.Copy).then_inc(S("probT_ready"), 1)

            with act.Fori(0, NBLK) as blk:
                for g in range(NG):
                    keep_q(blk, g)
                for i in range(5):
                    for g in range(NG):
                        if i < 4:
                            exp_scores(blk, i, g)
                        if i > 0:
                            keep_probT(blk, i - 1, g)
                    if i > 0:
                        keep_probT(blk, i - 1, NG)

            act.wait_ge(dve_once, at("ln3_var"))
            act.activation(nrm[:, 0, :], mv[:, :, 1], ACT.Sqrt, bias=eps_col[:, :]).then_inc(act_once, reached("ln3_sd"))
            with act.Fori(0, NT // 2) as i:
                for p in range(2):
                    t = 2 * i + p
                    act.wait_ge(S("x3_turned"), t + 1)
                    if p == 0:
                        act.wait_ge(S("route_mm"), 2 * i)
                    act.activation(x3T[:, p, :, :], bank[p][:, 0:D].rearrange("p (k n) -> p k n", k=KD), ACT.Copy
                                   ).then_inc(S("x3T_ready"), 1)

            def keep_hidden(n):
                for f in range(2):
                    act.wait_ge(S("up_mm"), 2 * n + f + 1)
                    if f == 0:
                        act.wait_ge(S("h_turned"), 2 * n)
                    act.activation(hid_e[:, f * 512:(f + 1) * 512], bank[f][:, :], ACT.Copy).then_inc(S("h_kept"), 1)

            def relu_half(n):
                e = act.value_load(expert_i[0:1, ds(n, 1)], min_val=0, max_val=NE - 1)
                act.wait_ge(S("h_turned"), 2 * n + 2)
                act.wait_ge(S("down_mm"), n)
                for f in range(4, 8):
                    i = act.activation(hidT[:, f, :], bank[3][:, (f - 4) * P:(f - 3) * P], ACT.Relu, bias=b1_cols[:, ds(e * NFF + f, 1)])
                i.then_inc(S("hT_half_b"), 1)

            act.wait_ge(dve_once, at("block_expert_ready"))
            keep_hidden(0)
            with act.Fori(0, NB - 1) as n:
                relu_half(n)
                keep_hidden(n + 1)
            relu_half(NB - 1)

        @block.vector
        def _(dve):
            dve.memset(eps_col[:, :], EPS).then_inc(dve_once, reached("eps_set"))
            for q in range(4):
                dve.wait_ge(S(f"x_loaded{q}"), 16)
                with dve.Fori(4 * q, 4 * q + 4) as t:
                    dve.bn_stats(stats[:, ds(t, 1), :], xres[:, ds(t, 1), :]).then_inc(S("bn_done"), 1)
            dve.wait_ge(S("bn_done"), NT)
            for t in range(NT):
                dve.bn_aggr(mv[:, t, :], stats[:, t, :]).then_inc(S("ln_agg"), 1)
            dve.wait_ge(S("ln_agg"), NT)
            dve.tensor_copy(nrm[:, 5, :], mv[:, :, 0]).then_inc(dve_once, reached("ln_var"))
            dve.wait_ge(act_once, at("ln_sd"))
            dve.reciprocal(nrm[:, 0, :], nrm[:, 0, :]).then_inc(dve_once, reached("rstd_1"))
            dve.wait_ge(dve_once, at("rstd_1"))
            dve.tensor_tensor(nrm[:, 1, :], mv[:, :, 1], nrm[:, 0, :], ALU.mult).then_inc(dve_once, reached("rstd_2"))
            dve.wait_ge(dve_once, at("rstd_2"))
            dve.tensor_tensor(nrm[:, 1, :], nrm[:, 1, :], nrm[:, 0, :], ALU.mult).then_inc(dve_once, reached("rms_var"))
            dve.wait_ge(act_once, at("rms_sd"))
            dve.reciprocal(nrm[:, 3, :], nrm[:, 2, :]).then_inc(dve_once, reached("rstd_3"))
            dve.wait_ge(dve_once, at("rstd_3"))
            dve.tensor_tensor(nrm[:, 3, :], nrm[:, 3, :], nrm[:, 0, :], ALU.mult).then_inc(dve_once, reached("rstd_4"))
            dve.wait_ge(S("w_loaded"), 16 * 2)
            dve.wait_ge(S("small_loaded"), 16 * 7)
            for k in range(KD):
                dve.tensor_scalar(w_in[:, k, 0:DI], w_in[:, k, 0:DI], norm_w[:, k:k + 1], 0.5, ALU.mult, ALU.mult
                                  ).then_inc(S("weights_ready"), 1)
                dve.tensor_scalar(w_in[:, k, DI:], w_in[:, k, DI:], norm_w[:, k:k + 1], None, ALU.mult
                                  ).then_inc(S("weights_ready"), 1)
            for k in range(NZ):
                dve.tensor_scalar(w_out[:, k, :], w_out[:, k, :], gnorm_w[:, k:k + 1], None, ALU.mult
                                  ).then_inc(S("weights_ready"), 1)
            dve.tensor_scalar(conv_w[:, :, :], conv_w[:, :, :], 0.5, None, ALU.mult).then_inc(S("weights_ready"), 1)
            dve.tensor_scalar(conv_b[:, :], conv_b[:, :], 0.5, None, ALU.mult).then_inc(S("weights_ready"), 1)
            dve.wait_ge(dve_once, at("rstd_4"))

            def add_dt_bias(t, p):
                dve.wait_ge(S("dt_mm"), t + 1)
                dve.tensor_tensor(dt_raw[:, ds(t * H, H)], bank[2 + p][:, 0:H], dt_bias[:, :], ALU.add
                                  ).then_inc(S("dt_kept"), 1)

            with dve.Fori(0, NT // 2) as i:
                for p in range(2):
                    t = 2 * i + p
                    if p == 0:
                        dve.wait_ge(S("res_added"), 2 * i)
                        dve.wait_ge(S("xn_transposed"), 2 * i)
                    xt = xres[:, ds(t, 1), :].rearrange("p a d -> p (a d)")
                    dve.tensor_scalar(xn[:, p, :], xt, nrm[:, 5, ds(t, 1)], nrm[:, 3, ds(t, 1)],
                                      ALU.subtract, ALU.mult).then_inc(S("xn_ready"), 1)
                    dve.tensor_scalar(x0[:, p, :], xt, nrm[:, 5, ds(t, 1)], nrm[:, 0, ds(t, 1)],
                                      ALU.subtract, ALU.mult).then_inc(S("x0_ready"), 1)
                for p in range(2):
                    add_dt_bias(2 * i + p, p)
            dve.wait_ge(S("res_added"), NT)
            dve.wait_ge(S("xnT_ready"), NT)
            dve.wait_ge(S("dt_kept"), NT)
            dve.tensor_scalar(dt_neg, dt_raw, -1.0, None, ALU.mult).then_inc(dve_once, reached("dt_steps_1"))
            dve.tensor_scalar(dt_pos, dt_raw, 0.0, None, ALU.max).then_inc(dve_once, reached("dt_steps_2"))
            dve.wait_ge(dve_once, at("dt_steps_2"))
            dve.tensor_tensor(dt_neg, dt_neg, dt_raw, ALU.min).then_inc(dve_once, reached("dt_abs"))

            def silu_conv(blk, f):
                dve.wait_ge(S("tanh_c_ready"), NX * blk + f + 1)
                dve.scalar_tensor_tensor(xbcT[:, f, ds(blk * BLK, BLK)], tanh_c[:, f % 2, :], 1.0, conv[:, f % 2, :],
                                         ALU.add, ALU.mult).then_inc(S("conv_done"), 1)

            dve.wait_ge(S("weights_ready"), 2 * KD + NZ + 2)
            with dve.Fori(0, B) as b:
                dve.wait_ge(S("raw_used"), NX * (NBLK // B) * b)
                dve.memset(raw[:, :, 0:TAPS - 1], 0.0).then_inc(S("past_cleared"), 1)
                with dve.Fori(0, NBLK // B) as j:
                    dve.wait_ge(S("past_cleared"), b + 1)
                    blk = b * (NBLK // B) + j
                    for f in range(NZ):
                        dve.wait_ge(S("tanh_z_ready"), NZ * blk + f + 1)
                        dve.scalar_tensor_tensor(zsT[:, f, ds(blk * BLK, BLK)], tanh_z[:, f % 2, :], 1.0, bank[f % 5][:, :],
                                                 ALU.add, ALU.mult).then_inc(S("zs_ready"), 1)
                    for f in range(NX):
                        dve.wait_ge(S("raw_ready"), NX * blk + f + 1)
                        acc = conv[:, f % 2, :]
                        dve.wait_ge(S("conv_done"), NX * blk + max(f - 1, 0))
                        dve.tensor_scalar(acc, raw[:, f, 0:BLK], conv_w[:, f, 0:1], conv_b[:, f:f + 1], ALU.mult, ALU.add
                                          ).then_inc(S("tap_done"), 1)
                        for k in range(1, TAPS):
                            dve.wait_ge(S("tap_done"), (TAPS - 1) * (NX * blk + f) + k)
                            i = dve.scalar_tensor_tensor(acc, raw[:, f, k:k + BLK], conv_w[:, f, k:k + 1], acc, ALU.mult, ALU.add)
                            i.then_inc(S("tap_done") if k < TAPS - 1 else S("conv_sum"), 1)
                        dve.tensor_copy(raw[:, f, 0:TAPS - 1], raw[:, f, BLK:BLK + TAPS - 1]).then_inc(S("raw_used"), 1)
                        if f >= 1:
                            silu_conv(blk, f - 1)
                    silu_conv(blk, NX - 1)

            dve.wait_ge(act_once, at("dt_ln"))
            dve.tensor_tensor(dt_v, dt_pos, dt_exp, ALU.add).then_inc(dve_once, reached("dt_sum"))
            dve.wait_ge(dve_once, at("dt_sum"))
            dve.wait_ge(act_once, at("a_exp"))
            dve.scalar_tensor_tensor(th(dta), th(dt_v), -1.0, a_log[:, :].unsqueeze(1).broadcast_to([P, NT, H]),
                                     ALU.mult, ALU.mult).then_inc(dve_once, reached("dt_ready"))
            dve.wait_ge(act_once, at("dec_exp"))
            dve.tensor_copy(tot, bank[1][:, 0:NT * H]).then_inc(dve_once, reached("tot_kept"))
            dve.wait_ge(dve_once, at("tot_kept"))
            dve.wait_ge(act_once, at("ecum_exp"))
            dve.tensor_tensor(wend, tot, bank[0][:, 0:NT * H], ALU.subtract).then_inc(dve_once, reached("wend_diff"))
            dve.memset(th(ecum)[:, 0:NT:TB, :], 0.0).then_inc(dve_once, reached("first_cleared_1"))
            dve.memset(th(dec)[:, 0:NT:TB, :], 0.0).then_inc(dve_once, reached("first_cleared_2"))
            dve.wait_ge(dve_once, at("first_cleared_2"))
            dve.wait_ge(act_once, at("wend_exp"))
            dve.tensor_tensor(wend, wend, dt_v, ALU.mult).then_inc(dve_once, reached("decay_ready"))
            dve.wait_ge(dve_once, at("decay_ready"))
            dve.wait_ge(S("conv_done"), NX * NBLK)

            def chunk_sides(t, p, wait):
                dve.wait_ge(S("g_mm"), t + 1)
                if wait:
                    dve.wait_ge(S("state_mm"), t - 1)
                dve.tensor_copy(b_tok[:, p, :], bank[1][:, 0:P])
                if wait:
                    dve.wait_ge(S("m_ready"), t - 1)
                dve.tensor_tensor(gmat[:, p, :], bank[1][:, P:2 * P], tri_le[:, :], ALU.mult).then_inc(S("g_ready"), 1)
                xv = bank[0][:, :].rearrange("p (h n) -> p h n", h=H)
                for dst, col in ((xdt, dt_v), (xend, wend)):
                    dve.tensor_tensor(dst[:, p, :].rearrange("p (h n) -> p h n", h=H), xv, heads(col[:, ds(t * H, H)], HP),
                                      ALU.mult)
                if wait:
                    dve.wait_ge(S("y_ready"), t - 1)
                dve.tensor_tensor(xskip[:, p, :].rearrange("p (h n) -> p h n", h=H), xv, heads(d_skip[:, :], HP),
                                  ALU.mult).then_inc(S("sides_ready"), 1)

            def gate(t, p, wait):
                dve.wait_ge(S("y_transposed"), t + 1)
                if wait:
                    dve.wait_ge(S("out_mm"), t - 1)
                    dve.wait_ge(S("sq_ready"), t - 1)
                dve.tensor_tensor(gated[:, p, :, :], bank[7][:, :].rearrange("p (k n) -> p k n", k=NZ),
                                  zsT[:, :, ds(t * P, P)], ALU.mult).then_inc(S("gated_ready"), 1)

            def sum_y(t, p, wait):
                yv = y_in[:, p, :]
                dve.wait_ge(S("inter_mm"), t + 1)
                if wait:
                    dve.wait_ge(S("y_transposed"), t - 1)
                dve.tensor_tensor(yv.rearrange("p (h n) -> p h n", h=H), bank[4][:, :].rearrange("p (h n) -> p h n", h=H),
                                  heads(ecum[:, ds(t * H, H)], HP), ALU.mult).then_inc(S("y_part"), 1)
                dve.wait_ge(S("intra_mm"), t + 1)
                dve.wait_ge(S("y_part"), 2 * t + 1)
                dve.tensor_tensor(yv, yv, bank[5][:, :], ALU.add).then_inc(S("y_part"), 1)
                dve.wait_ge(S("y_part"), 2 * t + 2)
                dve.wait_ge(S("sides_ready"), t + 1)
                dve.tensor_tensor(yv, yv, xskip[:, p, :], ALU.add).then_inc(S("y_ready"), 1)
                dve.wait_ge(S("state_mm"), t + 1)
                dve.wait_ge(S("state_decayed"), t + 1)
                dve.tensor_tensor(state, state, bank[6][:, :], ALU.add).then_inc(S("state_added"), 1)

            chunk_sides(0, 0, False)
            chunk_sides(1, 1, False)
            sum_y(0, 0, False)

            def dve_step(t, p, wait=True):
                chunk_sides(t + 1, 1 - p, True)
                gate(t - 1, 1 - p, wait)
                sum_y(t, p, wait)
            dve_step(1, 1, False)
            dve_step(2, 0)
            with dve.Fori(1, NT // 2 - 1) as i:
                dve_step(2 * i + 1, 1)
                dve_step(2 * i + 2, 0)
            gate(NT - 2, 0, True)
            sum_y(NT - 1, 1, True)
            gate(NT - 1, 1, True)

            dve.wait_ge(act_once, at("gn_sd"))
            dve.reciprocal(ssq[:, 1, :], ssq[:, 1, :]).then_inc(dve_once, reached("gn_rstd"))
            dve.wait_ge(dve_once, at("gn_rstd"))
            dve.wait_ge(S("state_added"), NT)
            dve.wait_ge(S("y_ready"), NT)
            with dve.Fori(0, NT // 2) as i:
                for p in range(2):
                    t = 2 * i + p
                    if p == 0:
                        dve.wait_ge(S("res_y_added"), 2 * i)
                        dve.wait_ge(S("y_st_transposed"), 2 * i)
                    yt = y_tok[:, ds(t, 1), :].rearrange("p a d -> p (a d)")
                    dve.tensor_scalar(y_st[:, p, :], yt, ssq[:, 1, ds(t, 1)], None, ALU.mult).then_inc(S("y_st_ready"), 1)
                    dve.tensor_scalar(yt, yt, ssq[:, 1, ds(t, 1)], None, ALU.mult).then_inc(S("y_tok_ready"), 1)
            dve.wait_ge(S("mem_w_loaded"), 16 * 7)
            dve.tensor_copy(scorer_w2b[:, :], scorer_w2[:, 0:1].broadcast_to([SD, P])).then_inc(dve_once, reached("w2b_ready"))
            dve.wait_ge(pool_once, at("pos_set"))
            dve.tensor_copy(pos[:, :], pos_i[:, :]).then_inc(dve_once, reached("pos_ready"))
            dve.memset(cols[:, :, :], 0.0).then_inc(dve_once, reached("cols_cleared"))
            with dve.Fori(0, NBLK // 2) as i:
                for p in range(2):
                    blk = 2 * i + p
                    dve.wait_ge(S("hid_mm"), blk + 1)
                    if p == 0:
                        dve.wait_ge(S("score_mm"), 2 * i)
                    dve.tensor_scalar(hid[0:SD, p, :], bank[2 + 4 * p][0:SD, :], 0.0, None, ALU.max).then_inc(S("hid_ready"), 1)
            with dve.Fori(0, NBLK) as blk:
                dve.wait_ge(S("score_tanh"), blk + 1)
                sv = sig[:, ds(blk * BLK, BLK)]
                dve.tensor_scalar(sv, sv, 0.5, 0.5, ALU.mult, ALU.add).then_inc(S("sig_ready"), 1)
            dve.wait_ge(S("sig_ready"), NBLK)
            dve.wait_ge(dve_once, at("cols_cleared"))
            with dve.Fori(0, NT) as t:
                dve.wait_ge(S("s_col_ready"), t)
                dve.scalar_tensor_tensor(junk[:, 0:P], sig[:, ds(t * P, P)], 1.0, ident[:, :], ALU.mult, ALU.mult,
                                         accum_out=s_col[:, ds(t, 1)]).then_inc(S("s_col_ready"), 1)
            dve.wait_ge(S("s_col_ready"), NT)
            dve.tensor_scalar(valid, s_col, 0.5, None, ALU.is_gt).then_inc(dve_once, reached("valid_ready"))
            RANKS = 3 * TB - 1
            with dve.Fori(0, B) as b:
                n = 0
                for k in range(TB):
                    sc = s_col[:, ds(b * TB + k, 1)]
                    if k:
                        dve.wait_ge(S("rank_counted"), RANKS * b + n)
                        dve.tensor_scalar(junk[:, 0:k * P], sig[:, ds(b * T, k * P)], sc, None, ALU.is_ge, ALU.add,
                                          accum_out=n_ge[:, ds(b * TB + k, 1)]).then_inc(S("rank_counted"), 1)
                        n += 1
                    dve.wait_ge(S("rank_counted"), RANKS * b + n)
                    dve.tensor_scalar(junk[:, 0:T - k * P], sig[:, ds(b * T + k * P, T - k * P)], sc, None, ALU.is_gt, ALU.add,
                                      accum_out=n_gt[:, ds(b * TB + k, 1)]).then_inc(S("rank_counted"), 1)
                    n += 1
                    dve.wait_ge(S("rank_counted"), RANKS * b + n)
                    dve.scalar_tensor_tensor(junk[:, 0:P], sig[:, ds(b * T + k * P, P)], sc, tri_gt[:, :], ALU.is_equal, ALU.mult,
                                             accum_out=n_eq[:, ds(b * TB + k, 1)]).then_inc(S("rank_counted"), 1)
                    n += 1
                assert n == RANKS
            dve.wait_ge(S("rank_counted"), RANKS * B)
            dve.tensor_tensor(rank, n_ge, n_gt, ALU.add).then_inc(dve_once, reached("rank_sum_1"))
            dve.wait_ge(dve_once, at("rank_sum_1"))
            dve.tensor_tensor(rank, rank, n_eq, ALU.add).then_inc(dve_once, reached("rank_sum_2"))
            dve.wait_ge(dve_once, at("rank_sum_2"))
            dve.wait_ge(S("mean_mm"), 1)
            dve.tensor_reduce(mean_s[:, :], bank[6][:, 0:NT].rearrange("p (b t) -> p b t", b=B), AX, ALU.add).then_inc(dve_once, reached("mean_ready_1"))
            dve.wait_ge(dve_once, at("mean_ready_1"))
            dve.tensor_scalar(mean_s[:, :], mean_s[:, :], 1.0 / T, 0.3, ALU.mult, ALU.is_gt).then_inc(dve_once, reached("mean_ready_2"))
            dve.wait_ge(dve_once, at("valid_ready"))
            dve.wait_ge(dve_once, at("pos_ready"))
            dve.wait_ge(dve_once, at("mean_ready_2"))
            with dve.Fori(0, B) as b:
                dve.wait_ge(S("select_mm"), b)
                dve.tensor_tensor(onehot, pos[:, :].unsqueeze(1).broadcast_to([P, TB, POOL]),
                                  rank[:, ds(b * TB, TB)].unsqueeze(2).broadcast_to([P, TB, POOL]), ALU.is_equal
                                  ).then_inc(S("onehot_part"), 1)
                dve.wait_ge(S("onehot_part"), b + 1)
                dve.tensor_tensor(onehot, onehot, valid[:, ds(b * TB, TB)].unsqueeze(2).broadcast_to([P, TB, POOL]), ALU.mult
                                  ).then_inc(S("onehot_ready"), 1)
                dve.wait_ge(S("select_mm"), b + 1)
                dve.wait_ge(S("logit_biased"), 2 * b)
                dve.tensor_copy(pool_tok[0:POOL, :], bank[5][0:POOL, 0:D]).then_inc(S("pool_tok_ready"), 1)
                dve.tensor_scalar(vbias[:, :], bank[6][:, 0:POOL], -1.0, 1e9, ALU.add, ALU.mult).then_inc(S("vbias_ready"), 1)
                dve.wait_ge(S("val_mm"), b + 1)
                dve.tensor_scalar(val[0:POOL, :], bank[6][0:POOL, 0:D], mean_s[0:POOL, ds(b, 1)], None, ALU.mult
                                  ).then_inc(S("val_ready"), 1)
                dve.wait_ge(S("vbias_ready"), b + 1)
                for j in range(T // BLK):
                    n = (T // BLK) * b + j
                    dve.wait_ge(S("logit_mm"), n + 1)
                    dve.wait_ge(S("attn_turned"), n)
                    dve.tensor_tensor(logit, bank[1][:, 0:4 * 64].rearrange("p (i n) -> p i n", i=4)[:, :, 0:POOL],
                                      vbias[:, :].unsqueeze(1).broadcast_to([P, 4, POOL]), ALU.add).then_inc(S("logit_biased"), 1)
                    dve.wait_ge(S("logit_biased"), n + 1)
                    dve.tensor_reduce(red[:, 0, :], logit, AX, ALU.max).then_inc(S("logit_max"), 1)
                    dve.wait_ge(S("logit_max"), n + 1)
                    dve.tensor_tensor(logit, logit, red[:, 0, :].unsqueeze(2).broadcast_to([P, 4, POOL]), ALU.subtract
                                      ).then_inc(S("logit_shifted"), 1)
                    dve.wait_ge(S("logit_exp"), n + 1)
                    dve.tensor_reduce(red[:, 1, :], logit, AX, ALU.add).then_inc(S("attn_sum"), 1)
                    dve.wait_ge(S("attn_sum"), n + 1)
                    dve.reciprocal(red[:, 2, :], red[:, 1, :]).then_inc(S("attn_inv"), 1)
                    dve.wait_ge(S("attn_inv"), n + 1)
                    dve.tensor_tensor(logit, logit, red[:, 2, :].unsqueeze(2).broadcast_to([P, 4, POOL]), ALU.mult
                                      ).then_inc(S("attn_ready"), 1)
                    for m in range(KD):
                        dve.wait_ge(S("gate_tanh"), KD * n + m + 1)
                        if m == 0:
                            dve.wait_ge(S("upd_turned"), 2 * n)
                        dve.scalar_tensor_tensor(upd[:, m, :], gate_t[:, m, :], 1.0, retT[:, m, :], ALU.add, ALU.mult
                                                 ).then_inc(S("upd_ready"), 1)
                    for m in range(2):
                        dve.wait_ge(S("upd_turned"), 2 * n + m + 1)
                        if j == 0 and m == 0:
                            dve.wait_ge(S("res_y_added"), NT)
                        xv = xres[:, ds(4 * n + 2 * m, 2), :]
                        dve.scalar_tensor_tensor(xv, bank[7 * (1 - m)][:, :].rearrange("p (t d) -> p t d", t=2), 0.5, xv,
                                                 ALU.mult, ALU.add).then_inc(S("x1_ready"), 1)

            dve.wait_ge(S("x1_ready"), 2 * NBLK)
            with dve.Fori(0, NT) as t:
                dve.bn_stats(stats[:, ds(t, 1), :], xres[:, ds(t, 1), :]).then_inc(S("bn_done"), 1)
            dve.wait_ge(S("bn_done"), 2 * NT)
            for t in range(NT):
                dve.bn_aggr(mv[:, t, :], stats[:, t, :]).then_inc(S("ln_agg"), 1)
            dve.wait_ge(S("ln_agg"), 2 * NT)
            dve.tensor_copy(nrm[:, 5, :], mv[:, :, 0]).then_inc(dve_once, reached("ln2_var"))
            dve.wait_ge(act_once, at("ln2_sd"))
            dve.reciprocal(nrm[:, 0, :], nrm[:, 0, :]).then_inc(dve_once, reached("ln2_rstd"))
            dve.wait_ge(dve_once, at("ln2_rstd"))
            dve.wait_ge(S("select_mm"), B)
            with dve.Fori(0, NT // 2) as i:
                for p in range(2):
                    t = 2 * i + p
                    if p == 0:
                        dve.wait_ge(S("ln2_transposed"), 2 * i)
                    dve.tensor_scalar(ln_st[:, p, :], xres[:, ds(t, 1), :].rearrange("p a d -> p (a d)"), nrm[:, 5, ds(t, 1)],
                                      nrm[:, 0, ds(t, 1)], ALU.subtract, ALU.mult).then_inc(S("ln2_ready"), 1)
            dve.wait_ge(S("x_w_loaded"), 16 * 9)
            dve.tensor_scalar(mask_row[:, :], mask_i[:, :], 0.0, 4 * NEG, ALU.is_gt, ALU.mult).then_inc(dve_once, reached("mask_row_ready"))
            dve.wait_ge(S("bias_turned"), 1)
            dve.tensor_copy(bias_cols[:, :, :], bank[2][:, 0:2 * NG].rearrange("p (n g) -> p n g", n=2)).then_inc(dve_once, reached("bias_cols_ready"))
            dve.wait_ge(dve_once, at("bias_cols_ready"))
            dve.wait_ge(pool_once, at("pads_zero_5"))
            for b in range(B):
                for g in range(NG):
                    n = NG * b + g
                    dve.wait_ge(S("keys_mm"), n + 1)
                    for h in range(GH):
                        r = slice(32 * h, 32 * h + 32)
                        i = dve.tensor_scalar(keys[r, b, g, h * LK:(h + 1) * LK], bank[3 + n % 2][r, 0:LK], bias_cols[r, 1, g:g + 1], 0.25,
                                              ALU.add, ALU.mult)
                    i.then_inc(S("keys_ready"), 1)
                dve.wait_ge(S("val_main_mm"), b + 1)
                dve.tensor_copy(v_main[0:KM, b, :, 0:HD], bank[5][0:KM, 0:D].rearrange("p (h d) -> p h d", d=HD)).then_inc(S("v_main_ready"), 1)
                dve.wait_ge(S("val_tail_mm"), b + 1)
                for h in range(GH):
                    r = slice(32 * h, 32 * h + 32)
                    dve.memset(v_tail[r, b, :, h * (HD + 1) + HD:(h + 1) * (HD + 1)], 1.0)
                    i = dve.tensor_copy(v_tail[r, b, :, h * (HD + 1):h * (HD + 1) + HD],
                                        bank[6][r, 0:D].rearrange("p (g h d) -> p g h d", g=NG, h=GH)[:, :, h, :])
                i.then_inc(S("v_tail_ready"), 1)

            def shift_scores(blk, i, g):
                n = 4 * blk + i
                for j in range(2):
                    m = 2 * (NG * n + g) + j
                    h0 = GH * g + 2 * j
                    sc = bank[(2 * g + j) % 4][:, 0:2 * LK].rearrange("p (h n) -> p h n", h=2)
                    dve.wait_ge(S("score_x_mm"), m + 1)
                    mx = xmax[:, i % 2, h0:h0 + 2]
                    dve.tensor_reduce(mx, sc, AX, ALU.max).then_inc(S("score_max"), 1)
                    dve.wait_ge(S("score_max"), m + 1)
                    dve.tensor_tensor(prob_m[i % 2][:, h0:h0 + 2, :], sc[:, :, 0:KM], mx.unsqueeze(2).broadcast_to([P, 2, KM]), ALU.subtract)
                    dve.tensor_tensor(prob_t[i % 2][:, h0:h0 + 2, :], sc[:, :, KM:LK], mx.unsqueeze(2).broadcast_to([P, 2, KT]), ALU.subtract
                                      ).then_inc(S("shifted"), 1)

            def weigh(blk, i):
                n = 4 * blk + i
                dve.wait_ge(S("pv_mm"), n + 1)
                ov = bank[7][:, 0:XH * (HD + 1)].rearrange("p (h c) -> p h c", c=HD + 1)
                dve.reciprocal(xinv[:, i % 2, :], ov[:, :, HD]).then_inc(S("x_inv"), 1)
                dve.wait_ge(S("x_inv"), n + 1)
                if i < 2:
                    dve.wait_ge(S("x2_ready"), 4 * blk)
                else:
                    dve.wait_ge(S("x2_ready"), 4 * blk + i - 1)
                dve.tensor_tensor(head_o[:, i % 2, :].rearrange("p (h d) -> p h d", d=HD), ov[:, :, 0:HD],
                                  xinv[:, i % 2, :].unsqueeze(2).broadcast_to([P, XH, HD]), ALU.mult).then_inc(S("head_o_ready"), 1)

            with dve.Fori(0, NBLK) as blk:
                for i in range(5):
                    for g in range(NG):
                        if i < 4:
                            if g == 0 and i >= 2:
                                dve.wait_ge(S("prob_turned"), (NG + 1) * (4 * blk + i - 1))
                            elif g == 0:
                                dve.wait_ge(S("prob_turned"), (NG + 1) * 4 * blk)
                            shift_scores(blk, i, g)
                    if i > 0:
                        weigh(blk, i - 1)

            dve.wait_ge(S("x2_ready"), NT)
            with dve.Fori(0, NT) as t:
                dve.bn_stats(stats[:, ds(t, 1), :], xres[:, ds(t, 1), :]).then_inc(S("bn_done"), 1)
            dve.wait_ge(S("bn_done"), 3 * NT)
            for t in range(NT):
                dve.bn_aggr(mv[:, t, :], stats[:, t, :]).then_inc(S("ln_agg"), 1)
            dve.wait_ge(S("ln_agg"), 3 * NT)
            dve.tensor_copy(nrm[:, 5, :], mv[:, :, 0]).then_inc(dve_once, reached("ln3_var"))
            dve.wait_ge(act_once, at("ln3_sd"))
            dve.reciprocal(nrm[:, 0, :], nrm[:, 0, :]).then_inc(dve_once, reached("ln3_rstd"))
            dve.wait_ge(dve_once, at("ln3_rstd"))
            dve.wait_ge(S("route_w_loaded"), 16 * 3)
            with dve.Fori(0, NT // 2) as i:
                for p in range(2):
                    t = 2 * i + p
                    if p == 0:
                        dve.wait_ge(S("x3_turned"), 2 * i)
                    dve.tensor_scalar(ln_st[:, p, :], xres[:, ds(t, 1), :].rearrange("p a d -> p (a d)"), nrm[:, 5, ds(t, 1)],
                                      nrm[:, 0, ds(t, 1)], ALU.subtract, ALU.mult).then_inc(S("x3_ready"), 1)
                for p in range(2):
                    t = 2 * i + p
                    dve.wait_ge(S("route_mm"), t + 1)
                    dve.tensor_tensor(logits[:, ds(t, 1), :].rearrange("p a e -> p (a e)"), bank[2 + p][:, 0:NE], br_row, ALU.add
                                      ).then_inc(S("logits_ready"), 1)
            dve.wait_ge(pool_once, at("counters_set"))
            dve.tensor_copy(desc, desc_i)
            dve.tensor_copy(thr, thr_i)
            dve.tensor_copy(blk_n, blk_i).then_inc(dve_once, reached("iotas_ready"))
            dve.wait_ge(dve_once, at("iotas_ready"))
            dve.wait_ge(S("logits_ready"), NT)

            def along(v, n):
                return v.unsqueeze(2).broadcast_to([P, v.shape[1], n])

            def across(v, n):
                return v.unsqueeze(1).broadcast_to([P, n, v.shape[1]])

            def link(ins):
                links[0] += 1
                ins.then_inc(S("route_step"), 1)
                dve.wait_ge(S("route_step"), links[0])
            links = [0]
            link(dve.tensor_reduce(best, logits, AX, ALU.max))
            link(dve.tensor_tensor(hot, logits, along(best, NE), ALU.is_equal))
            link(dve.tensor_tensor(hot, hot, across(desc, NT), ALU.mult))
            link(dve.tensor_reduce(best, hot, AX, ALU.max))
            dve.tensor_tensor(hot, across(desc, NT), along(best, NE), ALU.is_equal).then_inc(S("hot_ready"), 1)
            link(dve.memset(before[:, 0, :], 0.0))
            dve.wait_ge(S("count_mm"), 2)
            tile_n = bank[5][:, 0:NT * NE].rearrange("p (t e) -> p t e", e=NE)
            for t in range(NT):
                link(dve.tensor_tensor(before[:, t + 1, :], before[:, t, :], tile_n[:, t, :], ALU.add))
            link(dve.tensor_tensor(blocks_c, along(before[:, NT, :], NT), across(thr, NE), ALU.is_gt))
            link(dve.memset(first_blk[:, 0:1], 0.0))
            link(dve.tensor_reduce(first_blk[:, 1:], blocks_c, AX, ALU.add))
            for e in range(1, NE):
                link(dve.tensor_tensor(first_blk[:, e + 1:e + 2], first_blk[:, e + 1:e + 2], first_blk[:, e:e + 1], ALU.add))
            link(dve.tensor_tensor(slot_t, bank[4][:, 0:NT * NE].rearrange("p (t e) -> p t e", e=NE), before[:, 0:NT, :], ALU.add))
            link(dve.scalar_tensor_tensor(slot_t, across(first_blk[:, 0:NE], NT), float(P), slot_t, ALU.mult, ALU.add))
            link(dve.tensor_tensor(slot_t, slot_t, hot, ALU.mult))
            link(dve.tensor_reduce(slot_f, slot_t, AX, ALU.add))
            link(dve.tensor_scalar(slot_i, slot_f, -1.0, None, ALU.add))
            link(dve.tensor_tensor(expert_c, along(blk_n, NE), across(first_blk[:, 1:], NB), ALU.is_ge))
            link(dve.tensor_reduce(expert_f, expert_c, AX, ALU.add))
            dve.tensor_scalar(expert_i, expert_f, float(NE - 1), None, ALU.min).then_inc(dve_once, reached("block_expert_ready"))
            with dve.Fori(0, NT // 2) as i:
                for p in range(2):
                    t = 2 * i + p
                    dve.wait_ge(S(f"scattered{p}"), 16 * i)
                    xt = xres[:, ds(t, 1), :].rearrange("p a d -> p (a d)")
                    dve.tensor_scalar(rows[:, p, 0:D], xt, nrm[:, 5, ds(t, 1)], nrm[:, 0, ds(t, 1)], ALU.subtract, ALU.mult)
                    dve.tensor_copy(rows[:, p, D:2 * D], xt)
                    dve.tensor_copy(rows[:, p, 2 * D:].bitcast(I32), token_i[:, ds(t, 1)])
                    dve.tensor_copy(slot_now[:, p:p + 1], slot_i[:, ds(t, 1)]).then_inc(S("row_ready"), 1)

            def keep_xs(n, p):
                dve.wait_ge(S("xs_turned"), n + 1)
                dve.tensor_copy(xsT[:, p, :, :], bank[6][:, 0:D].rearrange("p (k n) -> p k n", k=KD)).then_inc(S("xsT_ready"), 1)

            def relu_and_add(n, p):
                e = dve.value_load(expert_i[0:1, ds(n, 1)], min_val=0, max_val=NE - 1)
                dve.wait_ge(S("h_turned"), 2 * n + 1)
                dve.wait_ge(S("down_mm"), n)
                for f in range(4):
                    i = dve.tensor_scalar(hidT[:, f, :], bank[2][:, f * P:(f + 1) * P], b1_cols[:, ds(e * NFF + f, 1)], 0.0, ALU.add, ALU.max)
                i.then_inc(S("hT_half_a"), 1)
                dve.wait_ge(S(f"rest_loaded{p}"), 8 * (n - p) + 16)
                dve.wait_ge(S(f"out_stored{p}"), 8 * (n - p))
                dve.tensor_tensor(yo[:, p, :], rest[:, p, 0:D], b2_rows[:, ds(e, 1), :].rearrange("p a d -> p (a d)"), ALU.add
                                  ).then_inc(S("yo_part"), 1)
                dve.wait_ge(S("yo_part"), n + 1)
                dve.wait_ge(S("down_mm"), n + 1)
                dve.tensor_tensor(yo[:, p, :], yo[:, p, :], bank[4][:, 0:D], ALU.add).then_inc(S("yo_ready"), 1)

            dve.wait_ge(S("w2_loaded"), 16 * 2 * NE)
            keep_xs(0, 0)
            with dve.Fori(0, NB // 2) as i:
                keep_xs(2 * i + 1, 1)
                relu_and_add(2 * i, 0)
                keep_xs(2 * i + 2, 0)
                relu_and_add(2 * i + 1, 1)
            relu_and_add(NB - 1, 0)

        @block.tensor
        def _(pe):
            pe.wait_ge(pool_once, at("masks_set_3"))
            pe.wait_ge(S("weights_ready"), 2 * KD + NZ + 2)

            def dt_product(t, p):
                pe.wait_ge(S("xn_tile_ready"), t + 1)
                for k in range(KD):
                    i = pe.matmul(bank[2 + p][:, 0:H], xn_tile[:, p, k, :], w_in[:, k, DI + NX * P:], start=(k == 0), stop=(k == KD - 1))
                i.then_inc(S("dt_mm"), 1)

            with pe.Fori(0, NT // 2) as i:
                pe.wait_ge(S("dt_kept"), 2 * i)
                for p in range(2):
                    t = 2 * i + p
                    pe.wait_ge(S("xn_ready"), t + 1)
                    if p == 0:
                        pe.wait_ge(S("xn_tile_ready"), 2 * i)
                    for k in range(KD):
                        m = pe.transpose(bank[p][:, k * P:(k + 1) * P], xn[:, p, k * P:(k + 1) * P], ident[:, :])
                    m.then_inc(S("xn_transposed"), 1)
                for p in range(2):
                    dt_product(2 * i + p, p)
            pe.wait_ge(S("xnT_ready"), NT)
            pe.wait_ge(S("dt_kept"), NT)
            with pe.Fori(0, NBLK) as blk:
                pe.wait_ge(S("raw_ready"), NX * blk)
                pe.wait_ge(S("zs_ready"), NZ * blk)
                for f in range(NZ + NX):
                    if 5 <= f < 5 + NZ:
                        pe.wait_ge(S("zs_ready"), NZ * blk + f - 4)
                    if f == 5 + NZ:
                        pe.wait_ge(S("raw_ready"), NX * blk + 1)
                    for k in range(KD):
                        m = pe.matmul(bank[f % 5][:, :], w_in[:, k, f * P:(f + 1) * P], featT[:, k, ds(blk * BLK, BLK)],
                                      start=(k == 0), stop=(k == KD - 1))
                    m.then_inc(S("proj_mm"), 1)
            pe.wait_ge(dve_once, at("dt_ready"))
            pe.wait_ge(S("raw_ready"), NX * NBLK)
            pe.wait_ge(S("zs_ready"), NZ * NBLK)
            pe.matmul(bank[0][:, 0:NT * H], tri_le[:, :], dta, start=True, stop=True).then_inc(S("cum_mm"), 1)
            pe.matmul(bank[1][:, 0:NT * H], ones[:, :], dta, start=True, stop=True).then_inc(S("cum_mm"), 1)
            pe.wait_ge(dve_once, at("decay_ready"))

            def turn(t, p, wait):
                pe.wait_ge(S(f"chunk_loaded{p}"), 8 * (t - p) + 16)
                if wait:
                    pe.wait_ge(S("sides_ready"), t)
                for k in range(NZ):
                    pe.transpose(bank[0][:, k * P:(k + 1) * P], xbc[:, p, k, :], ident[:, :])
                pe.transpose(bank[1][:, 0:P], xbc[:, p, NZ, :], ident[:, :])
                pe.matmul(bank[1][:, P:2 * P], xbc[:, p, NZ, :], xbc[:, p, NZ + 1, :], start=True, stop=True
                          ).then_inc(S("g_mm"), 1)

            def segments(t, p, wait):
                pe.wait_ge(S("seg_ready"), t + 1)
                if wait:
                    pe.wait_ge(S("decay_mat"), t)
                for q in range(2):
                    m = pe.matmul(bank[2 + q][:, :], tri_gt[:, :], seg[:, p, 4 * q:4 * q + 4, :], start=True, stop=True)
                m.then_inc(S("seg_mm"), 1)

            def transpose_y(t, p, wait):
                pe.wait_ge(S("y_ready"), t + 1)
                if wait:
                    pe.wait_ge(S("out_kept"), t)
                for k in range(NZ):
                    m = pe.transpose(bank[7][:, k * P:(k + 1) * P], y_in[:, p, k * P:(k + 1) * P], ident[:, :])
                m.then_inc(S("y_transposed"), 1)

            def mix(t, p, wait):
                pe.wait_ge(S("sides_ready"), t + 1)
                pe.wait_ge(S("state_added"), t) if wait else pe.wait_ge(pool_once, at("state_set"))
                pe.matmul(bank[4][:, :], xbc[:, p, NZ + 1, :], state, start=True, stop=True).then_inc(S("inter_mm"), 1)
                pe.wait_ge(S("m_ready"), t + 1)
                for h in range(H):
                    m = pe.matmul(bank[5][:, h * HP:(h + 1) * HP], lmat[:, p, h, :], xdt[:, p, h * HP:(h + 1) * HP],
                                  start=True, stop=True)
                m.then_inc(S("intra_mm"), 1)
                pe.matmul(bank[6][:, :], b_tok[:, p, :], xend[:, p, :], start=True, stop=True).then_inc(S("state_mm"), 1)

            def project_out(t, p):
                pe.wait_ge(S("gated_ready"), t + 1)
                for k in range(NZ):
                    pe.matmul(bank[7][:, 0:D], gated[:, p, k, :], w_out[:, k, :], start=(k == 0), stop=(k == NZ - 1))
                pe.wait_ge(S("sq_ready"), t + 1)
                for k in range(NZ):
                    m = pe.matmul(bank[7][:, D:D + 1], sq[:, p, k, :], ones[:, 0:1], start=(k == 0), stop=(k == NZ - 1))
                m.then_inc(S("out_mm"), 1)

            turn(0, 0, False)
            segments(0, 0, False)
            turn(1, 1, True)
            segments(1, 1, True)
            mix(0, 0, False)

            def pe_step(t, p, wait=True):
                turn(t + 1, 1 - p, True)
                segments(t + 1, 1 - p, True)
                transpose_y(t - 1, 1 - p, wait)
                mix(t, p, True)
                project_out(t - 1, 1 - p)
            pe_step(1, 1, False)
            pe_step(2, 0)
            with pe.Fori(1, NT // 2 - 1) as i:
                pe_step(2 * i + 1, 1)
                pe_step(2 * i + 2, 0)
            transpose_y(NT - 2, 0, True)
            mix(NT - 1, 1, True)
            project_out(NT - 2, 0)
            transpose_y(NT - 1, 1, True)
            project_out(NT - 1, 1)
            with pe.Fori(0, NT // 2) as i:
                for p in range(2):
                    t = 2 * i + p
                    pe.wait_ge(S("y_st_ready"), t + 1)
                    if p == 0:
                        pe.wait_ge(S("yT_ready"), 2 * i)
                    for k in range(KD):
                        m = pe.transpose(bank[p][:, k * P:(k + 1) * P], y_st[:, p, k * P:(k + 1) * P], ident[:, :])
                    m.then_inc(S("y_st_transposed"), 1)
            pe.wait_ge(S("yT_ready"), NT)
            pe.wait_ge(dve_once, at("w2b_ready"))
            with pe.Fori(0, NBLK // 2) as i:
                for p in range(2):
                    blk = 2 * i + p
                    if p == 0:
                        pe.wait_ge(S("hid_ready"), 2 * i)
                    for k in range(KD):
                        m = pe.matmul(bank[2 + 4 * p][0:SD, :], scorer_w1[:, k, :], featT[:, k, ds(blk * BLK, BLK)],
                                      start=(k == 0), stop=(k == KD - 1))
                    m.then_inc(S("hid_mm"), 1)
                for p in range(2):
                    blk = 2 * i + p
                    pe.wait_ge(S("hid_ready"), blk + 1)
                    pe.wait_ge(S("score_tanh"), blk)
                    pe.matmul(bank[3][:, :], scorer_w2b[:, :], hid[0:SD, p, :], start=True, stop=True).then_inc(S("score_mm"), 1)
            pe.wait_ge(S("s_col_ready"), NT)
            pe.matmul(bank[6][:, 0:NT], ones[:, :], s_col, start=True, stop=True).then_inc(S("mean_mm"), 1)
            pe.wait_ge(S("y_tok_ready"), NT)
            pe.wait_ge(dve_once, at("mean_ready_1"))
            for b in range(B):
                pe.wait_ge(S("onehot_ready"), b + 1)
                pe.wait_ge(S("gate_tanh"), 4 * b)
                for k in range(TB):
                    pe.matmul(bank[5][0:POOL, 0:D], onehot[:, k, :], y_tok[:, ds(b * TB + k, 1), :].rearrange("p a d -> p (a d)"),
                              start=(k == 0), stop=(k == TB - 1))
                for k in range(TB):
                    m = pe.matmul(bank[6][:, 0:POOL], ones[:, :], onehot[:, k, :], start=(k == 0), stop=(k == TB - 1))
                m.then_inc(S("select_mm"), 1)
                pe.wait_ge(S("pool_tok_ready"), b + 1)
                pe.wait_ge(pool_once, at("masks_set_3"))
                for k in range(KD):
                    m = pe.transpose(bank[4][:, k * POOL:(k + 1) * POOL], pool_tok[0:POOL, k * P:(k + 1) * P], ident[0:POOL, 0:POOL])
                m.then_inc(S("pool_tok_turned"), 1)
                pe.wait_ge(S("pool_tokT_ready"), b + 1)
                for k in range(KD):
                    m = pe.matmul(bank[5][0:SD, 0:POOL], summ_w[:, k, :], pool_tokT[:, k, :], start=(k == 0), stop=(k == KD - 1))
                m.then_inc(S("pool_mm"), 1)
                pe.wait_ge(S("poolT_ready"), b + 1)
                pe.wait_ge(S("mem_w_loaded"), 16 * 7)
                pe.matmul(bank[4][0:SD, 0:POOL], mem_k_w[:, :], poolT[0:SD, :], start=True, stop=True).then_inc(S("key_mm"), 1)
                pe.wait_ge(S("vbias_ready"), b + 1)
                pe.wait_ge(S("mem_w_loaded"), 16 * 7)
                pe.matmul(bank[6][0:POOL, 0:D], poolT[0:SD, :], mem_v_w[:, :], start=True, stop=True).then_inc(S("val_mm"), 1)
                for j in range(T // BLK):
                    n = (T // BLK) * b + j
                    pe.wait_ge(S("x1_ready"), 2 * n)
                    for k in range(KD):
                        m = pe.matmul(bank[0][0:SD, :], mem_q_w[:, k, :], featT[:, k, ds(n * BLK, BLK)], start=(k == 0), stop=(k == KD - 1))
                    m.then_inc(S("q_mem_mm"), 1)
                    pe.wait_ge(S("q_mem_ready"), n + 1)
                    pe.wait_ge(S("keyT_ready"), b + 1)
                    pe.wait_ge(S("mem_w_loaded"), 16 * 7)
                    for i in range(4):
                        m = pe.matmul(bank[1][:, i * 64:i * 64 + POOL], q_mem[0:SD, i * P:(i + 1) * P], keyT[0:SD, :], start=True, stop=True)
                    m.then_inc(S("logit_mm"), 1)
                    pe.wait_ge(S("attn_ready"), n + 1)
                    for i in range(4):
                        m = pe.transpose(bank[2][0:POOL, i * P:(i + 1) * P], logit[:, i, :], ident[:, :])
                    m.then_inc(S("attn_turned"), 1)
                    pe.wait_ge(S("attnT_ready"), n + 1)
                    pe.wait_ge(S("val_ready"), b + 1)
                    pe.wait_ge(S("mem_w_loaded"), 16 * 7)
                    for m_ in range(KD):
                        pe.matmul(bank[3 + m_][:, :], val[0:POOL, m_ * P:(m_ + 1) * P], attnT[0:POOL, :], start=True, stop=True
                                  ).then_inc(S("ret_mm"), 1)
                    for m_ in range(KD):
                        for k in range(2 * KD):
                            if k == KD and m_ == 0:
                                pe.wait_ge(S("retT_ready"), KD * n + KD)
                            side = featT[:, k, ds(n * BLK, BLK)] if k < KD else retT[:, k - KD, :]
                            m = pe.matmul(bank[5 + m_][:, :], gate_w[:, k, m_ * P:(m_ + 1) * P], side, start=(k == 0), stop=(k == 2 * KD - 1))
                        m.then_inc(S("gate_mm"), 1)
                    pe.wait_ge(S("upd_ready"), KD * n + KD)
                    for m_ in range(2):
                        for i in range(2):
                            for k in range(KD):
                                m = pe.transpose(bank[7 * (1 - m_)][:, (2 * i + k) * P:(2 * i + k + 1) * P],
                                                 upd[:, k, (2 * m_ + i) * P:(2 * m_ + i + 1) * P], ident[:, :])
                        m.then_inc(S("upd_turned"), 1)

            pe.wait_ge(S("x1_ready"), 2 * NBLK)
            with pe.Fori(0, NT // 2) as i:
                for p in range(2):
                    t = 2 * i + p
                    pe.wait_ge(S("ln2_ready"), t + 1)
                    if p == 0:
                        pe.wait_ge(S("hT_ready"), 2 * i)
                    for k in range(KD):
                        m = pe.transpose(bank[p][:, k * P:(k + 1) * P], ln_st[:, p, k * P:(k + 1) * P], ident[:, :])
                    m.then_inc(S("ln2_transposed"), 1)
            pe.wait_ge(S("x_w_loaded"), 16 * 9)
            pe.wait_ge(pool_once, at("bias_rows_cleared_2"))
            for n in range(2):
                m = pe.transpose(bank[2][:, n * NG:(n + 1) * NG], bias_rows[:, n, :, :].rearrange("g h c -> g (h c)"), ident[0:NG, 0:NG])
            m.then_inc(S("bias_turned"), 1)
            pe.wait_ge(S("pads_ready"), 4)
            pe.wait_ge(dve_once, at("mask_row_ready"))
            for b in range(B):
                for g in range(NG):
                    n = NG * b + g
                    if n >= 2:
                        pe.wait_ge(S("keys_ready"), n - 1)
                    for k in range(KD):
                        pe.matmul(bank[3 + n % 2][:, 0:LK], wk_pad[:, k, g * P:(g + 1) * P], ctxT[:, b, k, :], start=(k == 0), stop=False)
                    pe.matmul(bank[3 + n % 2][:, 0:LK], mask_sel[:, :], mask_row[:, b * LK:(b + 1) * LK], start=False, stop=True
                              ).then_inc(S("keys_mm"), 1)
                if b:
                    pe.wait_ge(S("v_main_ready"), b)
                    pe.wait_ge(S("v_tail_ready"), b)
                for dst, lhs, rows, done in ((bank[5], ctxT[:, b, :, 0:KM], KM, "val_main_mm"), (bank[6], tail_ctx[:, b, :, :], P, "val_tail_mm")):
                    for k in range(KD):
                        pe.matmul(dst[0:rows, 0:D], lhs[:, k, :], wv[:, k, :], start=(k == 0), stop=False)
                    pe.matmul(dst[0:rows, 0:D], ones[0:1, 0:rows], vb_row[:, :], start=False, stop=True).then_inc(S(done), 1)
            pe.wait_ge(S("hT_ready"), NT)
            pe.wait_ge(S("keys_ready"), B * NG)
            pe.wait_ge(S("v_main_ready"), B)
            pe.wait_ge(S("v_tail_ready"), B)

            def scores(blk, i, g):
                n = 4 * blk + i
                for j in range(2):
                    m = 2 * (NG * n + g) + j
                    if i == 0 and 2 * g + j < 4:
                        pe.wait_ge(S("shifted"), 2 * NG * 4 * blk)
                    else:
                        pe.wait_ge(S("shifted"), m - 3)
                    if j == 0:
                        pe.wait_ge(S("qT_ready"), NG * blk + g + 1)
                    pe.matmul(bank[(2 * g + j) % 4][:, 0:2 * LK], qT[:, g, i * P:(i + 1) * P],
                              keys_of[:, :, 2 * j * LK:(2 * j + 2) * LK][:, ds((blk_b(blk)) * NG + g, 1), :].rearrange("p a n -> p (a n)"),
                              start=True, stop=True).then_inc(S("score_x_mm"), 1)

            def turn_probs(blk, i, g):
                n = 4 * blk + i
                pe.wait_ge(S("prob_ready"), NG * n + (g + 1 if g < NG else NG))
                if i == 0 and g < 2:
                    pe.wait_ge(S("probT_ready"), (NG + 1) * 4 * blk)
                else:
                    pe.wait_ge(S("probT_ready"), (NG + 1) * n + g - 1)
                for h in range(GH):
                    if g < NG:
                        m = pe.transpose(bank[4 + g % 2][0:KM, h * P:(h + 1) * P], prob_m[i % 2][:, GH * g + h, :], ident[:, :])
                    else:
                        m = pe.transpose(bank[4 + g % 2][:, h * P:(h + 1) * P], 
                                         prob_t[i % 2][:, GH * h:GH * (h + 1), :].rearrange("p h n -> p (h n)"), ident[:, :])
                m.then_inc(S("prob_turned"), 1)

            def weigh_values(blk, i):
                n = 4 * blk + i
                pe.wait_ge(S("probT_ready"), (NG + 1) * (n + 1))
                pe.wait_ge(S("head_o_ready"), n)
                W = HD + 1
                for g in range(NG):
                    pe.matmul(bank[7][:, g * GH * W:(g + 1) * GH * W], probT[:, XH + g, :],
                              vt_of[:, ds(blk_b(blk) * NG + g, 1), :].rearrange("p a n -> p (a n)"), start=True, stop=False, skip_group_check=True)
                    for h in range(GH):
                        hh = GH * g + h
                        m = pe.matmul(bank[7][:, hh * W:(hh + 1) * W], probT[0:KM, hh, :],
                                      vm_of[0:KM, ds(blk_b(blk) * XH + hh, 1), :].rearrange("p a n -> p (a n)"), start=False, stop=(h == GH - 1),
                                      skip_group_check=True)
                m.then_inc(S("pv_mm"), 1)

            keys_of = keys.rearrange("p b g n -> p (b g) n")
            vt_of = v_tail.rearrange("p b g n -> p (b g) n")
            vm_of = v_main.rearrange("p b h n -> p (b h) n")
            batch_of = [0]

            def blk_b(blk):
                return batch_of[0]

            with pe.Fori(0, B) as b:
                batch_of[0] = b
                with pe.Fori(0, NBLK // B) as jj:
                    blk = b * (NBLK // B) + jj
                    for g in range(NG):
                        if g < 2:
                            pe.wait_ge(S("head_o_ready"), 4 * blk)
                        else:
                            pe.wait_ge(S("qT_ready"), NG * blk + g - 1)
                        for k in range(KD):
                            m = pe.matmul(bank[7 - g % 2][:, :], wq_pad[:, k, g * P:(g + 1) * P], featT[:, k, ds(blk * BLK, BLK)],
                                          start=(k == 0), stop=(k == KD - 1))
                        m.then_inc(S("q_mm"), 1)
                    for i in range(5):
                        for g in range(NG):
                            if i < 4:
                                scores(blk, i, g)
                            if i > 0:
                                turn_probs(blk, i - 1, g)
                        if i > 0:
                            turn_probs(blk, i - 1, NG)
                            if i == 1:
                                pe.wait_ge(S("qT_ready"), NG * (blk + 1))
                            weigh_values(blk, i - 1)

            pe.wait_ge(S("head_o_ready"), NT)
            pe.wait_ge(S("route_w_loaded"), 16 * 3)
            with pe.Fori(0, NT // 2) as i:
                for p in range(2):
                    t = 2 * i + p
                    pe.wait_ge(S("x3_ready"), t + 1)
                    if p == 0:
                        pe.wait_ge(S("x3T_ready"), 2 * i)
                    for k in range(KD):
                        m = pe.transpose(bank[p][:, k * P:(k + 1) * P], ln_st[:, p, k * P:(k + 1) * P], ident[:, :])
                    m.then_inc(S("x3_turned"), 1)
                for p in range(2):
                    t = 2 * i + p
                    pe.wait_ge(S("x3T_ready"), t + 1)
                    if p == 0:
                        pe.wait_ge(S("logits_ready"), 2 * i)
                    for k in range(KD):
                        m = pe.matmul(bank[2 + p][:, 0:NE], x3T[:, p, k, :], w_route[:, k, :], start=(k == 0), stop=(k == KD - 1))
                    m.then_inc(S("route_mm"), 1)
            pe.wait_ge(S("hot_ready"), 1)
            hot_flat = hot.rearrange("p t e -> p (t e)")
            pe.matmul(bank[4][:, 0:NT * NE], tri_le[:, :], hot_flat, start=True, stop=True).then_inc(S("count_mm"), 1)
            pe.matmul(bank[5][:, 0:NT * NE], ones[:, :], hot_flat, start=True, stop=True).then_inc(S("count_mm"), 1)
            pe.wait_ge(dve_once, at("block_expert_ready"))

            def turn_rows(n, p):
                pe.wait_ge(S(f"xs_loaded{p}"), 8 * (n - p) + 16)
                pe.wait_ge(S("xsT_ready"), n)
                for k in range(KD):
                    m = pe.transpose(bank[6][:, k * P:(k + 1) * P], xs[:, p, k * P:(k + 1) * P], ident[:, :])
                m.then_inc(S("xs_turned"), 1)

            def up(n, p):
                e = pe.value_load(expert_i[0:1, ds(n, 1)], min_val=0, max_val=NE - 1)
                pe.wait_ge(S("xsT_ready"), n + 1)
                pe.wait_ge(S("h_kept"), 2 * n)
                for f in range(2):
                    for k in range(KD):
                        m = pe.matmul(bank[f][:, :], xsT[:, p, k, :], w1_of[:, ds(e * KD + k, 1), f * 512:(f + 1) * 512].rearrange("p a n -> p (a n)"),
                                      start=(k == 0), stop=(k == KD - 1))
                    m.then_inc(S("up_mm"), 1)

            def down(n):
                e = pe.value_load(expert_i[0:1, ds(n, 1)], min_val=0, max_val=NE - 1)
                for half in range(2):
                    pe.wait_ge(S("h_kept"), 2 * n + half + 1)
                    pe.wait_ge(S("hT_half_a" if half == 0 else "hT_half_b"), n)
                    for f in range(4):
                        m = pe.transpose(bank[2 + half][:, f * P:(f + 1) * P], hid_e[:, (4 * half + f) * P:(4 * half + f + 1) * P], ident[:, :])
                    m.then_inc(S("h_turned"), 1)
                pe.wait_ge(S("yo_ready"), n)
                for f in range(NFF):
                    if f % 4 == 0:
                        pe.wait_ge(S("hT_half_a" if f == 0 else "hT_half_b"), n + 1)
                    m = pe.matmul(bank[4][:, 0:D], hidT[:, f, :], w2_of[:, ds(e * NFF + f, 1), :].rearrange("p a n -> p (a n)"),
                                  start=(f == 0), stop=(f == NFF - 1))
                m.then_inc(S("down_mm"), 1)

            w1_of = w1.rearrange("p e k f -> p (e k) f")
            w2_of = w2.rearrange("p e f d -> p (e f) d")
            pe.wait_ge(S("w1_loaded"), 16 * NE)
            turn_rows(0, 0)
            up(0, 0)
            pe.wait_ge(S("w2_loaded"), 16 * 2 * NE)
            with pe.Fori(0, NB // 2) as i:
                turn_rows(2 * i + 1, 1)
                up(2 * i + 1, 1)
                down(2 * i)
                turn_rows(2 * i + 2, 0)
                up(2 * i + 2, 0)
                down(2 * i + 1)
            down(NB - 1)


def layouts(inputs):
    g = {k: np.asarray(v) for k, v in inputs.items()}

    def c(v, *axes):
        return np.ascontiguousarray(v.transpose(*axes) if axes else v)

    def cols(v, *shape):
        return c(v.reshape(-1, P, *shape), 1, 0, *range(2, 2 + len(shape)))
    return {
        "x": c(g["x"]), "ctxT": c(g["ctx_1024"], 0, 2, 1), "mask": c(g["mask_BxS2_ik0"]),
        "attn_norm_w": cols(g["L0_attn_norm_w"]), "attn_in_wT": c(g["L0_attn_in_w"], 1, 0),
        "attn_conv_w": cols(g["L0_attn_conv_w"], TAPS), "attn_conv_b": cols(g["L0_attn_conv_b"]),
        "attn_dt_bias": c(g["L0_attn_dt_bias"]), "attn_A_log": c(g["L0_attn_A_log"]),
        "attn_D_param": c(g["L0_attn_D_param"]), "attn_gnorm_w": cols(g["L0_attn_gnorm_w"]),
        "attn_out_wT": c(g["L0_attn_out_w"], 1, 0), "scorer_w1T": c(g["L0_attn_scorer_w1"], 1, 0),
        "scorer_w2T": c(g["L0_attn_scorer_w2"], 1, 0), "summ_wT": c(g["L0_attn_summ_w"], 1, 0),
        "mem_q_wT": c(g["L0_attn_q_w"], 1, 0), "mem_k_wT": c(g["L0_attn_k_w"], 1, 0),
        "mem_v_wT": c(g["L0_attn_v_w"], 1, 0), "gate_wT": c(g["L0_attn_gate_w"], 1, 0),
        "q_w": c(g["L0_xattn_q_w"], 1, 0), "q_b": c(g["L0_xattn_q_b"]), "k_w": c(g["L0_xattn_k_w"], 1, 0),
        "k_b": c(g["L0_xattn_k_b"]), "v_w": c(g["L0_xattn_v_w"], 1, 0), "v_b": c(g["L0_xattn_v_b"]),
        "WrT": c(g["L0_ffn_Wr"], 1, 0), "br": c(g["L0_ffn_br"]),
        "W1T": c(g["L0_ffn_W1"], 0, 2, 1), "b1": c(g["L0_ffn_b1"].reshape(NE * NFF, P), 1, 0),
        "W2T": c(g["L0_ffn_W2"], 0, 2, 1), "b2": c(g["L0_ffn_b2"]),
    }


def kernel(**inputs):
    import concourse.bacc as bacc
    from concourse.bass_utils import run_bass_kernel_spmd

    nc = bacc.Bacc("TRN2", target_bir_lowering=False, num_devices=1)
    arrays = layouts(inputs)
    dram = {n: nc.dram_tensor(n, v.shape, mybir.dt.from_np(v.dtype), kind="ExternalInput").ap() for n, v in arrays.items()}
    out = nc.dram_tensor("out", (B, T, D), F32, kind="ExternalOutput").ap()
    build(nc, dram, out)
    return run_bass_kernel_spmd(nc, [arrays], core_ids=[0]).results[0]["out"]
```

```python
from contextlib import ExitStack

import numpy as np

import concourse.bass as bass
from concourse import mybir

F32 = mybir.dt.float32
I32 = mybir.dt.int32
BF16 = mybir.dt.bfloat16
ALU = mybir.AluOpType
ACT = mybir.ActivationFunctionType
AX = mybir.AxisListType.X
ds = bass.ds

P = 128
EPS = 1e-5
NEG = -1e30

B, T, D = 2, 1024, 256
NT = B * T // P
TB = T // P
KD = D // P
DI, NS, H, HP = 512, 128, 8, 64
TAPS = 4
NZ, NX = DI // P, (DI + 2 * NS) // P
BLK = 512
NBLK = B * T // BLK
POOL, SD = 50, 64
LK, XH, HD = 154, 16, 16
KT = 32
KM = LK - KT
GH, NG = 4, 4
NE, FF = 8, 1024
NFF = FF // P
NB = NT + NE - 1
ROW = 2 * D + 1

DVE_EVENTS = (
    "eps_set", "ln_var", "rstd_1", "rstd_2", "rms_var", "rstd_3", "rstd_4", "dt_steps_1", 
    "dt_steps_2", "dt_abs", "dt_sum", "dt_ready", "tot_kept", "wend_diff", "first_cleared_1", 
    "first_cleared_2", "decay_ready", "gn_rstd", "w2b_ready", "pos_ready", "cols_set", "valid_ready", 
    "rank_sum_1", "rank_sum_2", "rank_sum_3", "mean_ready_1", "mean_ready_2", "ln2_var", "ln2_rstd", 
    "mask_row_ready", "bias_cols_ready", "ln3_var", "ln3_rstd", "iotas_ready", "block_expert_ready",
)
ACT_EVENTS = (
    "ln_sd", "rms_sd", "dt_e", "a_exp", "dt_ln", "ecum_exp", "dec_exp", "wend_exp", "gn_sd", "ln2_sd", 
    "ln3_sd",
)
POOL_EVENTS = (
    "ones_set", "mask_init", "masks_set_1", "masks_set_2", "masks_set_3", "state_set", "pos_set", 
    "bias_rows_zero_1", "bias_rows_cleared_1", "bias_rows_zero_2", "bias_rows_cleared_2", 
    "pads_zero_1", "pads_zero_2", "pads_zero_3", "pads_zero_4", "pads_zero_5", "empty_ready_1", 
    "empty_ready_2", "counters_set",
)


def events_of(name):
    return next(events for events in (DVE_EVENTS, ACT_EVENTS, POOL_EVENTS) if name in events)


def at(name):
    return events_of(name).index(name) + 1


def build(nc, a, out):
    x_flat = a["x"].rearrange("b t d -> (b t) d")
    out_flat = out.rearrange("b t d -> (b t) d")

    with ExitStack() as ctx:
        def sb(name, shape, dt=F32):
            return ctx.enter_context(nc.sbuf_tensor(name, shape, dt))

        names = {}

        def sem(name):
            if name not in names:
                names[name] = ctx.enter_context(nc.semaphore(name))
            return names[name]

        dve_once, act_once, pool_once = sem("dve_once"), sem("act_once"), sem("pool_once")
        met = []

        def reached(name):
            met.append(name)
            events = events_of(name)
            assert [m for m in met if m in events] == list(events[:at(name)])
            return 1

        pair = [ctx.enter_context(nc.psum_tensor(f"pair{i}", [P, 2, 512], F32)) for i in range(2)]
        bank = [pair[i // 2][:, i % 2, :] for i in range(4)]
        bank += [ctx.enter_context(nc.psum_tensor(f"bank{i}", [P, 512], F32)) for i in range(4, 8)]

        GT = 4
        xres = sb("xres", [P, NT, D])
        featT = sb("featT", [P, KD, B * T])
        ybuf = sb("ybuf", [P, NT * D])
        arena = sb("arena", [P, 2 * NE * KD * FF])
        y_tok = ybuf[:, :].rearrange("p (t d) -> p t d", t=NT)
        IN_W = 2 * DI + 2 * NS + H
        w_in = ybuf[:, 0:KD * IN_W].rearrange("p (k n) -> p k n", k=KD)

        place = [0]

        def cut(shape):
            n = int(np.prod(shape))
            v = arena[:, place[0]:place[0] + n]
            place[0] += n
            if len(shape) == 2:
                v = v.rearrange("p (a b) -> p a b", a=shape[0])
            if len(shape) == 3:
                v = v.rearrange("p (a b c) -> p a b c", a=shape[0], b=shape[1])
            return v

        NXP = 4
        xbcT = cut([NX, B * T])
        zsT = cut([NZ, B * T])
        work0 = place[0]
        raw = cut([NX, TAPS - 1 + BLK])
        conv = cut([NX, BLK])
        tanh_c = cut([NX, BLK])
        tanh_z = cut([2, BLK])
        place[0] = work0
        xn = cut([GT, D])
        place[0] = work0
        xbc = cut([2, NX, P])
        seg = cut([2, H, P])
        lmat = cut([2, H, P])
        gmat = cut([2, P])
        b_tok = cut([2, P])
        xdt = cut([2, DI])
        xend = cut([2, DI])
        xskip = cut([2, DI])
        state = cut([DI])
        y_in = cut([2, DI])
        gated = cut([2, NZ, P])
        sq = featT[:, 0, 0:2 * NZ * P].rearrange("p (a b c) -> p a b c", a=2, b=NZ)
        assert place[0] <= 2 * NE * KD * FF

        ident = sb("ident", [P, P])
        ones = sb("ones", [P, P])
        tri_le = sb("tri_le", [P, P])
        tri_gt = sb("tri_gt", [P, P])
        w_out = sb("w_out", [P, NZ, D])
        norm_w = sb("norm_w", [P, KD])
        gnorm_w = sb("gnorm_w", [P, NZ])
        conv_w = sb("conv_w", [P, NX, TAPS])
        conv_b = sb("conv_b", [P, NX])
        dt_bias = sb("dt_bias", [P, H])
        a_log = sb("a_log", [P, H])
        d_skip = sb("d_skip", [P, H])
        stats = sb("stats", [P, NT, 6])
        mv = sb("mv", [P, NT, 2])
        nrm = sb("nrm", [P, 6, NT])
        dts = sb("dts", [P, 8, NT * H])
        ssq = sb("ssq", [P, 4, NT])
        eps_col = sb("eps_col", [P, 1])
        dt_raw, dt_neg, dt_pos, dt_exp = (dts[:, i, :] for i in range(4))
        dt_v, dta, ecum, dec = (dts[:, i, :] for i in range(4, 8))
        wend = dt_raw
        tot = dt_neg

        def th(v):
            return v.rearrange("p (t h) -> p t h", h=H)

        def heads(v, n):
            return v.unsqueeze(2).broadcast_to([P, H, n])

        w1 = arena[:, 0:NE * KD * FF].rearrange("p (e k f) -> p e k f", e=NE, k=KD)
        UP = NE * KD * FF
        place[0] = UP
        wq_dense = cut([KD, D])
        wk_dense = cut([KD, D])
        wv = cut([KD, D])
        ctxT = cut([B, KD, LK])
        after_loads = place[0]
        sig = cut([B * T])
        y_st = cut([2, D])
        hid = cut([2, BLK])
        junk = cut([T])
        greater = junk.bitcast(BF16).rearrange("p (a n) -> p a n", a=2)
        junk_eq = cut([2, P])
        ones_bf = cut([1]).bitcast(BF16)
        onehot = cut([NT, POOL])
        pool_tok = cut([B, D])
        pool_tokT = cut([B, KD, POOL])
        poolT = cut([B, POOL])
        keyT = cut([B, POOL])
        val = cut([B, D])
        val_now = cut([D])
        q_mem = cut([BLK])
        logit = cut([4, POOL])
        attnT = cut([BLK])
        retT = cut([KD, BLK])
        gate_t = cut([KD, BLK])
        upd = cut([KD, BLK])
        assert place[0] <= 2 * NE * KD * FF
        scorer_w1 = sb("scorer_w1", [P, KD, SD])
        scorer_w2 = sb("scorer_w2", [SD, 1])
        scorer_w2b = sb("scorer_w2b", [SD, P])
        summ_w = sb("summ_w", [P, KD, SD])
        mem_q_w = sb("mem_q_w", [P, KD, SD])
        mem_k_w = sb("mem_k_w", [SD, SD])
        mem_v_w = sb("mem_v_w", [SD, D])
        gate_w = sb("gate_w", [P, 2 * KD, D])
        mem_bank = [(bank[4], bank[5], bank[6]), (bank[1], bank[2], bank[7])]
        pos_i = sb("pos_i", [P, POOL], I32)
        pos = sb("pos", [P, POOL])
        tile_i = sb("tile_i", [P, NT], I32)
        cols = sb("cols", [P, 6, NT])
        s_col, n_earlier, n_gt, n_eq, rank, valid = (cols[:, i, :] for i in range(6))
        mean_s = sb("mean_s", [P, B])
        vbias = sb("vbias", [P, B, POOL])
        red = sb("red", [P, 3, 4])

        place[0] = after_loads
        wq_pad = cut([KD, NG * P])
        wk_pad = cut([KD, NG * P])
        tail_ctx = cut([B, KD, P])
        keys = cut([B, NG, GH * LK])
        v_main = cut([B, XH, HD + 1])
        v_tail = cut([B, NG, GH * (HD + 1)])
        qT = cut([2, NG, P])
        assert place[0] + XH * LK <= 2 * NE * KD * FF
        prob_a = cut([XH * LK])
        prob_b = sb("prob_b", [P, XH * LK])
        prob = (prob_a, prob_b[:, :])
        prob_m = [v[:, 0:XH * KM].rearrange("p (h n) -> p h n", h=XH) for v in prob]
        prob_t = [v[:, XH * KM:].rearrange("p (h n) -> p h n", h=XH) for v in prob]
        probT = ybuf[:, 0:(XH + NG) * P].rearrange("p (h n) -> p h n", h=XH + NG)
        ln_st = ybuf[:, (XH + NG) * P:(XH + NG) * P + 2 * D].rearrange("p (a d) -> p a d", a=2)
        st4 = ybuf[:, (XH + NG) * P:(XH + NG) * P + 4 * D].rearrange("p (a d) -> p a d", a=4)
        head_o = ybuf[:, (XH + NG) * P + 2 * D:(XH + NG) * P + 4 * D].rearrange("p (a d) -> p a d", a=2)
        bias_rows = sb("bias_rows", [NG, 2, GH, 32])
        bias_cols = sb("bias_cols", [P, 2, NG])
        rows1 = w_out[0:1, :, :].rearrange("p k n -> p (k n)")
        mask_i = rows1[:, 0:B * LK].bitcast(I32)
        mask_row = rows1[:, B * LK:2 * B * LK]
        vb_row = rows1[:, 2 * B * LK:2 * B * LK + D]
        mask_sel = rows1[:, 2 * B * LK + D:2 * B * LK + D + P]
        xmax = sb("xmax", [P, 2, XH])
        xinv = sb("xinv", [P, 2, XH])
        TURN_BANK = (4, 4, 5, 4, 5)

        w2 = arena[:, NE * KD * FF:].rearrange("p (e f d) -> p e f d", e=NE, f=NFF)
        sorted_rows = nc.dram_tensor("sorted_rows", [NB * P, ROW], F32, kind="Internal").ap()
        NOWHERE = 2 * B * T

        def parts(v, *shapes):
            at_, out_ = 0, []
            for shape in shapes:
                n = int(np.prod(shape))
                w = v[:, at_:at_ + n]
                if len(shape) == 2:
                    w = w.rearrange("p (a b) -> p a b", a=shape[0])
                if len(shape) == 3:
                    w = w.rearrange("p (a b c) -> p a b c", a=shape[0], b=shape[1])
                out_.append(w)
                at_ += n
            return out_
        g_flat = gate_w[:, :, :].rearrange("p k n -> p (k n)")
        b1_cols, w_route, br_row, empty = parts(g_flat, [NE * NFF], [KD, NE], [NE], [ROW])
        ints = g_flat[:, 640:].bitcast(I32)
        token_i, slot_i, slot_now, expert_i, desc_i, thr_i, blk_i = parts(ints, [NT], [NT], [GT], [NB], [NE], [NT], [NB])
        logits, hot, slot_t, before, blocks_c, expert_c, desc, thr, blk_n, first_blk, best, slot_f, expert_f = parts(
            w_out[:, :, :].rearrange("p k n -> p (k n)"), [NT, NE], [NT, NE], [NT, NE], [NT + 1, NE], [NE, NT], [NB, NE],
            [NE], [NT], [NB], [NE + 1], [NT], [NT], [NB])
        (rows,) = parts(ybuf[:, :], [GT, ROW])
        (xsT,) = parts(ybuf[:, (XH + NG) * P + 4 * D:], [2, KD, P])
        x3T = [ybuf[:, i * GT * D:(i + 1) * GT * D].rearrange("p (t k n) -> p t k n", t=GT, k=KD) for i in range(2)]
        hid_e, hidT = parts(prob_b[:, :], [FF], [NFF, P])
        b2_rows, xs, rest, yo = parts(featT[:, :, :].rearrange("p k n -> p (k n)"), [NE, D], [2, D], [2, D + 1], [2, D])

        block = ctx.enter_context(nc.Block())
        S = sem
        N_SMALL = 8

        @block.sync
        def _(sp):
            for q in range(4):
                sp.dma_start(xres[:, 4 * q:4 * q + 4, :],
                             x_flat[q * BLK:(q + 1) * BLK, :].rearrange("(t p) d -> p t d", p=P)
                             ).then_inc(S(f"x_loaded{q}"), 16)
            sp.dma_start(w_in, a["attn_in_wT"].rearrange("(k p) n -> p k n", p=P)).then_inc(S("w_loaded"), 16)
            sp.dma_start(w_out[:, :, :], a["attn_out_wT"].rearrange("(k p) n -> p k n", p=P)
                         ).then_inc(S("w_loaded"), 16)

            sp.wait_ge(S("conv_done"), NXP * NBLK)
            sp.wait_ge(S("conv_done_dve"), (NX - NXP) * NBLK)

            def load_chunk(t, p, wait):
                first, used = (sp.snap(t * P), sp.snap(t - 1)) if wait else (t * P, 0)
                if wait:
                    sp.wait_ge(S("state_mm"), used)
                sp.dma_start(xbc[:, p, :, :], xbcT[:, :, ds(first, P)]).then_inc(S(f"chunk_loaded{p}"), 16)
            load_chunk(0, 0, False)
            load_chunk(1, 1, False)
            with sp.Fori(1, NT // 2) as i:
                for p in range(2):
                    load_chunk(2 * i + p, p, True)

            for dst, src in ((scorer_w1[:, :, :], a["scorer_w1T"].rearrange("(k p) n -> p k n", p=P)),
                             (scorer_w2[:, :], a["scorer_w2T"]),
                             (summ_w[:, :, :], a["summ_wT"].rearrange("(k p) n -> p k n", p=P)),
                             (mem_q_w[:, :, :], a["mem_q_wT"].rearrange("(k p) n -> p k n", p=P)),
                             (mem_k_w[:, :], a["mem_k_wT"]),
                             (mem_v_w[:, :], a["mem_v_wT"]),
                             (gate_w[:, :, :], a["gate_wT"].rearrange("(k p) n -> p k n", p=P))):
                sp.dma_start(dst, src).then_inc(S("mem_w_loaded"), 16)
            sp.wait_ge(S("out_kept"), NT)
            sp.wait_ge(S("y_part"), 2 * NT)
            sp.wait_ge(S("state_added"), NT)

            for dst, src in ((wq_dense, a["q_w"].rearrange("(k p) n -> p k n", p=P)),
                             (wk_dense, a["k_w"].rearrange("(k p) n -> p k n", p=P)),
                             (wv, a["v_w"].rearrange("(k p) n -> p k n", p=P)),
                             (mask_i[:, :], a["mask"].rearrange("b k -> (b k)").unsqueeze(0)),
                             (vb_row[:, :], a["v_b"].unsqueeze(0))):
                sp.dma_start(dst, src).then_inc(S("x_w_loaded"), 16)
            for b in range(B):
                sp.dma_start(ctxT[:, b, :, :], a["ctxT"][b].rearrange("(k p) n -> p k n", p=P)).then_inc(S("x_w_loaded"), 16)
            sp.wait_ge(pool_once, at("bias_rows_cleared_2"))
            for n, name in enumerate(("q_b", "k_b")):
                sp.dma_start(bias_rows[:, n, :, 0:HD], a[name].rearrange("(g h d) -> g h d", g=NG, h=GH)).then_inc(S("x_w_loaded"), 16)
            for e in range(NE):
                sp.dma_start(w1[:, e, :, :], a["W1T"][e].rearrange("(k p) f -> p k f", p=P)).then_inc(S("w1_loaded"), 16)

            sp.wait_ge(S("gate_tanh"), 2 * NBLK)
            for dst, src in ((b1_cols, a["b1"]), (w_route, a["WrT"].rearrange("(k p) n -> p k n", p=P)),
                             (br_row, a["br"].partition_broadcast(P))):
                sp.dma_start(dst, src).then_inc(S("route_w_loaded"), 16)
            sp.wait_ge(pool_once, at("empty_ready_2"))
            sp.dma_start(sorted_rows.rearrange("(n p) r -> p n r", p=P), empty.unsqueeze(1).broadcast_to([P, NB, ROW])
                         ).then_inc(S("rows_emptied"), 16)
            sp.wait_ge(S("x2_ready"), NT)
            sp.wait_ge(S("prob_turned"), (NG + 1) * NT)
            for e in range(NE):
                sp.dma_start(w2[:, e, :, :], a["W2T"][e].rearrange("(f p) d -> p f d", p=P)).then_inc(S("w2_loaded"), 16)
            for e in range(NE):
                sp.dma_start(b2_rows[:, e, :], a["b2"][e].partition_broadcast(P)).then_inc(S("w2_loaded"), 16)
            for p in range(GT):
                sp.wait_ge(S(f"scattered{p}"), 16 * NT // GT)

            def load_xs(n, p, wait):
                first, used = (sp.snap(n * P), sp.snap(n - 1)) if wait else (n * P, 0)
                if wait:
                    sp.wait_ge(S("xs_turned"), used)
                sp.dma_start(xs[:, p, :], sorted_rows[ds(first, P), 0:D]).then_inc(S(f"xs_loaded{p}"), 16)

            def load_rest(n, p, wait):
                first, stored = (sp.snap(n * P), sp.snap(8 * (n - p))) if wait else (n * P, 0)
                if wait:
                    sp.wait_ge(S(f"out_stored{p}"), stored)
                sp.dma_start(rest[:, p, :], sorted_rows[ds(first, P), D:ROW]).then_inc(S(f"rest_loaded{p}"), 16)
            for n in range(2):
                load_xs(n, n, False)
                load_rest(n, n, False)
            sp.wait_ge(S("xs_turned"), 1)
            load_xs(2, 0, False)
            with sp.Fori(1, NB // 2) as i:
                for p in (1, 0):
                    n = 2 * i + 2 - p
                    load_xs(n, p, True)
                    load_rest(n - 1, 1 - p, True)
            load_rest(NB - 1, 0, True)

        @block.gpsimd
        def _(pool):
            pool.memset(ones[:, :], 1.0).then_inc(pool_once, reached("ones_set"))
            pool.memset(ident[:, :], 0.0).then_inc(pool_once, reached("mask_init"))
            pool.wait_ge(pool_once, at("ones_set"))
            pool.wait_ge(pool_once, at("mask_init"))
            pool.affine_select(out=ident[:, :], in_=ident[:, :], compare_op=ALU.not_equal, fill=1.0, base=0,
                               pattern=[[-1, P]], channel_multiplier=1).then_inc(pool_once, reached("masks_set_1"))
            pool.affine_select(out=tri_le[:, :], in_=ones[:, :], compare_op=ALU.is_ge, fill=0.0, base=0,
                               pattern=[[1, P]], channel_multiplier=-1).then_inc(pool_once, reached("masks_set_2"))
            pool.affine_select(out=tri_gt[:, :], in_=ones[:, :], compare_op=ALU.is_gt, fill=0.0, base=0,
                               pattern=[[-1, P]], channel_multiplier=1).then_inc(pool_once, reached("masks_set_3"))
            pool.wait_ge(S("res_cols"), 2)
            for t in range(NT):
                pool.wait_ge(S("xn_ready"), t + 1)
                pool.tensor_scalar(xres[:, t, :], xres[:, t, :], nrm[:, 1, t:t + 1], nrm[:, 2, t:t + 1], ALU.mult, ALU.subtract
                                   ).then_inc(S("res_added"), 1)
            with pool.Fori(0, NBLK) as blk:
                for f in range(NXP):
                    pool.wait_ge(S("tanh_c_ready"), NX * blk + f + 1)
                    pool.tensor_tensor(tanh_c[:, f, :], tanh_c[:, f, :], conv[:, f, :], ALU.mult).then_inc(S("silu_part"), 1)
                    pool.wait_ge(S("silu_part"), NXP * blk + f + 1)
                    pool.tensor_tensor(xbcT[:, f, ds(blk * BLK, BLK)], tanh_c[:, f, :], conv[:, f, :], ALU.add
                                       ).then_inc(S("conv_done"), 1)
            pool.wait_ge(dve_once, at("dt_ready"))
            pool.wait_ge(dve_once, at("decay_ready"))
            pool.wait_ge(S("conv_done"), NXP * NBLK)
            pool.wait_ge(S("conv_done_dve"), (NX - NXP) * NBLK)
            pool.memset(state, 0.0).then_inc(pool_once, reached("state_set"))

            def make_seg(t, p, wait):
                if wait:
                    pool.wait_ge(S("seg_mm"), t - 1)
                pool.tensor_tensor(seg[:, p, :, :], tri_le[:, :].unsqueeze(1).broadcast_to([P, H, P]),
                                   heads(dta[:, ds(t * H, H)], P), ALU.mult).then_inc(S("seg_ready"), 1)

            def make_m(t, p):
                pool.wait_ge(S("decay_mat"), t + 1)
                pool.wait_ge(S("g_ready"), t + 1)
                pool.tensor_tensor(lmat[:, p, :, :], lmat[:, p, :, :],
                                   gmat[:, p, :].unsqueeze(1).broadcast_to([P, H, P]), ALU.mult
                                   ).then_inc(S("m_ready"), 1)

            def decay_state(t):
                pool.wait_ge(S("inter_mm"), t + 1)
                pool.wait_ge(S("state_added"), t)
                sv = state.rearrange("p (h n) -> p h n", h=H)
                pool.tensor_tensor(sv, sv, heads(dec[:, ds(t * H, H)], HP), ALU.mult).then_inc(S("state_decayed"), 1)

            pool.wait_ge(pool_once, at("state_set"))
            make_seg(0, 0, False)
            make_seg(1, 1, False)
            make_m(0, 0)

            def step(t, p):
                make_seg(t + 2, p, True)
                make_m(t + 1, 1 - p)
                decay_state(t)
            with pool.Fori(0, NT // 2 - 1) as i:
                step(2 * i, 0)
                step(2 * i + 1, 1)
            make_m(NT - 1, 1)
            decay_state(NT - 2)
            decay_state(NT - 1)

            pool.iota(tile_i[:, :], pattern=[[0, B], [P, TB]], base=0, channel_multiplier=0)
            pool.iota(pos_i[:, :], pattern=[[1, POOL]], base=0, channel_multiplier=0).then_inc(pool_once, reached("pos_set"))
            with pool.Fori(0, NT // 2) as i:
                for p in range(2):
                    t = 2 * i + p
                    pool.wait_ge(S("y_st_ready"), t + 1)
                    pool.tensor_tensor(xres[:, ds(t, 1), :].rearrange("p a d -> p (a d)"),
                                       xres[:, ds(t, 1), :].rearrange("p a d -> p (a d)"), y_st[:, p, :], ALU.add
                                       ).then_inc(S("res_y_added"), 1)

            pool.memset(bias_rows[:, :, :, :], 0.0).then_inc(pool_once, reached("bias_rows_zero_1"))
            pool.wait_ge(pool_once, at("bias_rows_zero_1"))
            pool.memset(bias_rows[:, 0, :, HD:HD + 1], 1.0).then_inc(pool_once, reached("bias_rows_cleared_1"))
            pool.memset(mask_sel[:, :], 0.0).then_inc(pool_once, reached("bias_rows_zero_2"))
            pool.wait_ge(pool_once, at("bias_rows_zero_2"))
            pool.memset(mask_sel[:, :].rearrange("o (h c) -> o h c", c=32)[:, :, HD:HD + 1], 1.0).then_inc(pool_once, reached("bias_rows_cleared_2"))
            pool.wait_ge(S("x1_ready"), 2 * NBLK)
            pool.wait_ge(S("gate_tanh"), 2 * NBLK)
            pool.memset(wq_pad, 0.0).then_inc(pool_once, reached("pads_zero_1"))
            pool.memset(wk_pad, 0.0).then_inc(pool_once, reached("pads_zero_2"))
            pool.memset(keys, 0.0).then_inc(pool_once, reached("pads_zero_3"))
            pool.memset(v_tail, 0.0).then_inc(pool_once, reached("pads_zero_4"))
            pool.memset(v_main, 1.0).then_inc(pool_once, reached("pads_zero_5"))
            pool.wait_ge(S("x_w_loaded"), 16 * 9)
            pool.wait_ge(pool_once, at("pads_zero_5"))
            for pad, dense in ((wk_pad, wk_dense), (wq_pad, wq_dense)):
                pool.tensor_copy(pad.rearrange("p k (h c) -> p (k h) c", c=32)[:, :, 0:HD],
                                 dense.rearrange("p k (h d) -> p (k h) d", d=HD)).then_inc(S("pads_ready"), 1)
            for b in range(B):
                pool.tensor_copy(tail_ctx[:, b, :, :].rearrange("p k (r c) -> p k r c", c=KT),
                                 ctxT[:, b, :, KM:LK].unsqueeze(2).broadcast_to([P, KD, GH, KT])).then_inc(S("pads_ready"), 1)
            pool.wait_ge(S("x_w_loaded"), 16 * 9)
            pool.memset(empty, 0.0).then_inc(pool_once, reached("empty_ready_1"))
            pool.wait_ge(pool_once, at("empty_ready_1"))
            pool.memset(empty[:, ROW - 1:ROW].bitcast(I32), NOWHERE).then_inc(pool_once, reached("empty_ready_2"))
            pool.iota(token_i, pattern=[[P, NT]], base=0, channel_multiplier=1)
            pool.iota(desc_i, pattern=[[-1, NE]], base=NE, channel_multiplier=0)
            pool.iota(thr_i, pattern=[[P, NT]], base=0, channel_multiplier=0)
            pool.iota(blk_i, pattern=[[1, NB]], base=0, channel_multiplier=0).then_inc(pool_once, reached("counters_set"))
            with pool.Fori(0, NT // 2) as i:
                for p in range(2):
                    t = 2 * i + p
                    pool.wait_ge(S("head_o_ready"), t + 1)
                    pool.tensor_tensor(xres[:, ds(t, 1), :].rearrange("p a d -> p (a d)"),
                                       xres[:, ds(t, 1), :].rearrange("p a d -> p (a d)"), head_o[:, p, :], ALU.add
                                       ).then_inc(S("x2_ready"), 1)
            pool.wait_ge(S("rows_emptied"), 16)
            last_row, last_token = pool.to_reg(NB * P - 1), pool.to_reg(B * T - 1)
            with pool.Fori(0, NT // GT) as i:
                for p in range(GT):
                    pool.wait_ge(S("row_ready"), GT * i + p + 1)
                    pool.sem_inc(S("pool_turn"), 1)
                    pool.indirect_dma_start(out=sorted_rows, out_offset=bass.IndirectOffsetOnAxis(ap=slot_now[:, p:p + 1], axis=0),
                                            in_=rows[:, p, :], in_offset=None, bounds_check=last_row, oob_is_err=False
                                            ).then_inc(S(f"scattered{p}"), 16)

            def store(n, p):
                pool.wait_ge(S("yo_ready"), n + 1)
                pool.sem_inc(S("pool_turn"), 1)
                pool.indirect_dma_start(out=out_flat, out_offset=bass.IndirectOffsetOnAxis(ap=rest[:, p, D:D + 1].bitcast(I32), axis=0),
                                        in_=yo[:, p, :], in_offset=None, bounds_check=last_token, oob_is_err=False
                                        ).then_inc(S(f"out_stored{p}"), 16)
            with pool.Fori(0, NB // 2) as i:
                store(2 * i, 0)
                store(2 * i + 1, 1)
            store(NB - 1, 0)
            pool.wait_ge(S("out_stored0"), 16 * (NB // 2 + 1))
            pool.wait_ge(S("out_stored1"), 16 * (NB // 2))

        @block.scalar
        def _(act):
            for dst, src in ((norm_w[:, :], a["attn_norm_w"]),
                             (gnorm_w[:, :], a["attn_gnorm_w"]),
                             (conv_w[:, :, :], a["attn_conv_w"]),
                             (conv_b[:, :], a["attn_conv_b"]),
                             (dt_bias[:, :], a["attn_dt_bias"].partition_broadcast(P)),
                             (a_log[:, :], a["attn_A_log"].partition_broadcast(P)),
                             (d_skip[:, :], a["attn_D_param"].partition_broadcast(P))):
                act.dma_start(dst, src).then_inc(S("small_loaded"), 16)
            act.wait_ge(dve_once, at("eps_set"))
            act.wait_ge(dve_once, at("ln_var"))
            act.activation(nrm[:, 0, :], mv[:, :, 1], ACT.Sqrt, bias=eps_col[:, :]).then_inc(act_once, reached("ln_sd"))
            act.wait_ge(dve_once, at("rms_var"))
            act.activation(nrm[:, 2, :], nrm[:, 1, :], ACT.Sqrt, bias=eps_col[:, :]).then_inc(act_once, reached("rms_sd"))
            for n in range(NT // 2):
                act.wait_ge(S("xn_turned"), n + 1)
                act.activation(featT[:, :, 2 * n * P:(2 * n + 2) * P].rearrange("p k (t n) -> p t k n", t=2),
                               bank[n % 4][:, :].rearrange("p (t k n) -> p t k n", t=2, k=KD), ACT.Copy).then_inc(S("xnT_ready"), 1)
            act.wait_ge(dve_once, at("dt_abs"))
            act.activation(dt_exp, dt_neg, ACT.Exp).then_inc(act_once, reached("dt_e"))
            act.activation(a_log[:, :], a_log[:, :], ACT.Exp).then_inc(act_once, reached("a_exp"))
            act.wait_ge(act_once, at("dt_e"))
            act.activation(dt_exp, dt_exp, ACT.Ln, bias=1.0).then_inc(act_once, reached("dt_ln"))

            def tanh_conv(blk, f):
                act.wait_ge(S("conv_sum"), NX * blk + f + 1)
                act.activation(tanh_c[:, f, :], conv[:, f, :], ACT.Tanh).then_inc(S("tanh_c_ready"), 1)

            act.wait_ge(S("weights_ready"), 2 * KD + NZ + 2)
            with act.Fori(0, B) as b:
                with act.Fori(0, NBLK // B) as j:
                    blk = b * (NBLK // B) + j
                    for f in range(NZ):
                        act.wait_ge(S("proj_mm"), (NZ + NX) * blk + f + 1)
                        act.wait_ge(S("zs_ready"), NZ * blk + max(f - 1, 0))
                        act.activation(tanh_z[:, f % 2, :], bank[f % 5][:, :], ACT.Tanh).then_inc(S("tanh_z_ready"), 1)
                    for f in range(NX):
                        if f == 0:
                            act.wait_ge(S("raw_used"), NX * blk)
                            act.wait_ge(S("past_cleared"), b + 1)
                        act.wait_ge(S("proj_mm"), (NZ + NX) * blk + NZ + f + 1)
                        act.activation(raw[:, f, TAPS - 1:], bank[(NZ + f) % 5][:, :], ACT.Copy).then_inc(S("raw_ready"), 1)
                        if f == 0:
                            act.wait_ge(S("conv_done"), NXP * blk)
                            act.wait_ge(S("conv_done_dve"), (NX - NXP) * blk)
                        act.wait_ge(S("raw_ready"), NX * blk + f + 1)
                        act.activation(conv[:, f, :], raw[:, f, 0:BLK], ACT.Identity, bias=conv_b[:, f:f + 1],
                                       scale=conv_w[:, f, 0:1]).then_inc(S("tap0_ready"), 1)
                        if f >= 2:
                            tanh_conv(blk, f - 2)
                    tanh_conv(blk, NX - 2)
                    tanh_conv(blk, NX - 1)
            act.wait_ge(S("cum_mm"), 1)
            act.activation(ecum, bank[0][:, 0:NT * H], ACT.Exp).then_inc(act_once, reached("ecum_exp"))
            act.wait_ge(S("cum_mm"), 2)
            act.activation(dec, bank[1][:, 0:NT * H], ACT.Exp).then_inc(act_once, reached("dec_exp"))
            act.wait_ge(dve_once, at("wend_diff"))
            act.activation(wend, wend, ACT.Exp).then_inc(act_once, reached("wend_exp"))

            def decay_matrix(t, p, wait):
                act.wait_ge(S("seg_mm"), t + 1)
                if wait:
                    act.wait_ge(S("intra_mm"), t - 1)
                for q in range(2):
                    i = act.activation(lmat[:, p, 4 * q:4 * q + 4, :], bank[2 + q][:, :].rearrange("p (h n) -> p h n", h=4), ACT.Exp)
                i.then_inc(S("decay_mat"), 1)

            def square(t, p):
                act.wait_ge(S("gated_ready"), t + 1)
                act.activation(sq[:, p, :, :], gated[:, p, :, :], ACT.Square).then_inc(S("sq_ready"), 1)

            def keep_out(t):
                act.wait_ge(S("out_mm"), t + 1)
                act.activation(y_tok[:, ds(t, 1), :].rearrange("p a d -> p (a d)"), bank[7][:, 0:D], ACT.Copy)
                act.activation(ssq[:, 0, ds(t, 1)], bank[7][:, D:D + 1], ACT.Copy).then_inc(S("out_kept"), 1)

            act.wait_ge(S("conv_done"), NXP * NBLK)
            act.wait_ge(S("conv_done_dve"), (NX - NXP) * NBLK)
            decay_matrix(0, 0, False)
            decay_matrix(1, 1, False)

            def act_step(t, p):
                square(t - 1, 1 - p)
                decay_matrix(t + 1, 1 - p, True)
                keep_out(t - 1)
            with act.Fori(0, NT // 2 - 1) as i:
                act_step(2 * i + 1, 1)
                act_step(2 * i + 2, 0)
            square(NT - 2, 0)
            keep_out(NT - 2)
            square(NT - 1, 1)
            keep_out(NT - 1)

            act.wait_ge(S("out_kept"), NT)
            act.activation(ssq[:, 1, :], ssq[:, 0, :], ACT.Sqrt, bias=eps_col[:, :], scale=1.0 / DI).then_inc(act_once, reached("gn_sd"))
            with act.Fori(0, NT // 2) as i:
                for p in range(2):
                    t = 2 * i + p
                    act.wait_ge(S("y_st_transposed"), t + 1)
                    act.activation(featT[:, :, ds(t * P, P)], bank[p][:, 0:D].rearrange("p (k n) -> p k n", k=KD), ACT.Copy
                                   ).then_inc(S("yT_ready"), 1)
            with act.Fori(0, NBLK) as blk:
                act.wait_ge(S("score_mm"), blk + 1)
                act.activation(sig[:, ds(blk * BLK, BLK)], bank[3][:, :], ACT.Tanh, scale=0.5).then_inc(S("score_tanh"), 1)
            for b in range(B):
                act.wait_ge(S("pool_tok_turned"), b + 1)
                act.activation(pool_tokT[:, b, :, :], mem_bank[b][0][:, 0:KD * POOL].rearrange("p (k n) -> p k n", k=KD), ACT.Copy
                               ).then_inc(S("pool_tokT_ready"), 1)
            for b in range(B):
                act.wait_ge(S("pool_mm"), b + 1)
                act.activation(poolT[0:SD, b, :], mem_bank[b][1][0:SD, 0:POOL], ACT.Copy).then_inc(S("poolT_ready"), 1)
            for b in range(B):
                act.wait_ge(S("key_mm"), b + 1)
                act.activation(keyT[0:SD, b, :], mem_bank[b][0][0:SD, 0:POOL], ACT.Copy, scale=0.25).then_inc(S("keyT_ready"), 1)

            def keep_q_mem(n):
                act.wait_ge(S("q_mem_mm"), n + 1)
                act.activation(q_mem[0:SD, :], bank[0][0:SD, :], ACT.Copy).then_inc(S("q_mem_ready"), 1)

            def exp_logits(n):
                act.wait_ge(S("logit_shifted"), n + 1)
                act.activation(logit, logit, ACT.Exp).then_inc(S("logit_exp"), 1)

            def keep_retrieved(n):
                act.wait_ge(S("attn_turned"), n + 1)
                act.activation(attnT[0:POOL, :], bank[2][0:POOL, :], ACT.Copy).then_inc(S("attnT_ready"), 1)
                for m in range(KD):
                    act.wait_ge(S("ret_mm"), KD * n + m + 1)
                    act.activation(retT[:, m, :], bank[3 + m][:, :], ACT.Copy).then_inc(S("retT_ready"), 1)

            def gate_halves(n):
                for m in range(KD):
                    act.wait_ge(S("gate_mm"), KD * n + m + 1)
                    act.activation(gate_t[:, m, :], bank[5 + m][:, :], ACT.Tanh, scale=0.5).then_inc(S("gate_tanh"), 1)

            keep_q_mem(0)
            exp_logits(0)
            with act.Fori(0, NBLK - 1) as n:
                keep_retrieved(n)
                keep_q_mem(n + 1)
                exp_logits(n + 1)
                gate_halves(n)
            keep_retrieved(NBLK - 1)
            gate_halves(NBLK - 1)

            act.wait_ge(dve_once, at("ln2_var"))
            act.activation(nrm[:, 0, :], mv[:, :, 1], ACT.Sqrt, bias=eps_col[:, :]).then_inc(act_once, reached("ln2_sd"))
            with act.Fori(0, NT // 2) as i:
                for p in range(2):
                    t = 2 * i + p
                    act.wait_ge(S("ln2_transposed"), t + 1)
                    act.activation(featT[:, :, ds(t * P, P)], bank[p][:, 0:D].rearrange("p (k n) -> p k n", k=KD), ACT.Copy
                                   ).then_inc(S("hT_ready"), 1)

            def keep_q(t, p):
                act.wait_ge(S("q_mm"), t + 1)
                for g in range(NG):
                    m = act.activation(qT[:, p, g, :], bank[5][:, g * P:(g + 1) * P], ACT.Identity, bias=bias_cols[:, 0, g:g + 1])
                m.then_inc(S("qT_ready"), 1)

            def exp_scores(t, p, g):
                act.wait_ge(S("shifted"), NG * t + g + 1)
                mv_, tv = prob_m[p][:, GH * g:GH * (g + 1), :], prob_t[p][:, GH * g:GH * (g + 1), :]
                act.activation(mv_, mv_, ACT.Exp)
                act.activation(tv, tv, ACT.Exp).then_inc(S("prob_ready"), 1)

            def keep_probT(t, g, waits=True):
                act.wait_ge(S("prob_turned"), (NG + 1) * t + g + 1)
                if waits:
                    act.wait_ge(S("pv_mm"), (NG + 1) * (t - 1) + g + 1)
                rows = KM if g < NG else P
                act.activation(probT[0:rows, GH * g:GH * (g + 1), :], bank[TURN_BANK[g]][0:rows, :].rearrange("p (h n) -> p h n", h=GH),
                               ACT.Copy).then_inc(S("probT_ready"), 1)

            act.wait_ge(dve_once, at("bias_cols_ready"))
            keep_q(0, 0)

            def tile_step(t, p, now=True, before=True, waits=True, nxt=True):
                for g in range(NG):
                    if now:
                        exp_scores(t, p, g)
                    if nxt and g == 1:
                        keep_q(t + 1, 1 - p)
                    if before:
                        keep_probT(t - 1, g, waits)
                if before:
                    keep_probT(t - 1, NG, waits)
            tile_step(0, 0, before=False)
            tile_step(1, 1, waits=False)
            with act.Fori(1, NT // 2 - 1) as i:
                for p in range(2):
                    tile_step(2 * i + p, p)
            tile_step(NT - 2, 0)
            tile_step(NT - 1, 1, nxt=False)
            tile_step(NT, 0, now=False, nxt=False)

            act.wait_ge(dve_once, at("ln3_var"))
            act.activation(nrm[:, 0, :], mv[:, :, 1], ACT.Sqrt, bias=eps_col[:, :]).then_inc(act_once, reached("ln3_sd"))
            for j in range(NT // GT):
                if j >= 2:
                    act.wait_ge(S("route_mm"), j - 1)
                for q in range(2):
                    act.wait_ge(S("x3_turned"), 2 * j + q + 1)
                    act.activation(x3T[j % 2][:, 2 * q:2 * q + 2, :, :],
                                   bank[2 * (j % 2) + q][:, :].rearrange("p (t k n) -> p t k n", t=2, k=KD), ACT.Copy
                                   ).then_inc(S("x3T_ready"), 1)

            def keep_hidden(n):
                for f in range(2):
                    act.wait_ge(S("up_mm"), 2 * n + f + 1)
                    if f == 0:
                        act.wait_ge(S("h_turned"), 2 * n)
                    act.activation(hid_e[:, f * 512:(f + 1) * 512], bank[f][:, :], ACT.Copy).then_inc(S("h_kept"), 1)

            def relu_half(n):
                e = act.value_load(expert_i[0:1, ds(n, 1)], min_val=0, max_val=NE - 1)
                act.wait_ge(S("h_turned"), 2 * n + 2)
                act.wait_ge(S("down_mm"), n)
                for f in range(4, 8):
                    i = act.activation(hidT[:, f, :], bank[3][:, (f - 4) * P:(f - 3) * P], ACT.Relu, bias=b1_cols[:, ds(e * NFF + f, 1)])
                i.then_inc(S("hT_half_b"), 1)

            act.wait_ge(dve_once, at("block_expert_ready"))
            keep_hidden(0)
            with act.Fori(0, NB - 1) as n:
                relu_half(n)
                keep_hidden(n + 1)
            relu_half(NB - 1)

        @block.vector
        def _(dve):
            dve.memset(eps_col[:, :], EPS).then_inc(dve_once, reached("eps_set"))
            for q in range(4):
                dve.wait_ge(S(f"x_loaded{q}"), 16)
                for t in range(4 * q, 4 * q + 4):
                    dve.bn_stats(stats[:, t, :], xres[:, t, :]).then_inc(S("bn_done"), 1)
            for t in range(NT):
                dve.wait_ge(S("bn_done"), t + 1)
                dve.bn_aggr(mv[:, t, :], stats[:, t, :]).then_inc(S("ln_agg"), 1)
            dve.wait_ge(S("ln_agg"), NT)
            dve.tensor_copy(nrm[:, 5, :], mv[:, :, 0]).then_inc(dve_once, reached("ln_var"))
            dve.wait_ge(act_once, at("ln_sd"))
            dve.reciprocal(nrm[:, 0, :], nrm[:, 0, :]).then_inc(dve_once, reached("rstd_1"))
            dve.wait_ge(dve_once, at("rstd_1"))
            dve.tensor_tensor(nrm[:, 1, :], mv[:, :, 1], nrm[:, 0, :], ALU.mult).then_inc(dve_once, reached("rstd_2"))
            dve.wait_ge(dve_once, at("rstd_2"))
            dve.tensor_tensor(nrm[:, 1, :], nrm[:, 1, :], nrm[:, 0, :], ALU.mult).then_inc(dve_once, reached("rms_var"))
            dve.wait_ge(act_once, at("rms_sd"))
            dve.reciprocal(nrm[:, 3, :], nrm[:, 2, :]).then_inc(dve_once, reached("rstd_3"))
            dve.wait_ge(dve_once, at("rstd_3"))
            dve.tensor_tensor(nrm[:, 3, :], nrm[:, 3, :], nrm[:, 0, :], ALU.mult).then_inc(dve_once, reached("rstd_4"))
            dve.wait_ge(dve_once, at("rstd_4"))
            dve.tensor_scalar(nrm[:, 1, :], nrm[:, 0, :], 1.0, None, ALU.add).then_inc(S("res_cols"), 1)
            dve.tensor_tensor(nrm[:, 2, :], nrm[:, 5, :], nrm[:, 0, :], ALU.mult).then_inc(S("res_cols"), 1)
            for t in range(NT):
                if t >= GT and t % 2 == 0:
                    dve.wait_ge(S("xn_turned"), t // 2 - 1)
                dve.tensor_scalar(xn[:, t % GT, :], xres[:, t, :], nrm[:, 5, t:t + 1], nrm[:, 3, t:t + 1],
                                  ALU.subtract, ALU.mult).then_inc(S("xn_ready"), 1)
            dve.wait_ge(S("w_loaded"), 16 * 2)
            dve.wait_ge(S("small_loaded"), 16 * 7)
            for k in range(KD):
                dve.tensor_scalar(w_in[:, k, DI:], w_in[:, k, DI:], norm_w[:, k:k + 1], None, ALU.mult
                                  ).then_inc(S("weights_ready"), 1)
            for k in range(KD):
                dve.tensor_scalar(w_in[:, k, 0:DI], w_in[:, k, 0:DI], norm_w[:, k:k + 1], 0.5, ALU.mult, ALU.mult
                                  ).then_inc(S("weights_ready"), 1)
            dve.tensor_scalar(conv_w[:, :, :], conv_w[:, :, :], 0.5, None, ALU.mult).then_inc(S("weights_ready"), 1)
            dve.tensor_scalar(conv_b[:, :], conv_b[:, :], 0.5, None, ALU.mult).then_inc(S("weights_ready"), 1)
            for k in range(NZ):
                dve.tensor_scalar(w_out[:, k, :], w_out[:, k, :], gnorm_w[:, k:k + 1], None, ALU.mult
                                  ).then_inc(S("weights_ready"), 1)
            dve.wait_ge(S("dt_mm"), 1)
            dve.tensor_tensor(th(dt_raw), bank[4][:, 0:NT * H].rearrange("p (t h) -> p t h", h=H),
                              dt_bias[:, :].unsqueeze(1).broadcast_to([P, NT, H]), ALU.add).then_inc(S("dt_kept"), 1)
            dve.wait_ge(S("dt_kept"), 1)
            dve.tensor_scalar(dt_neg, dt_raw, -1.0, None, ALU.mult).then_inc(dve_once, reached("dt_steps_1"))
            dve.tensor_scalar(dt_pos, dt_raw, 0.0, None, ALU.max).then_inc(dve_once, reached("dt_steps_2"))
            dve.wait_ge(dve_once, at("dt_steps_2"))
            dve.tensor_tensor(dt_neg, dt_neg, dt_raw, ALU.min).then_inc(dve_once, reached("dt_abs"))

            dve.wait_ge(S("weights_ready"), 2 * KD + NZ + 2)
            dve.wait_ge(S("xn_turned"), NT // 2)
            with dve.Fori(0, B) as b:
                dve.wait_ge(S("raw_used"), NX * (NBLK // B) * b)
                dve.memset(raw[:, :, 0:TAPS - 1], 0.0).then_inc(S("past_cleared"), 1)
                with dve.Fori(0, NBLK // B) as j:
                    dve.wait_ge(S("past_cleared"), b + 1)
                    blk = b * (NBLK // B) + j
                    for f in range(NZ):
                        dve.wait_ge(S("tanh_z_ready"), NZ * blk + f + 1)
                        dve.scalar_tensor_tensor(zsT[:, f, ds(blk * BLK, BLK)], tanh_z[:, f % 2, :], 1.0, bank[f % 5][:, :],
                                                 ALU.add, ALU.mult).then_inc(S("zs_ready"), 1)
                    for f in range(0, NX, 2):
                        for k in range(1, TAPS):
                            for g in (f, f + 1):
                                if k == 1:
                                    dve.wait_ge(S("tap0_ready"), NX * blk + g + 1)
                                else:
                                    dve.wait_ge(S("tap_done"), (TAPS - 2) * (NX * blk + f) + 2 * (k - 2) + g - f + 1)
                                acc = conv[:, g, :]
                                i = dve.scalar_tensor_tensor(acc, raw[:, g, k:k + BLK], conv_w[:, g, k:k + 1], acc, ALU.mult, ALU.add)
                                i.then_inc(S("tap_done") if k < TAPS - 1 else S("conv_sum"), 1)
                        for g in (f, f + 1):
                            dve.tensor_copy(raw[:, g, 0:TAPS - 1], raw[:, g, BLK:BLK + TAPS - 1]).then_inc(S("raw_used"), 1)
                    for f in range(NXP, NX):
                        dve.wait_ge(S("tanh_c_ready"), NX * blk + f + 1)
                        dve.scalar_tensor_tensor(xbcT[:, f, ds(blk * BLK, BLK)], tanh_c[:, f, :], 1.0, conv[:, f, :],
                                                 ALU.add, ALU.mult).then_inc(S("conv_done_dve"), 1)

            dve.wait_ge(act_once, at("dt_ln"))
            dve.tensor_tensor(dt_v, dt_pos, dt_exp, ALU.add).then_inc(dve_once, reached("dt_sum"))
            dve.wait_ge(dve_once, at("dt_sum"))
            dve.wait_ge(act_once, at("a_exp"))
            dve.scalar_tensor_tensor(th(dta), th(dt_v), -1.0, a_log[:, :].unsqueeze(1).broadcast_to([P, NT, H]),
                                     ALU.mult, ALU.mult).then_inc(dve_once, reached("dt_ready"))
            dve.wait_ge(act_once, at("dec_exp"))
            dve.tensor_copy(tot, bank[1][:, 0:NT * H]).then_inc(dve_once, reached("tot_kept"))
            dve.wait_ge(dve_once, at("tot_kept"))
            dve.wait_ge(act_once, at("ecum_exp"))
            dve.tensor_tensor(wend, tot, bank[0][:, 0:NT * H], ALU.subtract).then_inc(dve_once, reached("wend_diff"))
            dve.memset(th(ecum)[:, 0:NT:TB, :], 0.0).then_inc(dve_once, reached("first_cleared_1"))
            dve.memset(th(dec)[:, 0:NT:TB, :], 0.0).then_inc(dve_once, reached("first_cleared_2"))
            dve.wait_ge(dve_once, at("first_cleared_2"))
            dve.wait_ge(act_once, at("wend_exp"))
            dve.tensor_tensor(wend, wend, dt_v, ALU.mult).then_inc(dve_once, reached("decay_ready"))
            dve.wait_ge(dve_once, at("decay_ready"))
            dve.wait_ge(S("conv_done"), NXP * NBLK)
            dve.wait_ge(S("conv_done_dve"), (NX - NXP) * NBLK)

            def chunk_sides(t, p, wait):
                dve.wait_ge(S("g_mm"), t + 1)
                if wait:
                    dve.wait_ge(S("state_mm"), t - 1)
                dve.tensor_copy(b_tok[:, p, :], bank[1][:, 0:P])
                if wait:
                    dve.wait_ge(S("m_ready"), t - 1)
                dve.tensor_tensor(gmat[:, p, :], bank[1][:, P:2 * P], tri_le[:, :], ALU.mult).then_inc(S("g_ready"), 1)
                xv = bank[0][:, :].rearrange("p (h n) -> p h n", h=H)
                for dst, col in ((xdt, dt_v), (xend, wend)):
                    dve.tensor_tensor(dst[:, p, :].rearrange("p (h n) -> p h n", h=H), xv, heads(col[:, ds(t * H, H)], HP),
                                      ALU.mult)
                if wait:
                    dve.wait_ge(S("y_ready"), t - 1)
                dve.tensor_tensor(xskip[:, p, :].rearrange("p (h n) -> p h n", h=H), xv, heads(d_skip[:, :], HP),
                                  ALU.mult).then_inc(S("sides_ready"), 1)

            def gate(t, p, wait):
                dve.wait_ge(S("y_transposed"), t + 1)
                if wait:
                    dve.wait_ge(S("out_mm"), t - 1)
                    dve.wait_ge(S("sq_ready"), t - 1)
                dve.tensor_tensor(gated[:, p, :, :], bank[7][:, :].rearrange("p (k n) -> p k n", k=NZ),
                                  zsT[:, :, ds(t * P, P)], ALU.mult).then_inc(S("gated_ready"), 1)

            def sum_y(t, p, wait):
                yv = y_in[:, p, :]
                dve.wait_ge(S("inter_mm"), t + 1)
                if wait:
                    dve.wait_ge(S("y_transposed"), t - 1)
                dve.tensor_tensor(yv.rearrange("p (h n) -> p h n", h=H), bank[4][:, :].rearrange("p (h n) -> p h n", h=H),
                                  heads(ecum[:, ds(t * H, H)], HP), ALU.mult).then_inc(S("y_part"), 1)
                dve.wait_ge(S("intra_mm"), t + 1)
                dve.wait_ge(S("y_part"), 2 * t + 1)
                dve.tensor_tensor(yv, yv, bank[5][:, :], ALU.add).then_inc(S("y_part"), 1)
                dve.wait_ge(S("y_part"), 2 * t + 2)
                dve.wait_ge(S("sides_ready"), t + 1)
                dve.tensor_tensor(yv, yv, xskip[:, p, :], ALU.add).then_inc(S("y_ready"), 1)
                dve.wait_ge(S("state_mm"), t + 1)
                dve.wait_ge(S("state_decayed"), t + 1)
                dve.tensor_tensor(state, state, bank[6][:, :], ALU.add).then_inc(S("state_added"), 1)

            chunk_sides(0, 0, False)
            chunk_sides(1, 1, False)
            sum_y(0, 0, False)

            def dve_step(t, p, wait=True):
                chunk_sides(t + 1, 1 - p, True)
                gate(t - 1, 1 - p, wait)
                sum_y(t, p, wait)
            dve_step(1, 1, False)
            dve_step(2, 0)
            with dve.Fori(1, NT // 2 - 1) as i:
                dve_step(2 * i + 1, 1)
                dve_step(2 * i + 2, 0)
            gate(NT - 2, 0, True)
            sum_y(NT - 1, 1, True)
            gate(NT - 1, 1, True)

            dve.wait_ge(act_once, at("gn_sd"))
            dve.reciprocal(ssq[:, 1, :], ssq[:, 1, :]).then_inc(dve_once, reached("gn_rstd"))
            dve.wait_ge(dve_once, at("gn_rstd"))
            dve.wait_ge(S("state_added"), NT)
            dve.wait_ge(S("y_ready"), NT)
            with dve.Fori(0, NT // 2) as i:
                for p in range(2):
                    t = 2 * i + p
                    if p == 0:
                        dve.wait_ge(S("res_y_added"), 2 * i)
                        dve.wait_ge(S("y_st_transposed"), 2 * i)
                    yt = y_tok[:, ds(t, 1), :].rearrange("p a d -> p (a d)")
                    dve.tensor_scalar(y_st[:, p, :], yt, ssq[:, 1, ds(t, 1)], None, ALU.mult).then_inc(S("y_st_ready"), 1)
                    dve.tensor_scalar(yt, yt, ssq[:, 1, ds(t, 1)], None, ALU.mult).then_inc(S("y_tok_ready"), 1)
            dve.wait_ge(S("mem_w_loaded"), 16 * 7)
            dve.tensor_copy(scorer_w2b[:, :], scorer_w2[:, 0:1].broadcast_to([SD, P])).then_inc(dve_once, reached("w2b_ready"))
            dve.wait_ge(pool_once, at("pos_set"))
            dve.tensor_copy(pos[:, :], pos_i[:, :]).then_inc(dve_once, reached("pos_ready"))
            dve.memset(ones_bf[:, 0:1], 1.0)
            dve.tensor_copy(n_earlier, tile_i[:, :]).then_inc(dve_once, reached("cols_set"))
            with dve.Fori(0, NBLK // 2) as i:
                for p in range(2):
                    blk = 2 * i + p
                    dve.wait_ge(S("hid_mm"), blk + 1)
                    if p == 0:
                        dve.wait_ge(S("score_mm"), 2 * i)
                    dve.tensor_scalar(hid[0:SD, p, :], bank[2 + 4 * p][0:SD, :], 0.0, None, ALU.max).then_inc(S("hid_ready"), 1)
            with dve.Fori(0, NBLK) as blk:
                dve.wait_ge(S("score_tanh"), blk + 1)
                sv = sig[:, ds(blk * BLK, BLK)]
                dve.tensor_scalar(sv, sv, 0.5, 0.5, ALU.mult, ALU.add).then_inc(S("sig_ready"), 1)
            dve.wait_ge(S("sig_ready"), NBLK)
            for b in range(B):
                dve.wait_ge(S("s_col_ready"), b)
                dve.tensor_tensor(junk.rearrange("p (t n) -> p t n", t=TB), sig[:, b * T:(b + 1) * T].rearrange("p (t n) -> p t n", t=TB),
                                  ident[:, :].unsqueeze(1).broadcast_to([P, TB, P]), ALU.mult).then_inc(S("memory_step"), 1)
                dve.wait_ge(S("memory_step"), b + 1)
                dve.tensor_reduce(s_col[:, b * TB:(b + 1) * TB], junk.rearrange("p (t n) -> p t n", t=TB), AX, ALU.add
                                  ).then_inc(S("s_col_ready"), 1)
            dve.wait_ge(S("s_col_ready"), B)
            dve.tensor_scalar(valid, s_col, 0.5, None, ALU.is_gt).then_inc(dve_once, reached("valid_ready"))
            for b in range(B):
                for k in range(TB):
                    t = b * TB + k
                    sc = s_col[:, t:t + 1]
                    if t >= 2:
                        dve.wait_ge(S("rank_counted"), 2 * (t - 1))
                    if k >= 2 or b:
                        dve.wait_ge(S("rank_cols"), (TB - 1) * b + max(k - 1, 0))
                    dve.tensor_scalar(greater[:, k % 2, k * P:T], sig[:, b * T + k * P:(b + 1) * T], sc, None, ALU.is_gt, ALU.add,
                                      accum_out=n_gt[:, t:t + 1]).then_inc(S("rank_counted"), 1)
                    dve.scalar_tensor_tensor(junk_eq[:, k % 2, :], sig[:, t * P:(t + 1) * P], sc, tri_gt[:, :], ALU.is_equal, ALU.mult,
                                             accum_out=n_eq[:, t:t + 1]).then_inc(S("rank_counted"), 1)
            dve.wait_ge(S("rank_counted"), 2 * NT)
            dve.tensor_tensor(rank, n_gt, n_eq, ALU.add).then_inc(dve_once, reached("rank_sum_1"))
            dve.wait_ge(dve_once, at("rank_sum_1"))
            dve.wait_ge(dve_once, at("cols_set"))
            dve.tensor_tensor(rank, rank, n_earlier, ALU.add).then_inc(dve_once, reached("rank_sum_2"))
            dve.wait_ge(dve_once, at("rank_sum_2"))
            dve.wait_ge(S("rank_cols"), (TB - 1) * B)
            later = [v.rearrange("p (b t) -> p b t", b=B)[:, :, 1:] for v in (rank, bank[7][:, 0:NT])]
            dve.tensor_tensor(later[0], later[0], later[1], ALU.subtract).then_inc(dve_once, reached("rank_sum_3"))
            dve.wait_ge(dve_once, at("rank_sum_3"))
            dve.wait_ge(S("mean_mm"), 1)
            dve.tensor_reduce(mean_s[:, :], bank[6][:, 0:NT].rearrange("p (b t) -> p b t", b=B), AX, ALU.add).then_inc(dve_once, reached("mean_ready_1"))
            dve.wait_ge(dve_once, at("mean_ready_1"))
            dve.tensor_scalar(mean_s[:, :], mean_s[:, :], 1.0 / T, 0.3, ALU.mult, ALU.is_gt).then_inc(dve_once, reached("mean_ready_2"))
            dve.wait_ge(dve_once, at("valid_ready"))
            dve.wait_ge(dve_once, at("pos_ready"))
            dve.wait_ge(dve_once, at("mean_ready_2"))
            for b in range(B):
                oh = onehot[:, b * TB:(b + 1) * TB, :]
                dve.tensor_tensor(oh, pos[:, :].unsqueeze(1).broadcast_to([P, TB, POOL]),
                                  rank[:, b * TB:(b + 1) * TB].unsqueeze(2).broadcast_to([P, TB, POOL]), ALU.is_equal
                                  ).then_inc(S("memory_step"), 1)
                dve.wait_ge(S("memory_step"), B + b + 1)
                dve.tensor_tensor(oh, oh, valid[:, b * TB:(b + 1) * TB].unsqueeze(2).broadcast_to([P, TB, POOL]), ALU.mult
                                  ).then_inc(S("onehot_ready"), 1)
            for b in range(B):
                dve.wait_ge(S("select_mm"), b + 1)
                dve.tensor_copy(pool_tok[0:POOL, b, :], mem_bank[b][1][0:POOL, 0:D]).then_inc(S("pool_tok_ready"), 1)
                dve.tensor_scalar(vbias[:, b, :], mem_bank[b][2][:, 0:POOL], -1.0, 1e9, ALU.add, ALU.mult).then_inc(S("vbias_ready"), 1)
            for b in range(B):
                dve.wait_ge(S("val_mm"), b + 1)
                dve.tensor_scalar(val[0:POOL, b, :], mem_bank[b][2][0:POOL, 0:D], mean_s[0:POOL, b:b + 1], None, ALU.mult
                                  ).then_inc(S("val_ready"), 1)
            dve.wait_ge(S("vbias_ready"), B)
            dve.wait_ge(S("val_ready"), B)

            def soften(n, first=False):
                dve.wait_ge(S("logit_mm"), n + 1)
                if not first:
                    dve.wait_ge(S("attn_turned"), n)
                b = n // (T // BLK)
                dve.tensor_tensor(logit, bank[1][:, 0:4 * 64].rearrange("p (i n) -> p i n", i=4)[:, :, 0:POOL],
                                  vbias[:, ds(b, 1), :].broadcast_to([P, 4, POOL]), ALU.add).then_inc(S("soften_step"), 1)
                dve.wait_ge(S("soften_step"), 4 * n + 1)
                dve.tensor_reduce(red[:, 0, :], logit, AX, ALU.max).then_inc(S("soften_step"), 1)
                dve.wait_ge(S("soften_step"), 4 * n + 2)
                dve.tensor_tensor(logit, logit, red[:, 0, :].unsqueeze(2).broadcast_to([P, 4, POOL]), ALU.subtract
                                  ).then_inc(S("logit_shifted"), 1)
                if not first:
                    dve.wait_ge(S("ret_mm"), KD * n)
                dve.tensor_copy(val_now[0:POOL, :], val[0:POOL, ds(b, 1), :].rearrange("p a d -> p (a d)")).then_inc(S("val_now_ready"), 1)
                dve.wait_ge(S("logit_exp"), n + 1)
                dve.tensor_reduce(red[:, 1, :], logit, AX, ALU.add).then_inc(S("soften_step"), 1)
                dve.wait_ge(S("soften_step"), 4 * n + 3)
                dve.reciprocal(red[:, 2, :], red[:, 1, :]).then_inc(S("soften_step"), 1)
                dve.wait_ge(S("soften_step"), 4 * n + 4)
                dve.tensor_tensor(logit, logit, red[:, 2, :].unsqueeze(2).broadcast_to([P, 4, POOL]), ALU.mult
                                  ).then_inc(S("attn_ready"), 1)

            def add_retrieved(n):
                for m in range(KD):
                    dve.wait_ge(S("gate_tanh"), KD * n + m + 1)
                    if m == 0:
                        dve.wait_ge(S("upd_turned"), 2 * n)
                    dve.scalar_tensor_tensor(upd[:, m, :], gate_t[:, m, :], 1.0, retT[:, m, :], ALU.add, ALU.mult
                                             ).then_inc(S("upd_ready"), 1)
                for m in range(2):
                    dve.wait_ge(S("upd_turned"), 2 * n + m + 1)
                    xv = xres[:, ds(4 * n + 2 * m, 2), :]
                    dve.scalar_tensor_tensor(xv, bank[7 * (1 - m)][:, :].rearrange("p (t d) -> p t d", t=2), 0.5, xv,
                                             ALU.mult, ALU.add).then_inc(S("x1_ready"), 1)
                dve.wait_ge(S("x1_ready"), 2 * n + 2)
                for i in range(4):
                    dve.bn_stats(stats[:, ds(4 * n + i, 1), :], xres[:, ds(4 * n + i, 1), :]).then_inc(S("bn_done"), 1)

            dve.wait_ge(S("res_y_added"), NT)
            soften(0, True)
            with dve.Fori(0, NBLK - 1) as n:
                soften(n + 1)
                add_retrieved(n)
            add_retrieved(NBLK - 1)

            dve.wait_ge(S("bn_done"), 2 * NT)
            for t in range(NT):
                dve.bn_aggr(mv[:, t, :], stats[:, t, :]).then_inc(S("ln_agg"), 1)
            dve.wait_ge(S("ln_agg"), 2 * NT)
            dve.tensor_copy(nrm[:, 5, :], mv[:, :, 0]).then_inc(dve_once, reached("ln2_var"))
            dve.wait_ge(act_once, at("ln2_sd"))
            dve.reciprocal(nrm[:, 0, :], nrm[:, 0, :]).then_inc(dve_once, reached("ln2_rstd"))
            dve.wait_ge(dve_once, at("ln2_rstd"))
            dve.wait_ge(S("select_mm"), B)
            with dve.Fori(0, NT // 2) as i:
                for p in range(2):
                    t = 2 * i + p
                    if p == 0:
                        dve.wait_ge(S("ln2_transposed"), 2 * i)
                    dve.tensor_scalar(ln_st[:, p, :], xres[:, ds(t, 1), :].rearrange("p a d -> p (a d)"), nrm[:, 5, ds(t, 1)],
                                      nrm[:, 0, ds(t, 1)], ALU.subtract, ALU.mult).then_inc(S("ln2_ready"), 1)
            dve.wait_ge(S("x_w_loaded"), 16 * 9)
            dve.tensor_scalar(mask_row[:, :], mask_i[:, :], 0.0, 4 * NEG, ALU.is_gt, ALU.mult).then_inc(dve_once, reached("mask_row_ready"))
            dve.wait_ge(S("bias_turned"), 1)
            dve.tensor_copy(bias_cols[:, :, :], bank[2][:, 0:2 * NG].rearrange("p (n g) -> p n g", n=2)).then_inc(dve_once, reached("bias_cols_ready"))
            dve.wait_ge(dve_once, at("bias_cols_ready"))
            dve.wait_ge(pool_once, at("pads_zero_5"))
            for b in range(B):
                for g in range(NG):
                    n = NG * b + g
                    dve.wait_ge(S("keys_mm"), n + 1)
                    for h in range(GH):
                        r = slice(32 * h, 32 * h + 32)
                        i = dve.tensor_scalar(keys[r, b, g, h * LK:(h + 1) * LK], bank[3 + n % 2][r, 0:LK], bias_cols[r, 1, g:g + 1], 0.25,
                                              ALU.add, ALU.mult)
                    i.then_inc(S("keys_ready"), 1)
                dve.wait_ge(S("val_main_mm"), b + 1)
                dve.tensor_copy(v_main[0:KM, b, :, 0:HD], bank[5][0:KM, 0:D].rearrange("p (h d) -> p h d", d=HD)).then_inc(S("v_main_ready"), 1)
                dve.wait_ge(S("val_tail_mm"), b + 1)
                for h in range(GH):
                    r = slice(32 * h, 32 * h + 32)
                    dve.memset(v_tail[r, b, :, h * (HD + 1) + HD:(h + 1) * (HD + 1)], 1.0)
                    i = dve.tensor_copy(v_tail[r, b, :, h * (HD + 1):h * (HD + 1) + HD],
                                        bank[6][r, 0:D].rearrange("p (g h d) -> p g h d", g=NG, h=GH)[:, :, h, :])
                i.then_inc(S("v_tail_ready"), 1)

            def shift_scores(t, p, g):
                m = NG * t + g
                h = slice(GH * g, GH * (g + 1))
                sc = pair[g % 2][:, :, 0:2 * LK].rearrange("p a (h n) -> p a h n", h=2)
                mx = xmax[:, p, h]
                mx4 = mx.rearrange("p (a h) -> p a h", a=2).unsqueeze(3)
                four = lambda v: v.rearrange("p (a h) n -> p a h n", a=2)
                dve.wait_ge(S("score_x_mm"), m + 1)
                dve.tensor_reduce(mx.rearrange("p (a h) -> p a h", a=2), sc, AX, ALU.max).then_inc(S("score_max"), 1)
                dve.wait_ge(S("score_max"), m + 1)
                dve.tensor_tensor(four(prob_m[p][:, h, :]), sc[:, :, :, 0:KM], mx4.broadcast_to([P, 2, 2, KM]), ALU.subtract)
                dve.tensor_tensor(four(prob_t[p][:, h, :]), sc[:, :, :, KM:LK], mx4.broadcast_to([P, 2, 2, KT]), ALU.subtract
                                  ).then_inc(S("shifted"), 1)

            def row_stats(t):
                dve.wait_ge(S("x2_ready"), t + 1)
                dve.bn_stats(stats[:, ds(t, 1), :], xres[:, ds(t, 1), :]).then_inc(S("bn_done"), 1)

            def weigh(t, p, waits=True):
                dve.wait_ge(S("pv_mm"), (NG + 1) * (t + 1))
                ov = bank[6 + p][:, 0:XH * (HD + 1)].rearrange("p (h c) -> p h c", c=HD + 1)
                dve.reciprocal(xinv[:, p, :], ov[:, :, HD]).then_inc(S("x_inv"), 1)
                dve.wait_ge(S("x_inv"), t + 1)
                if waits:
                    dve.wait_ge(S("x2_ready"), t - 1)
                dve.tensor_tensor(head_o[:, p, :].rearrange("p (h d) -> p h d", d=HD), ov[:, :, 0:HD],
                                  xinv[:, p, :].unsqueeze(2).broadcast_to([P, XH, HD]), ALU.mult).then_inc(S("head_o_ready"), 1)

            def tile_step(t, p, now=True, before=True, waits=True):
                if now and before:
                    dve.wait_ge(S("prob_turned"), (NG + 1) * (t - 1))
                for g in range(NG):
                    if now:
                        shift_scores(t, p, g)
                    if before and g == 1:
                        weigh(t - 2, p, waits)
                if before and waits:
                    row_stats(t - 4)
            tile_step(0, 0, before=False)
            tile_step(1, 1, before=False)
            tile_step(2, 0, waits=False)
            tile_step(3, 1, waits=False)
            with dve.Fori(2, NT // 2) as i:
                for p in range(2):
                    tile_step(2 * i + p, p)
            tile_step(NT, 0, now=False)
            tile_step(NT + 1, 1, now=False)
            row_stats(NT - 2)
            row_stats(NT - 1)

            dve.wait_ge(S("bn_done"), 3 * NT)
            for t in range(NT):
                dve.bn_aggr(mv[:, t, :], stats[:, t, :]).then_inc(S("ln_agg"), 1)
            dve.wait_ge(S("ln_agg"), 3 * NT)
            dve.tensor_copy(nrm[:, 5, :], mv[:, :, 0]).then_inc(dve_once, reached("ln3_var"))
            dve.wait_ge(act_once, at("ln3_sd"))
            dve.reciprocal(nrm[:, 0, :], nrm[:, 0, :]).then_inc(dve_once, reached("ln3_rstd"))
            dve.wait_ge(dve_once, at("ln3_rstd"))
            dve.wait_ge(S("route_w_loaded"), 16 * 3)

            def add_br(j):
                dve.wait_ge(S("route_mm"), j + 1)
                dve.tensor_tensor(logits[:, GT * j:GT * (j + 1), :], bank[4 + j % 2][:, 0:GT * NE].rearrange("p (t e) -> p t e", t=GT),
                                  br_row.unsqueeze(1).broadcast_to([P, GT, NE]), ALU.add).then_inc(S("logits_ready"), 1)

            for j in range(NT // GT):
                for q in range(GT):
                    t = GT * j + q
                    if j and q % 2 == 0:
                        dve.wait_ge(S("x3_turned"), 2 * (j - 1) + q // 2 + 1)
                    dve.tensor_scalar(st4[:, q, :], xres[:, t, :], nrm[:, 5, t:t + 1], nrm[:, 0, t:t + 1],
                                      ALU.subtract, ALU.mult).then_inc(S("x3_ready"), 1)
                if j:
                    add_br(j - 1)
            add_br(NT // GT - 1)
            dve.wait_ge(pool_once, at("counters_set"))
            dve.tensor_copy(desc, desc_i)
            dve.tensor_copy(thr, thr_i)
            dve.tensor_copy(blk_n, blk_i).then_inc(dve_once, reached("iotas_ready"))
            dve.wait_ge(dve_once, at("iotas_ready"))
            dve.wait_ge(S("logits_ready"), NT // GT)

            def along(v, n):
                return v.unsqueeze(2).broadcast_to([P, v.shape[1], n])

            def across(v, n):
                return v.unsqueeze(1).broadcast_to([P, n, v.shape[1]])

            def link(ins):
                links[0] += 1
                ins.then_inc(S("route_step"), 1)
                dve.wait_ge(S("route_step"), links[0])
            links = [0]
            link(dve.tensor_reduce(best, logits, AX, ALU.max))
            link(dve.tensor_tensor(hot, logits, along(best, NE), ALU.is_equal))
            link(dve.tensor_tensor(hot, hot, across(desc, NT), ALU.mult))
            link(dve.tensor_reduce(best, hot, AX, ALU.max))
            dve.tensor_tensor(hot, across(desc, NT), along(best, NE), ALU.is_equal).then_inc(S("hot_ready"), 1)
            link(dve.memset(before[:, 0, :], 0.0))
            dve.wait_ge(S("count_mm"), 2)
            tile_n = bank[5][:, 0:NT * NE].rearrange("p (t e) -> p t e", e=NE)
            for t in range(NT):
                link(dve.tensor_tensor(before[:, t + 1, :], before[:, t, :], tile_n[:, t, :], ALU.add))
            link(dve.tensor_tensor(blocks_c, along(before[:, NT, :], NT), across(thr, NE), ALU.is_gt))
            link(dve.memset(first_blk[:, 0:1], 0.0))
            link(dve.tensor_reduce(first_blk[:, 1:], blocks_c, AX, ALU.add))
            for e in range(1, NE):
                link(dve.tensor_tensor(first_blk[:, e + 1:e + 2], first_blk[:, e + 1:e + 2], first_blk[:, e:e + 1], ALU.add))
            link(dve.tensor_tensor(slot_t, bank[4][:, 0:NT * NE].rearrange("p (t e) -> p t e", e=NE), before[:, 0:NT, :], ALU.add))
            link(dve.scalar_tensor_tensor(slot_t, across(first_blk[:, 0:NE], NT), float(P), slot_t, ALU.mult, ALU.add))
            link(dve.tensor_tensor(slot_t, slot_t, hot, ALU.mult))
            link(dve.tensor_reduce(slot_f, slot_t, AX, ALU.add))
            link(dve.tensor_scalar(slot_i, slot_f, -1.0, None, ALU.add))
            link(dve.tensor_tensor(expert_c, along(blk_n, NE), across(first_blk[:, 1:], NB), ALU.is_ge))
            link(dve.tensor_reduce(expert_f, expert_c, AX, ALU.add))
            dve.tensor_scalar(expert_i, expert_f, float(NE - 1), None, ALU.min).then_inc(dve_once, reached("block_expert_ready"))
            with dve.Fori(0, NT // GT) as i:
                for p in range(GT):
                    t = GT * i + p
                    dve.wait_ge(S(f"scattered{p}"), 16 * i)
                    xt = xres[:, ds(t, 1), :].rearrange("p a d -> p (a d)")
                    dve.tensor_scalar(rows[:, p, 0:D], xt, nrm[:, 5, ds(t, 1)], nrm[:, 0, ds(t, 1)], ALU.subtract, ALU.mult)
                    dve.tensor_copy(rows[:, p, D:2 * D], xt)
                    dve.tensor_copy(rows[:, p, 2 * D:].bitcast(I32), token_i[:, ds(t, 1)])
                    dve.tensor_copy(slot_now[:, p:p + 1], slot_i[:, ds(t, 1)]).then_inc(S("row_ready"), 1)

            def keep_xs(n, p):
                dve.wait_ge(S("xs_turned"), n + 1)
                dve.tensor_copy(xsT[:, p, :, :], bank[6][:, 0:D].rearrange("p (k n) -> p k n", k=KD)).then_inc(S("xsT_ready"), 1)

            def relu_and_add(n, p, nxt=True):
                e = dve.value_load(expert_i[0:1, ds(n, 1)], min_val=0, max_val=NE - 1)
                dve.wait_ge(S("h_turned"), 2 * n + 1)
                dve.wait_ge(S("down_mm"), n)
                for f in range(4):
                    i = dve.tensor_scalar(hidT[:, f, :], bank[2][:, f * P:(f + 1) * P], b1_cols[:, ds(e * NFF + f, 1)], 0.0, ALU.add, ALU.max)
                i.then_inc(S("hT_half_a"), 1)
                dve.wait_ge(S(f"rest_loaded{p}"), 8 * (n - p) + 16)
                dve.wait_ge(S(f"out_stored{p}"), 8 * (n - p))
                dve.tensor_tensor(yo[:, p, :], rest[:, p, 0:D], b2_rows[:, ds(e, 1), :].rearrange("p a d -> p (a d)"), ALU.add
                                  ).then_inc(S("yo_part"), 1)
                if nxt:
                    keep_xs(n + 2, p)
                dve.wait_ge(S("yo_part"), n + 1)
                dve.wait_ge(S("down_mm"), n + 1)
                dve.tensor_tensor(yo[:, p, :], yo[:, p, :], bank[4][:, 0:D], ALU.add).then_inc(S("yo_ready"), 1)

            dve.wait_ge(S("w2_loaded"), 16 * 2 * NE)
            keep_xs(0, 0)
            keep_xs(1, 1)
            with dve.Fori(0, NB // 2 - 1) as i:
                relu_and_add(2 * i, 0)
                relu_and_add(2 * i + 1, 1)
            relu_and_add(NB - 3, 0)
            relu_and_add(NB - 2, 1, False)
            relu_and_add(NB - 1, 0, False)

        @block.tensor
        def _(pe):
            pe.wait_ge(pool_once, at("masks_set_3"))

            def turn_group(j):
                for q in range(GT):
                    t = GT * j + q
                    pe.wait_ge(S("xn_ready"), t + 1)
                    if t % 2 == 0 and t >= 2 * 4:
                        pe.wait_ge(S("xnT_ready"), t // 2 - 3)
                    for k in range(KD):
                        m = pe.transpose(bank[(t // 2) % 4][:, (t % 2) * D + k * P:(t % 2) * D + (k + 1) * P],
                                         xn[:, q, k * P:(k + 1) * P], ident[:, :])
                    if t % 2:
                        m.then_inc(S("xn_turned"), 1)

            def dt_group(j):
                pe.wait_ge(S("xnT_ready"), 2 * (j + 1))
                pe.wait_ge(S("weights_ready"), KD)
                for t in range(GT * j, GT * (j + 1)):
                    for k in range(KD):
                        m = pe.matmul(bank[4][:, t * H:(t + 1) * H], featT[:, k, t * P:(t + 1) * P], w_in[:, k, IN_W - H:],
                                      start=(k == 0), stop=(k == KD - 1))
                if j == NT // GT - 1:
                    m.then_inc(S("dt_mm"), 1)
            for j in range(NT // GT):
                turn_group(j)
            for j in range(NT // GT):
                dt_group(j)
            pe.wait_ge(S("weights_ready"), 2 * KD)
            pe.wait_ge(S("dt_kept"), 1)
            with pe.Fori(0, NBLK) as blk:
                pe.wait_ge(S("raw_ready"), NX * blk)
                pe.wait_ge(S("zs_ready"), NZ * blk)
                for f in range(NZ + NX):
                    if 5 <= f < 5 + NZ:
                        pe.wait_ge(S("zs_ready"), NZ * blk + f - 4)
                    if f == 5 + NZ:
                        pe.wait_ge(S("raw_ready"), NX * blk + 1)
                    for k in range(KD):
                        m = pe.matmul(bank[f % 5][:, :], w_in[:, k, f * P:(f + 1) * P], featT[:, k, ds(blk * BLK, BLK)],
                                      start=(k == 0), stop=(k == KD - 1))
                    m.then_inc(S("proj_mm"), 1)
            pe.wait_ge(dve_once, at("dt_ready"))
            pe.wait_ge(S("raw_ready"), NX * NBLK)
            pe.wait_ge(S("zs_ready"), NZ * NBLK)
            pe.matmul(bank[0][:, 0:NT * H], tri_le[:, :], dta, start=True, stop=True).then_inc(S("cum_mm"), 1)
            pe.matmul(bank[1][:, 0:NT * H], ones[:, :], dta, start=True, stop=True).then_inc(S("cum_mm"), 1)
            pe.wait_ge(dve_once, at("decay_ready"))

            def turn(t, p, wait):
                pe.wait_ge(S(f"chunk_loaded{p}"), 8 * (t - p) + 16)
                if wait:
                    pe.wait_ge(S("sides_ready"), t)
                for k in range(NZ):
                    pe.transpose(bank[0][:, k * P:(k + 1) * P], xbc[:, p, k, :], ident[:, :])
                pe.transpose(bank[1][:, 0:P], xbc[:, p, NZ, :], ident[:, :])
                pe.matmul(bank[1][:, P:2 * P], xbc[:, p, NZ, :], xbc[:, p, NZ + 1, :], start=True, stop=True
                          ).then_inc(S("g_mm"), 1)

            def segments(t, p, wait):
                pe.wait_ge(S("seg_ready"), t + 1)
                if wait:
                    pe.wait_ge(S("decay_mat"), t)
                for q in range(2):
                    m = pe.matmul(bank[2 + q][:, :], tri_gt[:, :], seg[:, p, 4 * q:4 * q + 4, :], start=True, stop=True)
                m.then_inc(S("seg_mm"), 1)

            def transpose_y(t, p, wait):
                pe.wait_ge(S("y_ready"), t + 1)
                if wait:
                    pe.wait_ge(S("out_kept"), t)
                for k in range(NZ):
                    m = pe.transpose(bank[7][:, k * P:(k + 1) * P], y_in[:, p, k * P:(k + 1) * P], ident[:, :])
                m.then_inc(S("y_transposed"), 1)

            def mix(t, p, wait):
                pe.wait_ge(S("sides_ready"), t + 1)
                pe.wait_ge(S("state_added"), t) if wait else pe.wait_ge(pool_once, at("state_set"))
                pe.matmul(bank[4][:, :], xbc[:, p, NZ + 1, :], state, start=True, stop=True).then_inc(S("inter_mm"), 1)
                pe.wait_ge(S("m_ready"), t + 1)
                for h in range(H):
                    m = pe.matmul(bank[5][:, h * HP:(h + 1) * HP], lmat[:, p, h, :], xdt[:, p, h * HP:(h + 1) * HP],
                                  start=True, stop=True)
                m.then_inc(S("intra_mm"), 1)
                pe.matmul(bank[6][:, :], b_tok[:, p, :], xend[:, p, :], start=True, stop=True).then_inc(S("state_mm"), 1)

            def project_out(t, p):
                pe.wait_ge(S("gated_ready"), t + 1)
                for k in range(NZ):
                    pe.matmul(bank[7][:, 0:D], gated[:, p, k, :], w_out[:, k, :], start=(k == 0), stop=(k == NZ - 1))
                pe.wait_ge(S("sq_ready"), t + 1)
                for k in range(NZ):
                    m = pe.matmul(bank[7][:, D:D + 1], sq[:, p, k, :], ones[:, 0:1], start=(k == 0), stop=(k == NZ - 1))
                m.then_inc(S("out_mm"), 1)

            turn(0, 0, False)
            segments(0, 0, False)
            turn(1, 1, True)
            segments(1, 1, True)
            mix(0, 0, False)

            def pe_step(t, p, wait=True):
                turn(t + 1, 1 - p, True)
                segments(t + 1, 1 - p, True)
                transpose_y(t - 1, 1 - p, wait)
                mix(t, p, True)
                project_out(t - 1, 1 - p)
            pe_step(1, 1, False)
            pe_step(2, 0)
            with pe.Fori(1, NT // 2 - 1) as i:
                pe_step(2 * i + 1, 1)
                pe_step(2 * i + 2, 0)
            transpose_y(NT - 2, 0, True)
            mix(NT - 1, 1, True)
            project_out(NT - 2, 0)
            transpose_y(NT - 1, 1, True)
            project_out(NT - 1, 1)
            with pe.Fori(0, NT // 2) as i:
                for p in range(2):
                    t = 2 * i + p
                    pe.wait_ge(S("y_st_ready"), t + 1)
                    if p == 0:
                        pe.wait_ge(S("yT_ready"), 2 * i)
                    for k in range(KD):
                        m = pe.transpose(bank[p][:, k * P:(k + 1) * P], y_st[:, p, k * P:(k + 1) * P], ident[:, :])
                    m.then_inc(S("y_st_transposed"), 1)
            pe.wait_ge(S("yT_ready"), NT)
            pe.wait_ge(dve_once, at("w2b_ready"))
            with pe.Fori(0, NBLK // 2) as i:
                for p in range(2):
                    blk = 2 * i + p
                    if p == 0:
                        pe.wait_ge(S("hid_ready"), 2 * i)
                    for k in range(KD):
                        m = pe.matmul(bank[2 + 4 * p][0:SD, :], scorer_w1[:, k, :], featT[:, k, ds(blk * BLK, BLK)],
                                      start=(k == 0), stop=(k == KD - 1))
                    m.then_inc(S("hid_mm"), 1)
                for p in range(2):
                    blk = 2 * i + p
                    pe.wait_ge(S("hid_ready"), blk + 1)
                    pe.wait_ge(S("score_tanh"), blk)
                    pe.matmul(bank[3][:, :], scorer_w2b[:, :], hid[0:SD, p, :], start=True, stop=True).then_inc(S("score_mm"), 1)
            pe.wait_ge(S("s_col_ready"), B)
            pe.wait_ge(dve_once, at("cols_set"))
            for b in range(B):
                for k in range(TB - 1):
                    pe.wait_ge(S("rank_counted"), 2 * (b * TB + k) + 1)
                    for j in range(k + 1, TB):
                        m = pe.matmul(bank[7][:, b * TB + j:b * TB + j + 1], greater[:, k % 2, j * P:(j + 1) * P], ones_bf[:, 0:1],
                                      start=(k == 0 and j == 1), stop=(k == j - 1), skip_group_check=True)
                    m.then_inc(S("rank_cols"), 1)
            pe.matmul(bank[6][:, 0:NT], ones[:, :], s_col, start=True, stop=True).then_inc(S("mean_mm"), 1)
            pe.wait_ge(S("y_tok_ready"), NT)
            pe.wait_ge(dve_once, at("mean_ready_1"))
            for b in range(B):
                pe.wait_ge(S("onehot_ready"), b + 1)
                for k in range(TB):
                    pe.matmul(mem_bank[b][1][0:POOL, 0:D], onehot[:, b * TB + k, :], y_tok[:, b * TB + k, :], start=(k == 0), stop=(k == TB - 1))
                for k in range(TB):
                    m = pe.matmul(mem_bank[b][2][:, 0:POOL], ones[:, :], onehot[:, b * TB + k, :], start=(k == 0), stop=(k == TB - 1))
                m.then_inc(S("select_mm"), 1)
            pe.wait_ge(pool_once, at("masks_set_3"))
            pe.wait_ge(S("mem_w_loaded"), 16 * 7)
            for b in range(B):
                pe.wait_ge(S("pool_tok_ready"), b + 1)
                for k in range(KD):
                    m = pe.transpose(mem_bank[b][0][:, k * POOL:(k + 1) * POOL], pool_tok[0:POOL, b, k * P:(k + 1) * P], ident[0:POOL, 0:POOL])
                m.then_inc(S("pool_tok_turned"), 1)
            for b in range(B):
                pe.wait_ge(S("pool_tokT_ready"), b + 1)
                for k in range(KD):
                    m = pe.matmul(mem_bank[b][1][0:SD, 0:POOL], summ_w[:, k, :], pool_tokT[:, b, k, :], start=(k == 0), stop=(k == KD - 1))
                m.then_inc(S("pool_mm"), 1)
            for b in range(B):
                pe.wait_ge(S("poolT_ready"), b + 1)
                pe.matmul(mem_bank[b][0][0:SD, 0:POOL], mem_k_w[:, :], poolT[0:SD, b, :], start=True, stop=True).then_inc(S("key_mm"), 1)
                pe.wait_ge(S("vbias_ready"), b + 1)
                pe.matmul(mem_bank[b][2][0:POOL, 0:D], poolT[0:SD, b, :], mem_v_w[:, :], start=True, stop=True).then_inc(S("val_mm"), 1)

            def query(n):
                for k in range(KD):
                    m = pe.matmul(bank[0][0:SD, :], mem_q_w[:, k, :], featT[:, k, ds(n * BLK, BLK)], start=(k == 0), stop=(k == KD - 1))
                m.then_inc(S("q_mem_mm"), 1)

            def logits_of(n):
                pe.wait_ge(S("q_mem_ready"), n + 1)
                b = n // (T // BLK)
                for i in range(4):
                    m = pe.matmul(bank[1][:, i * 64:i * 64 + POOL], q_mem[0:SD, i * P:(i + 1) * P],
                                  keyT[0:SD, ds(b, 1), :].rearrange("p a n -> p (a n)"), start=True, stop=True)
                m.then_inc(S("logit_mm"), 1)

            def gate(n, m_, ks):
                for k in ks:
                    side = featT[:, k, ds(n * BLK, BLK)] if k < KD else retT[:, k - KD, :]
                    m = pe.matmul(bank[5 + m_][:, :], gate_w[:, k, m_ * P:(m_ + 1) * P], side, start=(k == 0), stop=(k == 2 * KD - 1))
                return m

            def retrieve(n, nxt=True):
                pe.wait_ge(S("attn_ready"), n + 1)
                gate(n, 0, range(KD))
                for i in range(4):
                    m = pe.transpose(bank[2][0:POOL, i * P:(i + 1) * P], logit[:, i, :], ident[:, :])
                m.then_inc(S("attn_turned"), 1)
                if nxt:
                    pe.wait_ge(S("x1_ready"), 2 * n)
                    query(n + 1)
                pe.wait_ge(S("attnT_ready"), n + 1)
                pe.wait_ge(S("val_now_ready"), n + 1)
                for m_ in range(KD):
                    pe.matmul(bank[3 + m_][:, :], val_now[0:POOL, m_ * P:(m_ + 1) * P], attnT[0:POOL, :], start=True, stop=True
                              ).then_inc(S("ret_mm"), 1)
                if nxt:
                    logits_of(n + 1)
                pe.wait_ge(S("retT_ready"), KD * n + KD)
                gate(n, 0, range(KD, 2 * KD)).then_inc(S("gate_mm"), 1)
                gate(n, 1, range(2 * KD)).then_inc(S("gate_mm"), 1)
                if not nxt:
                    pe.wait_ge(S("x1_ready"), 2 * n)
                for m_ in range(2):
                    pe.wait_ge(S("upd_ready"), KD * n + KD)
                    for i in range(2):
                        for k in range(KD):
                            m = pe.transpose(bank[7 * (1 - m_)][:, (2 * i + k) * P:(2 * i + k + 1) * P],
                                             upd[:, k, (2 * m_ + i) * P:(2 * m_ + i + 1) * P], ident[:, :])
                    m.then_inc(S("upd_turned"), 1)

            pe.wait_ge(S("keyT_ready"), B)
            pe.wait_ge(S("val_ready"), B)
            query(0)
            logits_of(0)
            with pe.Fori(0, NBLK - 1) as n:
                retrieve(n)
            retrieve(NBLK - 1, False)

            pe.wait_ge(S("x1_ready"), 2 * NBLK)
            with pe.Fori(0, NT // 2) as i:
                for p in range(2):
                    t = 2 * i + p
                    pe.wait_ge(S("ln2_ready"), t + 1)
                    if p == 0:
                        pe.wait_ge(S("hT_ready"), 2 * i)
                    for k in range(KD):
                        m = pe.transpose(bank[p][:, k * P:(k + 1) * P], ln_st[:, p, k * P:(k + 1) * P], ident[:, :])
                    m.then_inc(S("ln2_transposed"), 1)
            pe.wait_ge(S("x_w_loaded"), 16 * 9)
            pe.wait_ge(pool_once, at("bias_rows_cleared_2"))
            for n in range(2):
                m = pe.transpose(bank[2][:, n * NG:(n + 1) * NG], bias_rows[:, n, :, :].rearrange("g h c -> g (h c)"), ident[0:NG, 0:NG])
            m.then_inc(S("bias_turned"), 1)
            pe.wait_ge(S("pads_ready"), 4)
            pe.wait_ge(dve_once, at("mask_row_ready"))
            for b in range(B):
                for g in range(NG):
                    n = NG * b + g
                    if n >= 2:
                        pe.wait_ge(S("keys_ready"), n - 1)
                    for k in range(KD):
                        pe.matmul(bank[3 + n % 2][:, 0:LK], wk_pad[:, k, g * P:(g + 1) * P], ctxT[:, b, k, :], start=(k == 0), stop=False)
                    pe.matmul(bank[3 + n % 2][:, 0:LK], mask_sel[:, :], mask_row[:, b * LK:(b + 1) * LK], start=False, stop=True
                              ).then_inc(S("keys_mm"), 1)
                if b:
                    pe.wait_ge(S("v_main_ready"), b)
                    pe.wait_ge(S("v_tail_ready"), b)
                for dst, lhs, rows, done in ((bank[5], ctxT[:, b, :, 0:KM], KM, "val_main_mm"), (bank[6], tail_ctx[:, b, :, :], P, "val_tail_mm")):
                    for k in range(KD):
                        pe.matmul(dst[0:rows, 0:D], lhs[:, k, :], wv[:, k, :], start=(k == 0), stop=False)
                    pe.matmul(dst[0:rows, 0:D], ones[0:1, 0:rows], vb_row[:, :], start=False, stop=True).then_inc(S(done), 1)
            pe.wait_ge(S("hT_ready"), NT)
            pe.wait_ge(S("keys_ready"), B * NG)
            pe.wait_ge(S("v_main_ready"), B)
            pe.wait_ge(S("v_tail_ready"), B)

            keys_of = keys.rearrange("p b g n -> p (b g) n")
            vt_of = v_tail.rearrange("p b g n -> p (b g) n")
            vm_of = v_main.rearrange("p b h n -> p (b h) n")
            W = HD + 1

            def queries(t):
                for g in range(NG):
                    for k in range(KD):
                        m = pe.matmul(bank[5][:, g * P:(g + 1) * P], wq_pad[:, k, g * P:(g + 1) * P], featT[:, k, ds(t * P, P)],
                                      start=(k == 0), stop=(k == KD - 1))
                m.then_inc(S("q_mm"), 1)

            def scores(t, p, g, waits):
                if waits:
                    pe.wait_ge(S("shifted"), NG * t + g - 1)
                if g == 0:
                    pe.wait_ge(S("qT_ready"), t + 1)
                for j in range(2):
                    m = pe.matmul(pair[g % 2][:, j, 0:2 * LK], qT[:, p, g, :],
                                  keys_of[:, :, 2 * j * LK:(2 * j + 2) * LK][:, ds((t // TB) * NG + g, 1), :].rearrange("p a n -> p (a n)"),
                                  start=True, stop=True)
                m.then_inc(S("score_x_mm"), 1)

            def turn_probs(t, p, g, waits):
                if g < NG:
                    pe.wait_ge(S("prob_ready"), NG * t + g + 1)
                if waits or g >= 1:
                    pe.wait_ge(S("probT_ready"), (NG + 1) * t + (-1, 1, 0, 2, 3)[g])
                for h in range(GH):
                    if g < NG:
                        m = pe.transpose(bank[TURN_BANK[g]][0:KM, h * P:(h + 1) * P], prob_m[p][:, GH * g + h, :], ident[:, :])
                    else:
                        m = pe.transpose(bank[TURN_BANK[g]][:, h * P:(h + 1) * P],
                                         prob_t[p][:, GH * h:GH * (h + 1), :].rearrange("p h n -> p (h n)"), ident[:, :])
                m.then_inc(S("prob_turned"), 1)

            def weigh_main(t, p, g, waits):
                pe.wait_ge(S("probT_ready"), (NG + 1) * t + g + 1)
                if g == 0 and waits:
                    pe.wait_ge(S("head_o_ready"), t - 1)
                for h in range(GH):
                    hh = GH * g + h
                    m = pe.matmul(bank[6 + p][:, hh * W:(hh + 1) * W], probT[0:KM, hh, :],
                                  vm_of[0:KM, ds((t // TB) * XH + hh, 1), :].rearrange("p a n -> p (a n)"), start=(hh == 0), stop=False,
                                  skip_group_check=True)
                m.then_inc(S("pv_mm"), 1)

            def weigh_tail(t, p):
                pe.wait_ge(S("probT_ready"), (NG + 1) * (t + 1))
                for g in range(NG):
                    m = pe.matmul(bank[6 + p][:, g * GH * W:(g + 1) * GH * W], probT[:, XH + g, :],
                                  vt_of[:, ds((t // TB) * NG + g, 1), :].rearrange("p a n -> p (a n)"), start=False, stop=True,
                                  skip_group_check=True)
                m.then_inc(S("pv_mm"), 1)

            def tile_step(t, p, now=True, before=True, before2=True, score_waits=True, turn_waits=True, pv_waits=True, nxt=True):
                for g in range(NG):
                    if now:
                        scores(t, p, g, score_waits or g > 1)
                    if nxt and g == 1:
                        if before and turn_waits:
                            pe.wait_ge(S("probT_ready"), (NG + 1) * (t - 1))
                        queries(t + 1)
                    if before:
                        if nxt and g == 2:
                            pe.wait_ge(S("qT_ready"), t + 2)
                        turn_probs(t - 1, 1 - p, g, turn_waits)
                    if before2 and g == 0:
                        weigh_main(t - 2, p, NG - 1, pv_waits)
                        weigh_tail(t - 2, p)
                    if before and g:
                        weigh_main(t - 1, 1 - p, g - 1, pv_waits)
                if before:
                    turn_probs(t - 1, 1 - p, NG, turn_waits)
            queries(0)
            pe.wait_ge(S("qT_ready"), 1)
            tile_step(0, 0, before=False, before2=False, score_waits=False)
            pe.wait_ge(S("qT_ready"), 2)
            tile_step(1, 1, before2=False, turn_waits=False, pv_waits=False)
            tile_step(2, 0, pv_waits=False)
            tile_step(3, 1)
            with pe.Fori(2, NT // 2 - 1) as i:
                for p in range(2):
                    tile_step(2 * i + p, p)
            tile_step(NT - 2, 0)
            tile_step(NT - 1, 1, nxt=False)
            tile_step(NT, 0, now=False, nxt=False)
            weigh_main(NT - 1, 1, NG - 1, True)
            weigh_tail(NT - 1, 1)

            pe.wait_ge(S("head_o_ready"), NT)
            pe.wait_ge(S("route_w_loaded"), 16 * 3)

            def turn_group(j):
                for q in range(GT):
                    pe.wait_ge(S("x3_ready"), GT * j + q + 1)
                    if j >= 2 and q == 0:
                        pe.wait_ge(S("x3T_ready"), 2 * (j - 1))
                    for k in range(KD):
                        m = pe.transpose(bank[2 * (j % 2) + q // 2][:, (q % 2) * D + k * P:(q % 2) * D + (k + 1) * P],
                                         st4[:, q, k * P:(k + 1) * P], ident[:, :])
                    if q % 2:
                        m.then_inc(S("x3_turned"), 1)

            def route_group(j):
                pe.wait_ge(S("x3T_ready"), 2 * j + 2)
                if j >= 2:
                    pe.wait_ge(S("logits_ready"), j - 1)
                for q in range(GT):
                    for k in range(KD):
                        m = pe.matmul(bank[4 + j % 2][:, q * NE:(q + 1) * NE], x3T[j % 2][:, q, k, :], w_route[:, k, :],
                                      start=(k == 0), stop=(k == KD - 1))
                m.then_inc(S("route_mm"), 1)
            turn_group(0)
            for j in range(1, NT // GT):
                turn_group(j)
                route_group(j - 1)
            route_group(NT // GT - 1)
            pe.wait_ge(S("hot_ready"), 1)
            hot_flat = hot.rearrange("p t e -> p (t e)")
            pe.matmul(bank[4][:, 0:NT * NE], tri_le[:, :], hot_flat, start=True, stop=True).then_inc(S("count_mm"), 1)
            pe.matmul(bank[5][:, 0:NT * NE], ones[:, :], hot_flat, start=True, stop=True).then_inc(S("count_mm"), 1)
            pe.wait_ge(dve_once, at("block_expert_ready"))

            def turn_rows(n, p):
                pe.wait_ge(S(f"xs_loaded{p}"), 8 * (n - p) + 16)
                pe.wait_ge(S("xsT_ready"), n)
                for k in range(KD):
                    m = pe.transpose(bank[6][:, k * P:(k + 1) * P], xs[:, p, k * P:(k + 1) * P], ident[:, :])
                m.then_inc(S("xs_turned"), 1)

            def up(n, p):
                e = pe.value_load(expert_i[0:1, ds(n, 1)], min_val=0, max_val=NE - 1)
                pe.wait_ge(S("xsT_ready"), n + 1)
                pe.wait_ge(S("h_kept"), 2 * n)
                for f in range(2):
                    for k in range(KD):
                        m = pe.matmul(bank[f][:, :], xsT[:, p, k, :], w1_of[:, ds(e * KD + k, 1), f * 512:(f + 1) * 512].rearrange("p a n -> p (a n)"),
                                      start=(k == 0), stop=(k == KD - 1))
                    m.then_inc(S("up_mm"), 1)

            def turn_hidden(n):
                for half in range(2):
                    pe.wait_ge(S("h_kept"), 2 * n + half + 1)
                    pe.wait_ge(S("hT_half_a" if half == 0 else "hT_half_b"), n)
                    for f in range(4):
                        m = pe.transpose(bank[2 + half][:, f * P:(f + 1) * P], hid_e[:, (4 * half + f) * P:(4 * half + f + 1) * P], ident[:, :])
                    m.then_inc(S("h_turned"), 1)

            def down(n):
                e = pe.value_load(expert_i[0:1, ds(n, 1)], min_val=0, max_val=NE - 1)
                pe.wait_ge(S("yo_ready"), n)
                for f in range(NFF):
                    if f % 4 == 0:
                        pe.wait_ge(S("hT_half_a" if f == 0 else "hT_half_b"), n + 1)
                    m = pe.matmul(bank[4][:, 0:D], hidT[:, f, :], w2_of[:, ds(e * NFF + f, 1), :].rearrange("p a n -> p (a n)"),
                                  start=(f == 0), stop=(f == NFF - 1))
                m.then_inc(S("down_mm"), 1)

            w1_of = w1.rearrange("p e k f -> p (e k) f")
            w2_of = w2.rearrange("p e f d -> p (e f) d")
            pe.wait_ge(S("w1_loaded"), 16 * NE)
            turn_rows(0, 0)
            up(0, 0)
            pe.wait_ge(S("w2_loaded"), 16 * 2 * NE)
            turn_rows(1, 1)

            def step(n, p):
                turn_hidden(n)
                up(n + 1, 1 - p)
                turn_rows(n + 2, p)
                down(n)
            with pe.Fori(0, NB // 2 - 1) as i:
                step(2 * i, 0)
                step(2 * i + 1, 1)
            step(NB - 3, 0)
            turn_hidden(NB - 2)
            up(NB - 1, 0)
            down(NB - 2)
            turn_hidden(NB - 1)
            down(NB - 1)


def layouts(inputs):
    g = {k: np.asarray(v) for k, v in inputs.items()}

    def c(v, *axes):
        return np.ascontiguousarray(v.transpose(*axes) if axes else v)

    def cols(v, *shape):
        return c(v.reshape(-1, P, *shape), 1, 0, *range(2, 2 + len(shape)))
    return {
        "x": c(g["x"]), "ctxT": c(g["ctx_1024"], 0, 2, 1), "mask": c(g["mask_BxS2_ik0"]),
        "attn_norm_w": cols(g["L0_attn_norm_w"]), "attn_in_wT": c(g["L0_attn_in_w"], 1, 0),
        "attn_conv_w": cols(g["L0_attn_conv_w"], TAPS), "attn_conv_b": cols(g["L0_attn_conv_b"]),
        "attn_dt_bias": c(g["L0_attn_dt_bias"]), "attn_A_log": c(g["L0_attn_A_log"]),
        "attn_D_param": c(g["L0_attn_D_param"]), "attn_gnorm_w": cols(g["L0_attn_gnorm_w"]),
        "attn_out_wT": c(g["L0_attn_out_w"], 1, 0), "scorer_w1T": c(g["L0_attn_scorer_w1"], 1, 0),
        "scorer_w2T": c(g["L0_attn_scorer_w2"], 1, 0), "summ_wT": c(g["L0_attn_summ_w"], 1, 0),
        "mem_q_wT": c(g["L0_attn_q_w"], 1, 0), "mem_k_wT": c(g["L0_attn_k_w"], 1, 0),
        "mem_v_wT": c(g["L0_attn_v_w"], 1, 0), "gate_wT": c(g["L0_attn_gate_w"], 1, 0),
        "q_w": c(g["L0_xattn_q_w"], 1, 0), "q_b": c(g["L0_xattn_q_b"]), "k_w": c(g["L0_xattn_k_w"], 1, 0),
        "k_b": c(g["L0_xattn_k_b"]), "v_w": c(g["L0_xattn_v_w"], 1, 0), "v_b": c(g["L0_xattn_v_b"]),
        "WrT": c(g["L0_ffn_Wr"], 1, 0), "br": c(g["L0_ffn_br"]),
        "W1T": c(g["L0_ffn_W1"], 0, 2, 1), "b1": c(g["L0_ffn_b1"].reshape(NE * NFF, P), 1, 0),
        "W2T": c(g["L0_ffn_W2"], 0, 2, 1), "b2": c(g["L0_ffn_b2"]),
    }


def kernel(**inputs):
    import concourse.bacc as bacc
    from concourse.bass_utils import run_bass_kernel_spmd

    nc = bacc.Bacc("TRN2", target_bir_lowering=False, num_devices=1)
    arrays = layouts(inputs)
    dram = {n: nc.dram_tensor(n, v.shape, mybir.dt.from_np(v.dtype), kind="ExternalInput").ap() for n, v in arrays.items()}
    out = nc.dram_tensor("out", (B, T, D), F32, kind="ExternalOutput").ap()
    build(nc, dram, out)
    return run_bass_kernel_spmd(nc, [arrays], core_ids=[0]).results[0]["out"]
```

```python
from contextlib import ExitStack

import numpy as np

import concourse.bass as bass
from concourse import mybir

F32 = mybir.dt.float32
I32 = mybir.dt.int32
BF16 = mybir.dt.bfloat16
ALU = mybir.AluOpType
ACT = mybir.ActivationFunctionType
AX = mybir.AxisListType.X
ds = bass.ds

P = 128
EPS = 1e-5
NEG = -1e30

B, T, D = 2, 1024, 256
NT = B * T // P
TB = T // P
KD = D // P
DI, NS, H, HP = 512, 128, 8, 64
TAPS = 4
NZ, NX = DI // P, (DI + 2 * NS) // P
BLK = 512
NBLK = B * T // BLK
POOL, SD = 50, 64
LK, XH, HD = 154, 16, 16
KT = 32
KM = LK - KT
GH, NG = 4, 4
NE, FF = 8, 1024
NFF = FF // P
NB = NT + NE - 1
ROW = 2 * D + 1

DVE_EVENTS = (
    "eps_set", "ln_var", "rstd_1", "rstd_2", "rms_var", "rstd_3", "rstd_4", "dt_steps_1", 
    "dt_steps_2", "dt_abs", "dt_sum", "dt_ready", "tot_kept", "wend_diff", "first_cleared_1", 
    "first_cleared_2", "decay_ready", "gn_rstd", "w2b_ready", "pos_ready", "cols_set", "valid_ready", 
    "rank_sum_1", "rank_sum_2", "rank_sum_3", "mean_ready_1", "mean_ready_2", "ln2_var", 
    "mask_row_ready", "bias_cols_ready", "ln2_rstd", "ln3_var", "ln3_rstd", "iotas_ready", 
    "block_expert_ready",
)
ACT_EVENTS = (
    "ln_sd", "rms_sd", "dt_e", "a_exp", "dt_ln", "ecum_exp", "dec_exp", "wend_exp", "gn_sd", "ln2_sd", 
    "ln3_sd",
)
POOL_EVENTS = (
    "ones_set", "mask_init", "masks_set_1", "masks_set_2", "masks_set_3", "state_set", "pos_set", 
    "bias_rows_zero_1", "bias_rows_cleared_1", "bias_rows_zero_2", "bias_rows_cleared_2", 
    "empty_ready_1", "empty_ready_2", "counters_set",
)
PE_EVENTS = (
    "dt_mm", "cum_mm_1", "cum_mm_2", "mean_mm", "bias_turned", "count_mm_1", "count_mm_2",
)


def events_of(name):
    return next(events for events in (DVE_EVENTS, ACT_EVENTS, POOL_EVENTS, PE_EVENTS) if name in events)


def at(name):
    return events_of(name).index(name) + 1


def build(nc, a, out):
    x_flat = a["x"].rearrange("b t d -> (b t) d")
    out_flat = out.rearrange("b t d -> (b t) d")

    with ExitStack() as ctx:
        def sb(name, shape, dt=F32):
            return ctx.enter_context(nc.sbuf_tensor(name, shape, dt))

        names = {}

        def sem(name):
            if name not in names:
                names[name] = ctx.enter_context(nc.semaphore(name))
            return names[name]

        dve_once, act_once, pool_once, pe_once = sem("dve_once"), sem("act_once"), sem("pool_once"), sem("pe_once")
        met = []

        def reached(name):
            met.append(name)
            events = events_of(name)
            assert [m for m in met if m in events] == list(events[:at(name)])
            return 1

        pair = [ctx.enter_context(nc.psum_tensor(f"pair{i}", [P, 2, 512], F32)) for i in range(2)]
        bank = [pair[i // 2][:, i % 2, :] for i in range(4)]
        bank += [ctx.enter_context(nc.psum_tensor(f"bank{i}", [P, 512], F32)) for i in range(4, 8)]

        GT = 4
        xres = sb("xres", [P, NT, D])
        featT = sb("featT", [P, KD, B * T])
        ybuf = sb("ybuf", [P, NT * D])
        arena = sb("arena", [P, 2 * NE * KD * FF])
        y_tok = ybuf[:, :].rearrange("p (t d) -> p t d", t=NT)
        IN_W = 2 * DI + 2 * NS + H
        w_in = ybuf[:, 0:KD * IN_W].rearrange("p (k n) -> p k n", k=KD)

        place = [0]

        def cut(shape):
            n = int(np.prod(shape))
            v = arena[:, place[0]:place[0] + n]
            place[0] += n
            if len(shape) == 2:
                v = v.rearrange("p (a b) -> p a b", a=shape[0])
            if len(shape) == 3:
                v = v.rearrange("p (a b c) -> p a b c", a=shape[0], b=shape[1])
            return v

        NXP = 4
        xbcT = cut([NX, B * T])
        zsT = cut([NZ, B * T])
        work0 = place[0]
        raw = cut([NX, TAPS - 1 + BLK])
        conv = cut([NX, BLK])
        tanh_c = cut([NX, BLK])
        tanh_z = cut([2, BLK])
        place[0] = work0
        xn = cut([GT, D])
        place[0] = work0
        xbc = cut([2, NX, P])
        seg = cut([2, H, P])
        lmat = cut([2, H, P])
        gmat = cut([2, P])
        b_tok = cut([2, P])
        xdt = cut([2, DI])
        xend = cut([2, DI])
        xskip = cut([2, DI])
        state = cut([DI])
        y_in = cut([2, DI])
        gated = cut([2, NZ, P])
        sq = featT[:, 0, 0:2 * NZ * P].rearrange("p (a b c) -> p a b c", a=2, b=NZ)
        assert place[0] <= 2 * NE * KD * FF

        ident = sb("ident", [P, P])
        ones = sb("ones", [P, P])
        tri_le = sb("tri_le", [P, P])
        tri_gt = sb("tri_gt", [P, P])
        w_out = sb("w_out", [P, NZ, D])
        norm_w = sb("norm_w", [P, KD])
        gnorm_w = sb("gnorm_w", [P, NZ])
        conv_w = sb("conv_w", [P, NX, TAPS])
        conv_b = sb("conv_b", [P, NX])
        dt_bias = sb("dt_bias", [P, H])
        a_log = sb("a_log", [P, H])
        d_skip = sb("d_skip", [P, H])
        stats = sb("stats", [P, NT, 6])
        mv = sb("mv", [P, NT, 2])
        nrm = sb("nrm", [P, 6, NT])
        dts = sb("dts", [P, 8, NT * H])
        ssq = sb("ssq", [P, 4, NT])
        eps_col = sb("eps_col", [P, 1])
        dt_raw, dt_neg, dt_pos, dt_exp = (dts[:, i, :] for i in range(4))
        dt_v, dta, ecum, dec = (dts[:, i, :] for i in range(4, 8))
        wend = dt_raw
        tot = dt_neg

        def th(v):
            return v.rearrange("p (t h) -> p t h", h=H)

        def heads(v, n):
            return v.unsqueeze(2).broadcast_to([P, H, n])

        w1 = arena[:, 0:NE * KD * FF].rearrange("p (e k f) -> p e k f", e=NE, k=KD)
        UP = NE * KD * FF
        place[0] = UP
        wq_dense = cut([KD, D])
        wk_dense = cut([KD, D])
        wv = cut([KD, D])
        ctxT = cut([B, KD, LK])
        after_loads = place[0]
        X_WORDS = 2 * KD * NG * P + B * KD * P + B * NG * GH * LK + 2 * B * XH * (HD + 1)
        sig = cut([B * T])
        hid = cut([2, BLK])
        junk = cut([T])
        greater = junk.bitcast(BF16).rearrange("p (a n) -> p a n", a=2)
        junk_eq = cut([2, P])
        ones_bf = cut([1]).bitcast(BF16)
        onehot = cut([NT, POOL])
        pool_tok = cut([B, D])
        pool_tokT = cut([B, KD, POOL])
        poolT = cut([B, POOL])
        place[0] = max(place[0], after_loads + X_WORDS)
        keyT = cut([B, POOL])
        val = cut([B, D])
        val_now = cut([D])
        q_now = cut([BLK])
        logit = cut([4, POOL])
        attnT = cut([BLK])
        retT = cut([KD, BLK])
        gate_t = cut([KD, BLK])
        upd = cut([KD, BLK])
        assert place[0] <= 2 * NE * KD * FF
        scorer_w1 = sb("scorer_w1", [P, KD, SD])
        scorer_w2 = sb("scorer_w2", [SD, 1])
        scorer_w2b = sb("scorer_w2b", [SD, P])
        summ_w = sb("summ_w", [P, KD, SD])
        mem_q_w = sb("mem_q_w", [P, KD, SD])
        mem_k_w = sb("mem_k_w", [SD, SD])
        mem_v_w = sb("mem_v_w", [SD, D])
        gate_w = sb("gate_w", [P, 2 * KD, D])
        prob_b = sb("prob_b", [P, XH * LK])
        q_mem = prob_b[0:SD, 0:B * T]
        mem_bank = [(bank[4], bank[5], bank[6]), (bank[1], bank[2], bank[7])]
        pos_i = sb("pos_i", [P, POOL], I32)
        pos = sb("pos", [P, POOL])
        tile_i = sb("tile_i", [P, NT], I32)
        cols = sb("cols", [P, 6, NT])
        s_col, n_earlier, n_gt, n_eq, rank, valid = (cols[:, i, :] for i in range(6))
        mean_s = sb("mean_s", [P, B])
        vbias = sb("vbias", [P, B, POOL])
        red = sb("red", [P, 3, 4])

        place[0] = after_loads
        wq_pad = cut([KD, NG * P])
        wk_pad = cut([KD, NG * P])
        tail_ctx = cut([B, KD, P])
        keys = cut([B, NG, GH * LK])
        v_main = cut([B, XH, HD + 1])
        v_tail = cut([B, NG, GH * (HD + 1)])
        assert place[0] == after_loads + X_WORDS
        qT = cut([2, NG, P])
        assert place[0] + XH * LK <= 2 * NE * KD * FF
        prob_a = cut([XH * LK])
        prob = (prob_a, prob_b[:, :])
        prob_m = [v[:, 0:XH * KM].rearrange("p (h n) -> p h n", h=XH) for v in prob]
        prob_t = [v[:, XH * KM:].rearrange("p (h n) -> p h n", h=XH) for v in prob]
        probT = ybuf[:, 0:(XH + NG) * P].rearrange("p (h n) -> p h n", h=XH + NG)
        st4 = ybuf[:, (XH + NG) * P:(XH + NG) * P + 4 * D].rearrange("p (a d) -> p a d", a=4)
        head_o = ybuf[:, (XH + NG) * P + 2 * D:(XH + NG) * P + 4 * D].rearrange("p (a d) -> p a d", a=2)
        bias_rows = sb("bias_rows", [NG, 2, GH, 32])
        bias_cols = sb("bias_cols", [P, 2, NG])
        rows1 = w_out[0:1, :, :].rearrange("p k n -> p (k n)")
        mask_i = rows1[:, 0:B * LK].bitcast(I32)
        mask_row = rows1[:, B * LK:2 * B * LK]
        vb_row = rows1[:, 2 * B * LK:2 * B * LK + D]
        mask_sel = rows1[:, 2 * B * LK + D:2 * B * LK + D + P]
        xmax = sb("xmax", [P, 2, XH])
        xinv = sb("xinv", [P, 2, XH])
        TURN_BANK = (4, 4, 5, 4, 5)

        w2 = arena[:, NE * KD * FF:].rearrange("p (e f d) -> p e f d", e=NE, f=NFF)
        sorted_rows = nc.dram_tensor("sorted_rows", [NB * P, ROW], F32, kind="Internal").ap()
        NOWHERE = 2 * B * T

        def parts(v, *shapes):
            at_, out_ = 0, []
            for shape in shapes:
                n = int(np.prod(shape))
                w = v[:, at_:at_ + n]
                if len(shape) == 2:
                    w = w.rearrange("p (a b) -> p a b", a=shape[0])
                if len(shape) == 3:
                    w = w.rearrange("p (a b c) -> p a b c", a=shape[0], b=shape[1])
                out_.append(w)
                at_ += n
            return out_
        g_flat = gate_w[:, :, :].rearrange("p k n -> p (k n)")
        b1_cols, w_route, br_row, empty = parts(g_flat, [NE * NFF], [KD, NE], [NE], [ROW])
        ints = g_flat[:, 640:].bitcast(I32)
        token_i, slot_i, slot_now, expert_i, desc_i, thr_i, blk_i = parts(ints, [NT], [NT], [GT], [NB], [NE], [NT], [NB])
        logits, hot, slot_t, before, blocks_c, expert_c, desc, thr, blk_n, first_blk, best, slot_f, expert_f = parts(
            w_out[:, :, :].rearrange("p k n -> p (k n)"), [NT, NE], [NT, NE], [NT, NE], [NT + 1, NE], [NE, NT], [NB, NE],
            [NE], [NT], [NB], [NE + 1], [NT], [NT], [NB])
        (rows,) = parts(ybuf[:, :], [GT, ROW])
        (xsT,) = parts(ybuf[:, (XH + NG) * P + 4 * D:], [2, KD, P])
        x3T = [ybuf[:, i * GT * D:(i + 1) * GT * D].rearrange("p (t k n) -> p t k n", t=GT, k=KD) for i in range(2)]
        hid_e, hidT = parts(prob_b[:, :], [FF], [NFF, P])
        b2_rows, xs, rest, yo = parts(featT[:, :, :].rearrange("p k n -> p (k n)"), [NE, D], [2, D], [2, D + 1], [2, D])

        block = ctx.enter_context(nc.Block())
        S = sem
        N_SMALL = 8

        @block.sync
        def _(sp):
            for q in range(4):
                sp.dma_start(xres[:, 4 * q:4 * q + 4, :],
                             x_flat[q * BLK:(q + 1) * BLK, :].rearrange("(t p) d -> p t d", p=P)
                             ).then_inc(S(f"x_loaded{q}"), 16)
            sp.dma_start(w_in, a["attn_in_wT"].rearrange("(k p) n -> p k n", p=P)).then_inc(S("w_loaded"), 16)
            sp.dma_start(w_out[:, :, :], a["attn_out_wT"].rearrange("(k p) n -> p k n", p=P)
                         ).then_inc(S("w_loaded"), 16)

            sp.wait_ge(S("conv_done"), NXP * NBLK)
            sp.wait_ge(S("conv_done_dve"), (NX - NXP) * NBLK)

            def load_chunk(t, p, wait):
                first, used = (sp.snap(t * P), sp.snap(t - 1)) if wait else (t * P, 0)
                if wait:
                    sp.wait_ge(S("inter_mm"), used)
                sp.dma_start(xbc[:, p, :, :], xbcT[:, :, ds(first, P)]).then_inc(S(f"chunk_loaded{p}"), 16)
            load_chunk(0, 0, False)
            load_chunk(1, 1, False)
            with sp.Fori(1, NT // 2) as i:
                for p in range(2):
                    load_chunk(2 * i + p, p, True)

            for dst, src in ((scorer_w1[:, :, :], a["scorer_w1T"].rearrange("(k p) n -> p k n", p=P)),
                             (scorer_w2[:, :], a["scorer_w2T"]),
                             (summ_w[:, :, :], a["summ_wT"].rearrange("(k p) n -> p k n", p=P)),
                             (mem_q_w[:, :, :], a["mem_q_wT"].rearrange("(k p) n -> p k n", p=P)),
                             (mem_k_w[:, :], a["mem_k_wT"]),
                             (mem_v_w[:, :], a["mem_v_wT"]),
                             (gate_w[:, :, :], a["gate_wT"].rearrange("(k p) n -> p k n", p=P))):
                sp.dma_start(dst, src).then_inc(S("mem_w_loaded"), 16)
            sp.wait_ge(S("out_kept"), NT)
            sp.wait_ge(S("y_part"), 2 * NT)
            sp.wait_ge(S("state_added"), NT)

            for dst, src in ((wq_dense, a["q_w"].rearrange("(k p) n -> p k n", p=P)),
                             (wk_dense, a["k_w"].rearrange("(k p) n -> p k n", p=P)),
                             (wv, a["v_w"].rearrange("(k p) n -> p k n", p=P)),
                             (mask_i[:, :], a["mask"].rearrange("b k -> (b k)").unsqueeze(0)),
                             (vb_row[:, :], a["v_b"].unsqueeze(0))):
                sp.dma_start(dst, src).then_inc(S("x_w_loaded"), 16)
            for b in range(B):
                sp.dma_start(ctxT[:, b, :, :], a["ctxT"][b].rearrange("(k p) n -> p k n", p=P)).then_inc(S("x_w_loaded"), 16)
            sp.wait_ge(pool_once, at("bias_rows_cleared_2"))
            for n, name in enumerate(("q_b", "k_b")):
                sp.dma_start(bias_rows[:, n, :, 0:HD], a[name].rearrange("(g h d) -> g h d", g=NG, h=GH)).then_inc(S("x_w_loaded"), 16)
            for e in range(NE):
                sp.dma_start(w1[:, e, :, :], a["W1T"][e].rearrange("(k p) f -> p k f", p=P)).then_inc(S("w1_loaded"), 16)

            sp.wait_ge(S("gate_tanh"), 2 * NBLK)
            for dst, src in ((b1_cols, a["b1"]), (w_route, a["WrT"].rearrange("(k p) n -> p k n", p=P)),
                             (br_row, a["br"].partition_broadcast(P))):
                sp.dma_start(dst, src).then_inc(S("route_w_loaded"), 16)
            sp.wait_ge(pool_once, at("empty_ready_2"))
            sp.dma_start(sorted_rows.rearrange("(n p) r -> p n r", p=P), empty.unsqueeze(1).broadcast_to([P, NB, ROW])
                         ).then_inc(S("rows_emptied"), 16)
            sp.wait_ge(S("x2_ready"), NT)
            sp.wait_ge(S("prob_turned"), (NG + 1) * NT)
            for e in range(NE):
                sp.dma_start(w2[:, e, :, :], a["W2T"][e].rearrange("(f p) d -> p f d", p=P)).then_inc(S("w2_loaded"), 16)
            for e in range(NE):
                sp.dma_start(b2_rows[:, e, :], a["b2"][e].partition_broadcast(P)).then_inc(S("w2_loaded"), 16)
            for p in range(GT):
                sp.wait_ge(S(f"scattered{p}"), 16 * NT // GT)

            def load_xs(n, p, wait):
                first, used = (sp.snap(n * P), sp.snap(n - 1)) if wait else (n * P, 0)
                if wait:
                    sp.wait_ge(S("xs_turned"), used)
                sp.dma_start(xs[:, p, :], sorted_rows[ds(first, P), 0:D]).then_inc(S(f"xs_loaded{p}"), 16)

            def load_rest(n, p, wait):
                first, stored = (sp.snap(n * P), sp.snap(8 * (n - p))) if wait else (n * P, 0)
                if wait:
                    sp.wait_ge(S(f"out_stored{p}"), stored)
                sp.dma_start(rest[:, p, :], sorted_rows[ds(first, P), D:ROW]).then_inc(S(f"rest_loaded{p}"), 16)
            for n in range(2):
                load_xs(n, n, False)
                load_rest(n, n, False)
            sp.wait_ge(S("xs_turned"), 1)
            load_xs(2, 0, False)
            with sp.Fori(1, NB // 2) as i:
                for p in (1, 0):
                    n = 2 * i + 2 - p
                    load_xs(n, p, True)
                    load_rest(n - 1, 1 - p, True)
            load_rest(NB - 1, 0, True)

        @block.gpsimd
        def _(pool):
            pool.memset(ones[:, :], 1.0).then_inc(pool_once, reached("ones_set"))
            pool.memset(ident[:, :], 0.0).then_inc(pool_once, reached("mask_init"))
            pool.wait_ge(pool_once, at("ones_set"))
            pool.wait_ge(pool_once, at("mask_init"))
            pool.affine_select(out=ident[:, :], in_=ident[:, :], compare_op=ALU.not_equal, fill=1.0, base=0,
                               pattern=[[-1, P]], channel_multiplier=1).then_inc(pool_once, reached("masks_set_1"))
            pool.affine_select(out=tri_le[:, :], in_=ones[:, :], compare_op=ALU.is_ge, fill=0.0, base=0,
                               pattern=[[1, P]], channel_multiplier=-1).then_inc(pool_once, reached("masks_set_2"))
            pool.affine_select(out=tri_gt[:, :], in_=ones[:, :], compare_op=ALU.is_gt, fill=0.0, base=0,
                               pattern=[[-1, P]], channel_multiplier=1).then_inc(pool_once, reached("masks_set_3"))
            pool.wait_ge(S("res_cols"), 2)
            for t in range(NT):
                pool.wait_ge(S("xn_ready"), t + 1)
                pool.tensor_scalar(xres[:, t, :], xres[:, t, :], nrm[:, 1, t:t + 1], nrm[:, 2, t:t + 1], ALU.mult, ALU.subtract
                                   ).then_inc(S("res_added"), 1)
            with pool.Fori(0, NBLK) as blk:
                for f in range(NXP):
                    pool.wait_ge(S("tanh_c_ready"), NX * blk + f + 1)
                    pool.tensor_tensor(tanh_c[:, f, :], tanh_c[:, f, :], conv[:, f, :], ALU.mult).then_inc(S("silu_part"), 1)
                    pool.wait_ge(S("silu_part"), NXP * blk + f + 1)
                    pool.tensor_tensor(xbcT[:, f, ds(blk * BLK, BLK)], tanh_c[:, f, :], conv[:, f, :], ALU.add
                                       ).then_inc(S("conv_done"), 1)
            pool.wait_ge(dve_once, at("dt_ready"))
            pool.wait_ge(dve_once, at("decay_ready"))
            pool.wait_ge(S("conv_done"), NXP * NBLK)
            pool.wait_ge(S("conv_done_dve"), (NX - NXP) * NBLK)
            pool.memset(state, 0.0).then_inc(pool_once, reached("state_set"))

            def make_seg(t, p, wait):
                if wait:
                    pool.wait_ge(S("seg_mm"), t - 1)
                pool.tensor_tensor(seg[:, p, :, :], tri_le[:, :].unsqueeze(1).broadcast_to([P, H, P]),
                                   heads(dta[:, ds(t * H, H)], P), ALU.mult).then_inc(S("seg_ready"), 1)

            def make_m(t, p):
                pool.wait_ge(S("decay_mat"), t + 1)
                pool.wait_ge(S("g_ready"), t + 1)
                pool.tensor_tensor(lmat[:, p, :, :], lmat[:, p, :, :],
                                   gmat[:, p, :].unsqueeze(1).broadcast_to([P, H, P]), ALU.mult
                                   ).then_inc(S("m_ready"), 1)

            def decay_state(t):
                pool.wait_ge(S("inter_mm"), t + 1)
                pool.wait_ge(S("state_added"), t)
                sv = state.rearrange("p (h n) -> p h n", h=H)
                pool.tensor_tensor(sv, sv, heads(dec[:, ds(t * H, H)], HP), ALU.mult).then_inc(S("state_decayed"), 1)

            def sum_squares(t, p):
                pool.wait_ge(S("sq_ready"), t + 1)
                pool.tensor_tensor(sq[:, p, 0:2, :], sq[:, p, 0:2, :], sq[:, p, 2:4, :], ALU.add).then_inc(S("sq_part"), 1)
                pool.wait_ge(S("sq_part"), t + 1)
                pool.tensor_tensor(sq[:, p, 0, :], sq[:, p, 0, :], sq[:, p, 1, :], ALU.add).then_inc(S("sq_summed"), 1)

            pool.wait_ge(pool_once, at("state_set"))
            make_seg(0, 0, False)
            make_seg(1, 1, False)
            make_m(0, 0)

            def step(t, p, first=False):
                make_seg(t + 2, p, True)
                make_m(t + 1, 1 - p)
                decay_state(t)
                if not first:
                    sum_squares(t - 1, 1 - p)
            step(0, 0, True)
            step(1, 1)
            with pool.Fori(1, NT // 2 - 1) as i:
                step(2 * i, 0)
                step(2 * i + 1, 1)
            make_m(NT - 1, 1)
            decay_state(NT - 2)
            sum_squares(NT - 3, 1)
            decay_state(NT - 1)
            sum_squares(NT - 2, 0)
            sum_squares(NT - 1, 1)

            pool.iota(tile_i[:, :], pattern=[[0, B], [P, TB]], base=0, channel_multiplier=0)
            pool.iota(pos_i[:, :], pattern=[[1, POOL]], base=0, channel_multiplier=0).then_inc(pool_once, reached("pos_set"))
            with pool.Fori(0, NT // 2) as i:
                for p in range(2):
                    t = 2 * i + p
                    pool.wait_ge(S("y_tok_ready"), t + 1)
                    pool.tensor_tensor(xres[:, ds(t, 1), :].rearrange("p a d -> p (a d)"),
                                       xres[:, ds(t, 1), :].rearrange("p a d -> p (a d)"), y_tok[:, ds(t, 1), :].rearrange("p a d -> p (a d)"), ALU.add
                                       ).then_inc(S("res_y_added"), 1)

            pool.memset(bias_rows[:, :, :, :], 0.0).then_inc(pool_once, reached("bias_rows_zero_1"))
            pool.wait_ge(pool_once, at("bias_rows_zero_1"))
            pool.memset(bias_rows[:, 0, :, HD:HD + 1], 1.0).then_inc(pool_once, reached("bias_rows_cleared_1"))
            pool.memset(mask_sel[:, :], 0.0).then_inc(pool_once, reached("bias_rows_zero_2"))
            pool.wait_ge(pool_once, at("bias_rows_zero_2"))
            pool.memset(mask_sel[:, :].rearrange("o (h c) -> o h c", c=32)[:, :, HD:HD + 1], 1.0).then_inc(pool_once, reached("bias_rows_cleared_2"))
            pool.wait_ge(S("keyT_ready"), B)
            pool.wait_ge(S("val_ready"), B)
            pool.wait_ge(S("x_w_loaded"), 16 * 9)
            for pad, dense, n in ((wk_pad, wk_dense, 1), (wq_pad, wq_dense, 2)):
                pool.memset(pad, 0.0).then_inc(S("pads_zero"), 1)
                pool.wait_ge(S("pads_zero"), n)
                pool.tensor_copy(pad.rearrange("p k (h c) -> p (k h) c", c=32)[:, :, 0:HD],
                                 dense.rearrange("p k (h d) -> p (k h) d", d=HD)).then_inc(S("pads_ready"), 1)
            for b in range(B):
                pool.tensor_copy(tail_ctx[:, b, :, :].rearrange("p k (r c) -> p k r c", c=KT),
                                 ctxT[:, b, :, KM:LK].unsqueeze(2).broadcast_to([P, KD, GH, KT])).then_inc(S("pads_ready"), 1)
            pool.memset(v_tail, 0.0).then_inc(S("pads_zero"), 1)
            pool.memset(v_main, 1.0).then_inc(S("pads_zero"), 1)
            pool.memset(keys, 0.0).then_inc(S("pads_zero"), 1)
            pool.wait_ge(S("x1_ready"), 2 * NBLK)
            pool.wait_ge(S("gate_tanh"), 2 * NBLK)
            pool.wait_ge(S("x_w_loaded"), 16 * 9)
            pool.memset(empty, 0.0).then_inc(pool_once, reached("empty_ready_1"))
            pool.wait_ge(pool_once, at("empty_ready_1"))
            pool.memset(empty[:, ROW - 1:ROW].bitcast(I32), NOWHERE).then_inc(pool_once, reached("empty_ready_2"))
            pool.iota(token_i, pattern=[[P, NT]], base=0, channel_multiplier=1)
            pool.iota(desc_i, pattern=[[-1, NE]], base=NE, channel_multiplier=0)
            pool.iota(thr_i, pattern=[[P, NT]], base=0, channel_multiplier=0)
            pool.iota(blk_i, pattern=[[1, NB]], base=0, channel_multiplier=0).then_inc(pool_once, reached("counters_set"))
            with pool.Fori(0, NT // 2) as i:
                for p in range(2):
                    t = 2 * i + p
                    pool.wait_ge(S("head_o_ready"), t + 1)
                    pool.tensor_tensor(xres[:, ds(t, 1), :].rearrange("p a d -> p (a d)"),
                                       xres[:, ds(t, 1), :].rearrange("p a d -> p (a d)"), head_o[:, p, :], ALU.add
                                       ).then_inc(S("x2_ready"), 1)
            pool.wait_ge(S("rows_emptied"), 16)
            last_row, last_token = pool.to_reg(NB * P - 1), pool.to_reg(B * T - 1)
            with pool.Fori(0, NT // GT) as i:
                for p in range(GT):
                    pool.wait_ge(S("row_ready"), GT * i + p + 1)
                    pool.sem_inc(S("pool_turn"), 1)
                    pool.indirect_dma_start(out=sorted_rows, out_offset=bass.IndirectOffsetOnAxis(ap=slot_now[:, p:p + 1], axis=0),
                                            in_=rows[:, p, :], in_offset=None, bounds_check=last_row, oob_is_err=False
                                            ).then_inc(S(f"scattered{p}"), 16)

            def store(n, p):
                pool.wait_ge(S("yo_ready"), n + 1)
                pool.sem_inc(S("pool_turn"), 1)
                pool.indirect_dma_start(out=out_flat, out_offset=bass.IndirectOffsetOnAxis(ap=rest[:, p, D:D + 1].bitcast(I32), axis=0),
                                        in_=yo[:, p, :], in_offset=None, bounds_check=last_token, oob_is_err=False
                                        ).then_inc(S(f"out_stored{p}"), 16)
            with pool.Fori(0, NB // 2) as i:
                store(2 * i, 0)
                store(2 * i + 1, 1)
            store(NB - 1, 0)
            pool.wait_ge(S("out_stored0"), 16 * (NB // 2 + 1))
            pool.wait_ge(S("out_stored1"), 16 * (NB // 2))

        @block.scalar
        def _(act):
            for dst, src in ((norm_w[:, :], a["attn_norm_w"]),
                             (gnorm_w[:, :], a["attn_gnorm_w"]),
                             (conv_w[:, :, :], a["attn_conv_w"]),
                             (conv_b[:, :], a["attn_conv_b"]),
                             (dt_bias[:, :], a["attn_dt_bias"].partition_broadcast(P)),
                             (a_log[:, :], a["attn_A_log"].partition_broadcast(P)),
                             (d_skip[:, :], a["attn_D_param"].partition_broadcast(P))):
                act.dma_start(dst, src).then_inc(S("small_loaded"), 16)
            act.wait_ge(dve_once, at("eps_set"))
            act.wait_ge(dve_once, at("ln_var"))
            act.activation(nrm[:, 0, :], mv[:, :, 1], ACT.Sqrt, bias=eps_col[:, :]).then_inc(act_once, reached("ln_sd"))
            act.wait_ge(dve_once, at("rms_var"))
            act.activation(nrm[:, 2, :], nrm[:, 1, :], ACT.Sqrt, bias=eps_col[:, :]).then_inc(act_once, reached("rms_sd"))
            for n in range(NT // 2):
                act.wait_ge(S("xn_turned"), n + 1)
                act.activation(featT[:, :, 2 * n * P:(2 * n + 2) * P].rearrange("p k (t n) -> p t k n", t=2),
                               bank[n % 4][:, :].rearrange("p (t k n) -> p t k n", t=2, k=KD), ACT.Copy).then_inc(S("xnT_ready"), 1)
            act.wait_ge(dve_once, at("dt_abs"))
            act.activation(dt_exp, dt_neg, ACT.Exp).then_inc(act_once, reached("dt_e"))
            act.activation(a_log[:, :], a_log[:, :], ACT.Exp).then_inc(act_once, reached("a_exp"))
            act.wait_ge(act_once, at("dt_e"))
            act.activation(dt_exp, dt_exp, ACT.Ln, bias=1.0).then_inc(act_once, reached("dt_ln"))

            LAG = 4

            def tanh_conv(blk, f):
                act.wait_ge(S("conv_sum"), NX * blk + f + 1)
                act.activation(tanh_c[:, f, :], conv[:, f, :], ACT.Tanh).then_inc(S("tanh_c_ready"), 1)

            act.wait_ge(S("weights_ready"), 3 * KD + NZ + 2)
            with act.Fori(0, B) as b:
                with act.Fori(0, NBLK // B) as j:
                    blk = b * (NBLK // B) + j
                    for f in range(NZ):
                        act.wait_ge(S("proj_mm"), (NZ + NX) * blk + f + 1)
                        act.wait_ge(S("zs_ready"), NZ * blk + max(f - 1, 0))
                        act.activation(tanh_z[:, f % 2, :], bank[f % 5][:, :], ACT.Tanh).then_inc(S("tanh_z_ready"), 1)
                    for f in range(NX):
                        if f == 0:
                            act.wait_ge(S("raw_used"), NX * blk)
                            act.wait_ge(S("past_cleared"), b + 1)
                        act.wait_ge(S("proj_mm"), (NZ + NX) * blk + NZ + f + 1)
                        act.activation(raw[:, f, TAPS - 1:], bank[(NZ + f) % 5][:, :], ACT.Copy).then_inc(S("raw_ready"), 1)
                        if f == 0:
                            act.wait_ge(S("conv_done"), NXP * blk)
                            act.wait_ge(S("conv_done_dve"), (NX - NXP) * blk)
                        act.wait_ge(S("raw_ready"), NX * blk + f + 1)
                        act.activation(conv[:, f, :], raw[:, f, 0:BLK], ACT.Identity, bias=conv_b[:, f:f + 1],
                                       scale=conv_w[:, f, 0:1]).then_inc(S("tap0_ready"), 1)
                        if f >= LAG:
                            tanh_conv(blk, f - LAG)
                    for f in range(NX - LAG, NX):
                        tanh_conv(blk, f)
            act.wait_ge(pe_once, at("cum_mm_1"))
            act.activation(ecum, bank[0][:, 0:NT * H], ACT.Exp).then_inc(act_once, reached("ecum_exp"))
            act.wait_ge(pe_once, at("cum_mm_2"))
            act.activation(dec, bank[1][:, 0:NT * H], ACT.Exp).then_inc(act_once, reached("dec_exp"))
            act.wait_ge(dve_once, at("wend_diff"))
            act.activation(wend, wend, ACT.Exp).then_inc(act_once, reached("wend_exp"))

            def decay_matrix(t, p, wait):
                act.wait_ge(S("seg_mm"), t + 1)
                if wait:
                    act.wait_ge(S("intra_mm"), t - 1)
                for q in range(2):
                    i = act.activation(lmat[:, p, 4 * q:4 * q + 4, :], bank[2 + q][:, :].rearrange("p (h n) -> p h n", h=4), ACT.Exp)
                i.then_inc(S("decay_mat"), 1)

            def square(t, p):
                act.wait_ge(S("gated_ready"), t + 1)
                act.activation(sq[:, p, :, :], gated[:, p, :, :], ACT.Square).then_inc(S("sq_ready"), 1)

            def keep_out(t, first=False):
                act.wait_ge(S("out_mm"), t + 1)
                i = act.activation(y_tok[:, ds(t, 1), :].rearrange("p a d -> p (a d)"), bank[7][:, 0:D], ACT.Copy)
                if not first:
                    i = act.activation(ssq[:, 0, ds(t - 1, 1)], bank[7][:, D:D + 1], ACT.Copy)
                i.then_inc(S("out_kept"), 1)

            act.wait_ge(S("conv_done"), NXP * NBLK)
            act.wait_ge(S("conv_done_dve"), (NX - NXP) * NBLK)
            decay_matrix(0, 0, False)
            decay_matrix(1, 1, False)

            def act_step(t, p, first=False):
                square(t - 1, 1 - p)
                decay_matrix(t + 1, 1 - p, True)
                keep_out(t - 1, first)
            act_step(1, 1, True)
            act_step(2, 0)
            with act.Fori(1, NT // 2 - 1) as i:
                act_step(2 * i + 1, 1)
                act_step(2 * i + 2, 0)
            square(NT - 2, 0)
            keep_out(NT - 2)
            square(NT - 1, 1)
            keep_out(NT - 1)
            act.wait_ge(S("out_mm"), NT + 1)
            act.activation(ssq[:, 0, NT - 1:NT], bank[7][:, D:D + 1], ACT.Copy).then_inc(S("out_kept"), 1)

            act.wait_ge(S("out_kept"), NT + 1)
            act.activation(ssq[:, 1, :], ssq[:, 0, :], ACT.Sqrt, bias=eps_col[:, :], scale=1.0 / DI).then_inc(act_once, reached("gn_sd"))
            def tanh_scores(blk):
                act.wait_ge(S("score_mm"), blk + 1)
                act.activation(sig[:, blk * BLK:(blk + 1) * BLK], bank[6 + blk % 2][:, :], ACT.Tanh, scale=0.5).then_inc(S("score_tanh"), 1)

            for n in range(NT // 2):
                act.wait_ge(S("y_turned"), n + 1)
                act.activation(featT[:, :, 2 * n * P:(2 * n + 2) * P].rearrange("p k (t n) -> p t k n", t=2),
                               bank[n % 4][:, :].rearrange("p (t k n) -> p t k n", t=2, k=KD), ACT.Copy).then_inc(S("yT_ready"), 1)
                if n % 2 and n >= 5:
                    tanh_scores(n // 2 - 2)
            tanh_scores(NBLK - 2)
            tanh_scores(NBLK - 1)
            for n in range(NBLK):
                act.wait_ge(S("q_mem_mm"), n + 1)
                act.activation(q_mem[:, n * BLK:(n + 1) * BLK], bank[n][0:SD, :], ACT.Copy).then_inc(S("q_mem_ready"), 1)
            for b in range(B):
                act.wait_ge(S("pool_tok_turned"), b + 1)
                act.activation(pool_tokT[:, b, :, :], mem_bank[b][0][:, 0:KD * POOL].rearrange("p (k n) -> p k n", k=KD), ACT.Copy
                               ).then_inc(S("pool_tokT_ready"), 1)
            for b in range(B):
                act.wait_ge(S("pool_mm"), b + 1)
                act.activation(poolT[0:SD, b, :], mem_bank[b][1][0:SD, 0:POOL], ACT.Copy).then_inc(S("poolT_ready"), 1)
            for b in range(B):
                act.wait_ge(S("key_mm"), b + 1)
                act.activation(keyT[0:SD, b, :], mem_bank[b][0][0:SD, 0:POOL], ACT.Copy, scale=0.25).then_inc(S("keyT_ready"), 1)

            def stage_q(n, first=False):
                if not first:
                    act.wait_ge(S("logit_mm"), n)
                act.activation(q_now[0:SD, :], q_mem[:, ds(n * BLK, BLK)], ACT.Copy).then_inc(S("q_now_ready"), 1)

            act.wait_ge(S("q_mem_ready"), NBLK)

            def exp_logits(n):
                act.wait_ge(S("logit_shifted"), n + 1)
                act.activation(logit, logit, ACT.Exp).then_inc(S("logit_exp"), 1)

            def keep_retrieved(n):
                act.wait_ge(S("attn_turned"), n + 1)
                act.activation(attnT[0:POOL, :], bank[2][0:POOL, :], ACT.Copy).then_inc(S("attnT_ready"), 1)
                for m in range(KD):
                    act.wait_ge(S("ret_mm"), KD * n + m + 1)
                    act.activation(retT[:, m, :], bank[3 + m][:, :], ACT.Copy).then_inc(S("retT_ready"), 1)

            def gate_halves(n):
                for m in range(KD):
                    act.wait_ge(S("gate_mm"), KD * n + m + 1)
                    act.activation(gate_t[:, m, :], bank[5 + m][:, :], ACT.Tanh, scale=0.5).then_inc(S("gate_tanh"), 1)

            stage_q(0, True)
            exp_logits(0)
            with act.Fori(0, NBLK - 1) as n:
                keep_retrieved(n)
                stage_q(n + 1)
                exp_logits(n + 1)
                gate_halves(n)
            keep_retrieved(NBLK - 1)
            gate_halves(NBLK - 1)

            act.wait_ge(dve_once, at("ln2_var"))
            act.activation(nrm[:, 0, :], mv[:, :, 1], ACT.Sqrt, bias=eps_col[:, :]).then_inc(act_once, reached("ln2_sd"))
            act.wait_ge(dve_once, at("bias_cols_ready"))
            act.wait_ge(S("pads_zero"), 5)
            for b in range(B):
                for g in range(NG):
                    n = NG * b + g
                    act.wait_ge(S("keys_mm"), n + 1)
                    for h in range(GH):
                        r = slice(32 * h, 32 * h + 32)
                        i = act.activation(keys[r, b, g, h * LK:(h + 1) * LK], bank[3 + n % 2][r, 0:LK], ACT.Identity,
                                           bias=bias_cols[r, 1, g:g + 1], scale=0.25)
                    i.then_inc(S("keys_ready"), 1)
            for n in range(NT // 2):
                act.wait_ge(S("ln2_turned"), n + 1)
                act.activation(featT[:, :, 2 * n * P:(2 * n + 2) * P].rearrange("p k (t n) -> p t k n", t=2),
                               bank[n % 2][:, :].rearrange("p (t k n) -> p t k n", t=2, k=KD), ACT.Copy).then_inc(S("hT_ready"), 1)

            def keep_q(t, p):
                act.wait_ge(S("q_mm"), t + 1)
                for g in range(NG):
                    m = act.activation(qT[:, p, g, :], bank[5][:, g * P:(g + 1) * P], ACT.Identity, bias=bias_cols[:, 0, g:g + 1])
                m.then_inc(S("qT_ready"), 1)

            def exp_scores(t, p, g):
                act.wait_ge(S("shifted"), NG * t + g + 1)
                mv_, tv = prob_m[p][:, GH * g:GH * (g + 1), :], prob_t[p][:, GH * g:GH * (g + 1), :]
                act.activation(mv_, mv_, ACT.Exp)
                act.activation(tv, tv, ACT.Exp).then_inc(S("prob_ready"), 1)

            def keep_probT(t, g, waits=True):
                act.wait_ge(S("prob_turned"), (NG + 1) * t + g + 1)
                if waits:
                    act.wait_ge(S("pv_mm"), (NG + 1) * (t - 1) + g + 1)
                rows = KM if g < NG else P
                act.activation(probT[0:rows, GH * g:GH * (g + 1), :], bank[TURN_BANK[g]][0:rows, :].rearrange("p (h n) -> p h n", h=GH),
                               ACT.Copy).then_inc(S("probT_ready"), 1)

            keep_q(0, 0)

            def tile_step(t, p, now=True, before=True, waits=True, nxt=True):
                for g in range(NG):
                    if nxt and g == 1:
                        keep_q(t + 1, 1 - p)
                    if before:
                        keep_probT(t - 1, g, waits)
                    if before and g == NG - 1:
                        keep_probT(t - 1, NG, waits)
                    if now:
                        exp_scores(t, p, g)
            tile_step(0, 0, before=False)
            tile_step(1, 1, waits=False)
            with act.Fori(1, NT // 2 - 1) as i:
                for p in range(2):
                    tile_step(2 * i + p, p)
            tile_step(NT - 2, 0)
            tile_step(NT - 1, 1, nxt=False)
            tile_step(NT, 0, now=False, nxt=False)

            act.wait_ge(dve_once, at("ln3_var"))
            act.activation(nrm[:, 0, :], mv[:, :, 1], ACT.Sqrt, bias=eps_col[:, :]).then_inc(act_once, reached("ln3_sd"))
            for j in range(NT // GT):
                if j >= 2:
                    act.wait_ge(S("route_mm"), j - 1)
                for q in range(2):
                    act.wait_ge(S("x3_turned"), 2 * j + q + 1)
                    act.activation(x3T[j % 2][:, 2 * q:2 * q + 2, :, :],
                                   bank[2 * (j % 2) + q][:, :].rearrange("p (t k n) -> p t k n", t=2, k=KD), ACT.Copy
                                   ).then_inc(S("x3T_ready"), 1)

            def keep_hidden(n):
                for f in range(2):
                    act.wait_ge(S("up_mm"), 2 * n + f + 1)
                    if f == 0:
                        act.wait_ge(S("h_turned"), 2 * n)
                    act.activation(hid_e[:, f * 512:(f + 1) * 512], bank[f][:, :], ACT.Copy).then_inc(S("h_kept"), 1)

            def relu_half(n):
                e = act.value_load(expert_i[0:1, ds(n, 1)], min_val=0, max_val=NE - 1)
                act.wait_ge(S("h_turned"), 2 * n + 2)
                act.wait_ge(S("down_mm"), n)
                for f in range(4, 8):
                    i = act.activation(hidT[:, f, :], bank[3][:, (f - 4) * P:(f - 3) * P], ACT.Relu, bias=b1_cols[:, ds(e * NFF + f, 1)])
                i.then_inc(S("hT_half_b"), 1)

            act.wait_ge(dve_once, at("block_expert_ready"))
            keep_hidden(0)
            with act.Fori(0, NB - 1) as n:
                relu_half(n)
                keep_hidden(n + 1)
            relu_half(NB - 1)

        @block.vector
        def _(dve):
            dve.memset(eps_col[:, :], EPS).then_inc(dve_once, reached("eps_set"))
            for q in range(4):
                dve.wait_ge(S(f"x_loaded{q}"), 16)
                for t in range(4 * q, 4 * q + 4):
                    dve.bn_stats(stats[:, t, :], xres[:, t, :]).then_inc(S("bn_done"), 1)
            for t in range(NT):
                dve.wait_ge(S("bn_done"), t + 1)
                dve.bn_aggr(mv[:, t, :], stats[:, t, :]).then_inc(S("ln_agg"), 1)
            dve.wait_ge(S("ln_agg"), NT)
            dve.tensor_copy(nrm[:, 5, :], mv[:, :, 0]).then_inc(dve_once, reached("ln_var"))
            dve.wait_ge(act_once, at("ln_sd"))
            dve.reciprocal(nrm[:, 0, :], nrm[:, 0, :]).then_inc(dve_once, reached("rstd_1"))
            dve.wait_ge(dve_once, at("rstd_1"))
            dve.tensor_tensor(nrm[:, 1, :], mv[:, :, 1], nrm[:, 0, :], ALU.mult).then_inc(dve_once, reached("rstd_2"))
            dve.wait_ge(dve_once, at("rstd_2"))
            dve.tensor_tensor(nrm[:, 1, :], nrm[:, 1, :], nrm[:, 0, :], ALU.mult).then_inc(dve_once, reached("rms_var"))
            dve.wait_ge(act_once, at("rms_sd"))
            dve.reciprocal(nrm[:, 3, :], nrm[:, 2, :]).then_inc(dve_once, reached("rstd_3"))
            dve.wait_ge(dve_once, at("rstd_3"))
            dve.tensor_tensor(nrm[:, 3, :], nrm[:, 3, :], nrm[:, 0, :], ALU.mult).then_inc(dve_once, reached("rstd_4"))
            dve.wait_ge(dve_once, at("rstd_4"))
            dve.tensor_scalar(nrm[:, 1, :], nrm[:, 0, :], 1.0, None, ALU.add).then_inc(S("res_cols"), 1)
            dve.tensor_tensor(nrm[:, 2, :], nrm[:, 5, :], nrm[:, 0, :], ALU.mult).then_inc(S("res_cols"), 1)
            for t in range(NT):
                if t == GT:
                    dve.wait_ge(S("w_loaded"), 16 * 2)
                    dve.wait_ge(S("small_loaded"), 16 * 7)
                    for k in range(KD):
                        dve.tensor_scalar(w_in[:, k, IN_W - H:], w_in[:, k, IN_W - H:], norm_w[:, k:k + 1], None, ALU.mult
                                          ).then_inc(S("weights_ready"), 1)
                if t >= GT and t % 2 == 0:
                    dve.wait_ge(S("xn_turned"), t // 2 - 1)
                dve.tensor_scalar(xn[:, t % GT, :], xres[:, t, :], nrm[:, 5, t:t + 1], nrm[:, 3, t:t + 1],
                                  ALU.subtract, ALU.mult).then_inc(S("xn_ready"), 1)
            for k in range(KD):
                dve.tensor_scalar(w_in[:, k, DI:IN_W - H], w_in[:, k, DI:IN_W - H], norm_w[:, k:k + 1], None, ALU.mult
                                  ).then_inc(S("weights_ready"), 1)
            for k in range(KD):
                dve.tensor_scalar(w_in[:, k, 0:DI], w_in[:, k, 0:DI], norm_w[:, k:k + 1], 0.5, ALU.mult, ALU.mult
                                  ).then_inc(S("weights_ready"), 1)
            dve.tensor_scalar(conv_w[:, :, :], conv_w[:, :, :], 0.5, None, ALU.mult).then_inc(S("weights_ready"), 1)
            dve.tensor_scalar(conv_b[:, :], conv_b[:, :], 0.5, None, ALU.mult).then_inc(S("weights_ready"), 1)
            for k in range(NZ):
                dve.tensor_scalar(w_out[:, k, :], w_out[:, k, :], gnorm_w[:, k:k + 1], None, ALU.mult
                                  ).then_inc(S("weights_ready"), 1)
            dve.wait_ge(pe_once, at("dt_mm"))
            dve.tensor_tensor(th(dt_raw), bank[4][:, 0:NT * H].rearrange("p (t h) -> p t h", h=H),
                              dt_bias[:, :].unsqueeze(1).broadcast_to([P, NT, H]), ALU.add).then_inc(S("dt_kept"), 1)
            dve.wait_ge(S("dt_kept"), 1)
            dve.tensor_scalar(dt_neg, dt_raw, -1.0, None, ALU.mult).then_inc(dve_once, reached("dt_steps_1"))
            dve.tensor_scalar(dt_pos, dt_raw, 0.0, None, ALU.max).then_inc(dve_once, reached("dt_steps_2"))
            dve.wait_ge(dve_once, at("dt_steps_2"))
            dve.tensor_tensor(dt_neg, dt_neg, dt_raw, ALU.min).then_inc(dve_once, reached("dt_abs"))

            dve.wait_ge(S("weights_ready"), 3 * KD + NZ + 2)
            dve.wait_ge(S("xn_turned"), NT // 2)
            with dve.Fori(0, B) as b:
                dve.wait_ge(S("raw_used"), NX * (NBLK // B) * b)
                dve.memset(raw[:, :, 0:TAPS - 1], 0.0).then_inc(S("past_cleared"), 1)
                with dve.Fori(0, NBLK // B) as j:
                    dve.wait_ge(S("past_cleared"), b + 1)
                    blk = b * (NBLK // B) + j
                    for f in range(NZ):
                        dve.wait_ge(S("tanh_z_ready"), NZ * blk + f + 1)
                        dve.scalar_tensor_tensor(zsT[:, f, ds(blk * BLK, BLK)], tanh_z[:, f % 2, :], 1.0, bank[f % 5][:, :],
                                                 ALU.add, ALU.mult).then_inc(S("zs_ready"), 1)
                    for f in range(0, NX, 2):
                        for k in range(1, TAPS):
                            for g in (f, f + 1):
                                if k == 1:
                                    dve.wait_ge(S("tap0_ready"), NX * blk + g + 1)
                                else:
                                    dve.wait_ge(S("tap_done"), (TAPS - 2) * (NX * blk + f) + 2 * (k - 2) + g - f + 1)
                                acc = conv[:, g, :]
                                i = dve.scalar_tensor_tensor(acc, raw[:, g, k:k + BLK], conv_w[:, g, k:k + 1], acc, ALU.mult, ALU.add)
                                i.then_inc(S("tap_done") if k < TAPS - 1 else S("conv_sum"), 1)
                        for g in (f, f + 1):
                            dve.tensor_copy(raw[:, g, 0:TAPS - 1], raw[:, g, BLK:BLK + TAPS - 1]).then_inc(S("raw_used"), 1)
                    for f in range(NXP, NX):
                        dve.wait_ge(S("tanh_c_ready"), NX * blk + f + 1)
                        dve.scalar_tensor_tensor(xbcT[:, f, ds(blk * BLK, BLK)], tanh_c[:, f, :], 1.0, conv[:, f, :],
                                                 ALU.add, ALU.mult).then_inc(S("conv_done_dve"), 1)

            dve.wait_ge(act_once, at("dt_ln"))
            dve.tensor_tensor(dt_v, dt_pos, dt_exp, ALU.add).then_inc(dve_once, reached("dt_sum"))
            dve.wait_ge(dve_once, at("dt_sum"))
            dve.wait_ge(act_once, at("a_exp"))
            dve.scalar_tensor_tensor(th(dta), th(dt_v), -1.0, a_log[:, :].unsqueeze(1).broadcast_to([P, NT, H]),
                                     ALU.mult, ALU.mult).then_inc(dve_once, reached("dt_ready"))
            dve.wait_ge(act_once, at("dec_exp"))
            dve.tensor_copy(tot, bank[1][:, 0:NT * H]).then_inc(dve_once, reached("tot_kept"))
            dve.wait_ge(dve_once, at("tot_kept"))
            dve.wait_ge(act_once, at("ecum_exp"))
            dve.tensor_tensor(wend, tot, bank[0][:, 0:NT * H], ALU.subtract).then_inc(dve_once, reached("wend_diff"))
            dve.memset(th(ecum)[:, 0:NT:TB, :], 0.0).then_inc(dve_once, reached("first_cleared_1"))
            dve.memset(th(dec)[:, 0:NT:TB, :], 0.0).then_inc(dve_once, reached("first_cleared_2"))
            dve.wait_ge(dve_once, at("first_cleared_2"))
            dve.wait_ge(act_once, at("wend_exp"))
            dve.tensor_tensor(wend, wend, dt_v, ALU.mult).then_inc(dve_once, reached("decay_ready"))
            dve.wait_ge(dve_once, at("decay_ready"))
            dve.wait_ge(S("conv_done"), NXP * NBLK)
            dve.wait_ge(S("conv_done_dve"), (NX - NXP) * NBLK)

            def chunk_sides(t, p, wait):
                dve.wait_ge(S("g_mm"), t + 1)
                if wait:
                    dve.wait_ge(S("state_mm"), t - 1)
                dve.tensor_copy(b_tok[:, p, :], bank[1][:, 0:P])
                if wait:
                    dve.wait_ge(S("m_ready"), t - 1)
                dve.tensor_tensor(gmat[:, p, :], bank[1][:, P:2 * P], tri_le[:, :], ALU.mult).then_inc(S("g_ready"), 1)
                xv = bank[0][:, :].rearrange("p (h n) -> p h n", h=H)
                for dst, col in ((xdt, dt_v), (xend, wend)):
                    dve.tensor_tensor(dst[:, p, :].rearrange("p (h n) -> p h n", h=H), xv, heads(col[:, ds(t * H, H)], HP),
                                      ALU.mult)
                if wait:
                    dve.wait_ge(S("y_ready"), t - 1)
                dve.tensor_tensor(xskip[:, p, :].rearrange("p (h n) -> p h n", h=H), xv, heads(d_skip[:, :], HP),
                                  ALU.mult).then_inc(S("sides_ready"), 1)

            def gate(t, p, wait):
                dve.wait_ge(S("y_transposed"), t + 1)
                if wait:
                    dve.wait_ge(S("out_mm"), t - 1)
                    dve.wait_ge(S("sq_ready"), t - 1)
                dve.tensor_tensor(gated[:, p, :, :], bank[7][:, :].rearrange("p (k n) -> p k n", k=NZ),
                                  zsT[:, :, ds(t * P, P)], ALU.mult).then_inc(S("gated_ready"), 1)

            def sum_y(t, p, wait):
                yv = y_in[:, p, :]
                dve.wait_ge(S("inter_mm"), t + 1)
                if wait:
                    dve.wait_ge(S("y_transposed"), t - 1)
                dve.tensor_tensor(yv.rearrange("p (h n) -> p h n", h=H), bank[4][:, :].rearrange("p (h n) -> p h n", h=H),
                                  heads(ecum[:, ds(t * H, H)], HP), ALU.mult).then_inc(S("y_part"), 1)
                dve.wait_ge(S("intra_mm"), t + 1)
                dve.wait_ge(S("y_part"), 2 * t + 1)
                dve.tensor_tensor(yv, yv, bank[5][:, :], ALU.add).then_inc(S("y_part"), 1)
                dve.wait_ge(S("y_part"), 2 * t + 2)
                dve.wait_ge(S("sides_ready"), t + 1)
                dve.tensor_tensor(yv, yv, xskip[:, p, :], ALU.add).then_inc(S("y_ready"), 1)
                dve.wait_ge(S("state_mm"), t + 1)
                dve.wait_ge(S("state_decayed"), t + 1)
                dve.tensor_tensor(state, state, bank[6][:, :], ALU.add).then_inc(S("state_added"), 1)

            chunk_sides(0, 0, False)
            chunk_sides(1, 1, False)
            sum_y(0, 0, False)

            def dve_step(t, p, wait=True):
                chunk_sides(t + 1, 1 - p, True)
                gate(t - 1, 1 - p, wait)
                sum_y(t, p, wait)
            dve_step(1, 1, False)
            dve_step(2, 0)
            with dve.Fori(1, NT // 2 - 1) as i:
                dve_step(2 * i + 1, 1)
                dve_step(2 * i + 2, 0)
            gate(NT - 2, 0, True)
            sum_y(NT - 1, 1, True)
            gate(NT - 1, 1, True)

            dve.wait_ge(act_once, at("gn_sd"))
            dve.reciprocal(ssq[:, 1, :], ssq[:, 1, :]).then_inc(dve_once, reached("gn_rstd"))
            dve.wait_ge(dve_once, at("gn_rstd"))
            dve.wait_ge(S("state_added"), NT)
            dve.wait_ge(S("y_ready"), NT)
            for t in range(NT):
                dve.tensor_scalar(y_tok[:, t, :], y_tok[:, t, :], ssq[:, 1, t:t + 1], None, ALU.mult).then_inc(S("y_tok_ready"), 1)
            dve.wait_ge(S("mem_w_loaded"), 16 * 7)
            dve.tensor_copy(scorer_w2b[:, :], scorer_w2[:, 0:1].broadcast_to([SD, P])).then_inc(dve_once, reached("w2b_ready"))
            dve.wait_ge(pool_once, at("pos_set"))
            dve.tensor_copy(pos[:, :], pos_i[:, :]).then_inc(dve_once, reached("pos_ready"))
            dve.memset(ones_bf[:, 0:1], 1.0)
            dve.tensor_copy(n_earlier, tile_i[:, :]).then_inc(dve_once, reached("cols_set"))
            def half_plus(blk):
                dve.wait_ge(S("score_tanh"), blk + 1)
                sv = sig[:, blk * BLK:(blk + 1) * BLK]
                dve.tensor_scalar(sv, sv, 0.5, 0.5, ALU.mult, ALU.add).then_inc(S("sig_ready"), 1)

            for blk in range(NBLK):
                dve.wait_ge(S("hid_mm"), blk + 1)
                if blk >= 2:
                    dve.wait_ge(S("score_mm"), blk - 1)
                dve.tensor_scalar(hid[0:SD, blk % 2, :], bank[4 + blk % 2][0:SD, :], 0.0, None, ALU.max).then_inc(S("hid_ready"), 1)
                if blk >= 2:
                    half_plus(blk - 2)
            half_plus(NBLK - 2)
            half_plus(NBLK - 1)
            dve.wait_ge(S("sig_ready"), NBLK)
            for b in range(B):
                dve.wait_ge(S("s_col_ready"), b)
                dve.tensor_tensor(junk.rearrange("p (t n) -> p t n", t=TB), sig[:, b * T:(b + 1) * T].rearrange("p (t n) -> p t n", t=TB),
                                  ident[:, :].unsqueeze(1).broadcast_to([P, TB, P]), ALU.mult).then_inc(S("memory_step"), 1)
                dve.wait_ge(S("memory_step"), b + 1)
                dve.tensor_reduce(s_col[:, b * TB:(b + 1) * TB], junk.rearrange("p (t n) -> p t n", t=TB), AX, ALU.add
                                  ).then_inc(S("s_col_ready"), 1)
            dve.wait_ge(S("s_col_ready"), B)
            dve.tensor_scalar(valid, s_col, 0.5, None, ALU.is_gt).then_inc(dve_once, reached("valid_ready"))
            for b in range(B):
                for k in range(TB):
                    t = b * TB + k
                    sc = s_col[:, t:t + 1]
                    if t >= 2:
                        dve.wait_ge(S("rank_counted"), 2 * (t - 1))
                    if k >= 2 or b:
                        dve.wait_ge(S("rank_cols"), (TB - 1) * b + max(k - 1, 0))
                    dve.tensor_scalar(greater[:, k % 2, k * P:T], sig[:, b * T + k * P:(b + 1) * T], sc, None, ALU.is_gt, ALU.add,
                                      accum_out=n_gt[:, t:t + 1]).then_inc(S("rank_counted"), 1)
                    dve.scalar_tensor_tensor(junk_eq[:, k % 2, :], sig[:, t * P:(t + 1) * P], sc, tri_gt[:, :], ALU.is_equal, ALU.mult,
                                             accum_out=n_eq[:, t:t + 1]).then_inc(S("rank_counted"), 1)
            dve.wait_ge(S("rank_counted"), 2 * NT)
            dve.tensor_tensor(rank, n_gt, n_eq, ALU.add).then_inc(dve_once, reached("rank_sum_1"))
            dve.wait_ge(dve_once, at("rank_sum_1"))
            dve.wait_ge(dve_once, at("cols_set"))
            dve.tensor_tensor(rank, rank, n_earlier, ALU.add).then_inc(dve_once, reached("rank_sum_2"))
            dve.wait_ge(dve_once, at("rank_sum_2"))
            dve.wait_ge(S("rank_cols"), (TB - 1) * B)
            later = [v.rearrange("p (b t) -> p b t", b=B)[:, :, 1:] for v in (rank, bank[7][:, 0:NT])]
            dve.tensor_tensor(later[0], later[0], later[1], ALU.subtract).then_inc(dve_once, reached("rank_sum_3"))
            dve.wait_ge(dve_once, at("rank_sum_3"))
            dve.wait_ge(pe_once, at("mean_mm"))
            dve.tensor_reduce(mean_s[:, :], bank[6][:, 0:NT].rearrange("p (b t) -> p b t", b=B), AX, ALU.add).then_inc(dve_once, reached("mean_ready_1"))
            dve.wait_ge(dve_once, at("mean_ready_1"))
            dve.tensor_scalar(mean_s[:, :], mean_s[:, :], 1.0 / T, 0.3, ALU.mult, ALU.is_gt).then_inc(dve_once, reached("mean_ready_2"))
            dve.wait_ge(dve_once, at("valid_ready"))
            dve.wait_ge(dve_once, at("pos_ready"))
            dve.wait_ge(dve_once, at("mean_ready_2"))
            for b in range(B):
                oh = onehot[:, b * TB:(b + 1) * TB, :]
                dve.tensor_tensor(oh, pos[:, :].unsqueeze(1).broadcast_to([P, TB, POOL]),
                                  rank[:, b * TB:(b + 1) * TB].unsqueeze(2).broadcast_to([P, TB, POOL]), ALU.is_equal
                                  ).then_inc(S("memory_step"), 1)
                dve.wait_ge(S("memory_step"), B + b + 1)
                dve.tensor_tensor(oh, oh, valid[:, b * TB:(b + 1) * TB].unsqueeze(2).broadcast_to([P, TB, POOL]), ALU.mult
                                  ).then_inc(S("onehot_ready"), 1)
            for b in range(B):
                dve.wait_ge(S("select_mm"), b + 1)
                dve.tensor_copy(pool_tok[0:POOL, b, :], mem_bank[b][1][0:POOL, 0:D]).then_inc(S("pool_tok_ready"), 1)
                dve.tensor_scalar(vbias[:, b, :], mem_bank[b][2][:, 0:POOL], -1.0, 1e9, ALU.add, ALU.mult).then_inc(S("vbias_ready"), 1)
            for b in range(B):
                dve.wait_ge(S("val_mm"), b + 1)
                dve.tensor_scalar(val[0:POOL, b, :], mem_bank[b][2][0:POOL, 0:D], mean_s[0:POOL, b:b + 1], None, ALU.mult
                                  ).then_inc(S("val_ready"), 1)
            dve.wait_ge(S("vbias_ready"), B)
            dve.wait_ge(S("val_ready"), B)

            def soften(n, first=False):
                dve.wait_ge(S("logit_mm"), n + 1)
                if not first:
                    dve.wait_ge(S("attn_turned"), n)
                b = n // (T // BLK)
                dve.tensor_tensor(logit, bank[1][:, 0:4 * 64].rearrange("p (i n) -> p i n", i=4)[:, :, 0:POOL],
                                  vbias[:, ds(b, 1), :].broadcast_to([P, 4, POOL]), ALU.add).then_inc(S("soften_step"), 1)
                dve.wait_ge(S("soften_step"), 4 * n + 1)
                dve.tensor_reduce(red[:, 0, :], logit, AX, ALU.max).then_inc(S("soften_step"), 1)
                dve.wait_ge(S("soften_step"), 4 * n + 2)
                dve.tensor_tensor(logit, logit, red[:, 0, :].unsqueeze(2).broadcast_to([P, 4, POOL]), ALU.subtract
                                  ).then_inc(S("logit_shifted"), 1)
                if not first:
                    dve.wait_ge(S("ret_mm"), KD * n)
                dve.tensor_copy(val_now[0:POOL, :], val[0:POOL, ds(b, 1), :].rearrange("p a d -> p (a d)")).then_inc(S("val_now_ready"), 1)
                dve.wait_ge(S("logit_exp"), n + 1)
                dve.tensor_reduce(red[:, 1, :], logit, AX, ALU.add).then_inc(S("soften_step"), 1)
                dve.wait_ge(S("soften_step"), 4 * n + 3)
                dve.reciprocal(red[:, 2, :], red[:, 1, :]).then_inc(S("soften_step"), 1)
                dve.wait_ge(S("soften_step"), 4 * n + 4)
                dve.tensor_tensor(logit, logit, red[:, 2, :].unsqueeze(2).broadcast_to([P, 4, POOL]), ALU.mult
                                  ).then_inc(S("attn_ready"), 1)

            def add_retrieved(n):
                for m in range(KD):
                    dve.wait_ge(S("gate_tanh"), KD * n + m + 1)
                    if m == 0:
                        dve.wait_ge(S("upd_turned"), 2 * n)
                    dve.scalar_tensor_tensor(upd[:, m, :], gate_t[:, m, :], 1.0, retT[:, m, :], ALU.add, ALU.mult
                                             ).then_inc(S("upd_ready"), 1)
                for m in range(2):
                    dve.wait_ge(S("upd_turned"), 2 * n + m + 1)
                    xv = xres[:, ds(4 * n + 2 * m, 2), :]
                    dve.scalar_tensor_tensor(xv, bank[7 * (1 - m)][:, :].rearrange("p (t d) -> p t d", t=2), 0.5, xv,
                                             ALU.mult, ALU.add).then_inc(S("x1_ready"), 1)
                dve.wait_ge(S("x1_ready"), 2 * n + 2)
                for i in range(4):
                    dve.bn_stats(stats[:, ds(4 * n + i, 1), :], xres[:, ds(4 * n + i, 1), :]).then_inc(S("bn_done"), 1)

            dve.wait_ge(S("res_y_added"), NT)
            soften(0, True)
            with dve.Fori(0, NBLK - 1) as n:
                soften(n + 1)
                add_retrieved(n)
            add_retrieved(NBLK - 1)

            dve.wait_ge(S("bn_done"), 2 * NT)
            for t in range(NT):
                dve.bn_aggr(mv[:, t, :], stats[:, t, :]).then_inc(S("ln_agg"), 1)
            dve.wait_ge(S("ln_agg"), 2 * NT)
            dve.tensor_copy(nrm[:, 5, :], mv[:, :, 0]).then_inc(dve_once, reached("ln2_var"))
            dve.wait_ge(S("x_w_loaded"), 16 * 9)
            dve.tensor_scalar(mask_row[:, :], mask_i[:, :], 0.0, 4 * NEG, ALU.is_gt, ALU.mult).then_inc(dve_once, reached("mask_row_ready"))
            dve.wait_ge(pe_once, at("bias_turned"))
            dve.tensor_copy(bias_cols[:, 0, :], bank[2][:, 0:NG])
            dve.tensor_scalar(bias_cols[:, 1, :], bank[2][:, NG:2 * NG], 0.25, None, ALU.mult).then_inc(dve_once, reached("bias_cols_ready"))
            dve.wait_ge(act_once, at("ln2_sd"))
            dve.reciprocal(nrm[:, 0, :], nrm[:, 0, :]).then_inc(dve_once, reached("ln2_rstd"))
            dve.wait_ge(dve_once, at("ln2_rstd"))

            def norm_row(t):
                if t >= GT and t % 2 == 0:
                    dve.wait_ge(S("ln2_turned"), t // 2 - 1)
                dve.tensor_scalar(st4[:, t % GT, :], xres[:, t, :], nrm[:, 5, t:t + 1],
                                  nrm[:, 0, t:t + 1], ALU.subtract, ALU.mult).then_inc(S("ln2_ready"), 1)
            for t in range(GT):
                norm_row(t)
            dve.wait_ge(S("pads_zero"), 5)
            for b in range(B):
                dve.wait_ge(S("val_main_mm"), b + 1)
                dve.tensor_copy(v_main[0:KM, b, :, 0:HD], bank[5][0:KM, 0:D].rearrange("p (h d) -> p h d", d=HD)).then_inc(S("v_main_ready"), 1)
                dve.wait_ge(S("val_tail_mm"), b + 1)
                for h in range(GH):
                    r = slice(32 * h, 32 * h + 32)
                    dve.memset(v_tail[r, b, :, h * (HD + 1) + HD:(h + 1) * (HD + 1)], 1.0)
                    i = dve.tensor_copy(v_tail[r, b, :, h * (HD + 1):h * (HD + 1) + HD],
                                        bank[6][r, 0:D].rearrange("p (g h d) -> p g h d", g=NG, h=GH)[:, :, h, :])
                i.then_inc(S("v_tail_ready"), 1)
            for t in range(GT, NT):
                norm_row(t)

            def shift_scores(t, p, g):
                m = NG * t + g
                h = slice(GH * g, GH * (g + 1))
                sc = pair[g % 2][:, :, 0:2 * LK].rearrange("p a (h n) -> p a h n", h=2)
                mx = xmax[:, p, h]
                mx4 = mx.rearrange("p (a h) -> p a h", a=2).unsqueeze(3)
                four = lambda v: v.rearrange("p (a h) n -> p a h n", a=2)
                dve.wait_ge(S("score_x_mm"), m + 1)
                dve.tensor_reduce(mx.rearrange("p (a h) -> p a h", a=2), sc, AX, ALU.max).then_inc(S("score_max"), 1)
                dve.wait_ge(S("score_max"), m + 1)
                dve.tensor_tensor(four(prob_m[p][:, h, :]), sc[:, :, :, 0:KM], mx4.broadcast_to([P, 2, 2, KM]), ALU.subtract)
                dve.tensor_tensor(four(prob_t[p][:, h, :]), sc[:, :, :, KM:LK], mx4.broadcast_to([P, 2, 2, KT]), ALU.subtract
                                  ).then_inc(S("shifted"), 1)

            def row_stats(t):
                dve.wait_ge(S("x2_ready"), t + 1)
                dve.bn_stats(stats[:, ds(t, 1), :], xres[:, ds(t, 1), :]).then_inc(S("bn_done"), 1)

            def weigh(t, p, waits=True):
                dve.wait_ge(S("pv_mm"), (NG + 1) * (t + 1))
                ov = bank[6 + p][:, 0:XH * (HD + 1)].rearrange("p (h c) -> p h c", c=HD + 1)
                dve.reciprocal(xinv[:, p, :], ov[:, :, HD]).then_inc(S("x_inv"), 1)
                dve.wait_ge(S("x_inv"), t + 1)
                if waits:
                    dve.wait_ge(S("x2_ready"), t - 1)
                dve.tensor_tensor(head_o[:, p, :].rearrange("p (h d) -> p h d", d=HD), ov[:, :, 0:HD],
                                  xinv[:, p, :].unsqueeze(2).broadcast_to([P, XH, HD]), ALU.mult).then_inc(S("head_o_ready"), 1)

            def tile_step(t, p, now=True, before=True, waits=True):
                if now and before:
                    dve.wait_ge(S("prob_turned"), (NG + 1) * (t - 1))
                for g in range(NG):
                    if now:
                        shift_scores(t, p, g)
                    if before and g == 1:
                        weigh(t - 2, p, waits)
                if before and waits:
                    row_stats(t - 4)
            tile_step(0, 0, before=False)
            tile_step(1, 1, before=False)
            tile_step(2, 0, waits=False)
            tile_step(3, 1, waits=False)
            with dve.Fori(2, NT // 2) as i:
                for p in range(2):
                    tile_step(2 * i + p, p)
            tile_step(NT, 0, now=False)
            tile_step(NT + 1, 1, now=False)
            row_stats(NT - 2)
            row_stats(NT - 1)

            dve.wait_ge(S("bn_done"), 3 * NT)
            for t in range(NT):
                dve.bn_aggr(mv[:, t, :], stats[:, t, :]).then_inc(S("ln_agg"), 1)
            dve.wait_ge(S("ln_agg"), 3 * NT)
            dve.tensor_copy(nrm[:, 5, :], mv[:, :, 0]).then_inc(dve_once, reached("ln3_var"))
            dve.wait_ge(act_once, at("ln3_sd"))
            dve.reciprocal(nrm[:, 0, :], nrm[:, 0, :]).then_inc(dve_once, reached("ln3_rstd"))
            dve.wait_ge(dve_once, at("ln3_rstd"))
            dve.wait_ge(S("route_w_loaded"), 16 * 3)

            def add_br(j):
                dve.wait_ge(S("route_mm"), j + 1)
                dve.tensor_tensor(logits[:, GT * j:GT * (j + 1), :], bank[4 + j % 2][:, 0:GT * NE].rearrange("p (t e) -> p t e", t=GT),
                                  br_row.unsqueeze(1).broadcast_to([P, GT, NE]), ALU.add).then_inc(S("logits_ready"), 1)

            for j in range(NT // GT):
                for q in range(GT):
                    t = GT * j + q
                    if j and q % 2 == 0:
                        dve.wait_ge(S("x3_turned"), 2 * (j - 1) + q // 2 + 1)
                    dve.tensor_scalar(st4[:, q, :], xres[:, t, :], nrm[:, 5, t:t + 1], nrm[:, 0, t:t + 1],
                                      ALU.subtract, ALU.mult).then_inc(S("x3_ready"), 1)
                if j:
                    add_br(j - 1)
            add_br(NT // GT - 1)
            dve.wait_ge(pool_once, at("counters_set"))
            dve.tensor_copy(desc, desc_i)
            dve.tensor_copy(thr, thr_i)
            dve.tensor_copy(blk_n, blk_i).then_inc(dve_once, reached("iotas_ready"))
            dve.wait_ge(dve_once, at("iotas_ready"))
            dve.wait_ge(S("logits_ready"), NT // GT)

            def along(v, n):
                return v.unsqueeze(2).broadcast_to([P, v.shape[1], n])

            def across(v, n):
                return v.unsqueeze(1).broadcast_to([P, n, v.shape[1]])

            def link(ins):
                links[0] += 1
                ins.then_inc(S("route_step"), 1)
                dve.wait_ge(S("route_step"), links[0])
            links = [0]
            link(dve.tensor_reduce(best, logits, AX, ALU.max))
            link(dve.tensor_tensor(hot, logits, along(best, NE), ALU.is_equal))
            link(dve.tensor_tensor(hot, hot, across(desc, NT), ALU.mult))
            link(dve.tensor_reduce(best, hot, AX, ALU.max))
            dve.tensor_tensor(hot, across(desc, NT), along(best, NE), ALU.is_equal).then_inc(S("hot_ready"), 1)
            link(dve.memset(before[:, 0, :], 0.0))
            dve.wait_ge(pe_once, at("count_mm_2"))
            tile_n = bank[5][:, 0:NT * NE].rearrange("p (t e) -> p t e", e=NE)
            for t in range(NT):
                link(dve.tensor_tensor(before[:, t + 1, :], before[:, t, :], tile_n[:, t, :], ALU.add))
            link(dve.tensor_tensor(blocks_c, along(before[:, NT, :], NT), across(thr, NE), ALU.is_gt))
            link(dve.memset(first_blk[:, 0:1], 0.0))
            link(dve.tensor_reduce(first_blk[:, 1:], blocks_c, AX, ALU.add))
            for e in range(1, NE):
                link(dve.tensor_tensor(first_blk[:, e + 1:e + 2], first_blk[:, e + 1:e + 2], first_blk[:, e:e + 1], ALU.add))
            link(dve.tensor_tensor(slot_t, bank[4][:, 0:NT * NE].rearrange("p (t e) -> p t e", e=NE), before[:, 0:NT, :], ALU.add))
            link(dve.scalar_tensor_tensor(slot_t, across(first_blk[:, 0:NE], NT), float(P), slot_t, ALU.mult, ALU.add))
            link(dve.tensor_tensor(slot_t, slot_t, hot, ALU.mult))
            link(dve.tensor_reduce(slot_f, slot_t, AX, ALU.add))
            link(dve.tensor_scalar(slot_i, slot_f, -1.0, None, ALU.add))
            link(dve.tensor_tensor(expert_c, along(blk_n, NE), across(first_blk[:, 1:], NB), ALU.is_ge))
            link(dve.tensor_reduce(expert_f, expert_c, AX, ALU.add))
            dve.tensor_scalar(expert_i, expert_f, float(NE - 1), None, ALU.min).then_inc(dve_once, reached("block_expert_ready"))
            with dve.Fori(0, NT // GT) as i:
                for p in range(GT):
                    t = GT * i + p
                    dve.wait_ge(S(f"scattered{p}"), 16 * i)
                    xt = xres[:, ds(t, 1), :].rearrange("p a d -> p (a d)")
                    dve.tensor_scalar(rows[:, p, 0:D], xt, nrm[:, 5, ds(t, 1)], nrm[:, 0, ds(t, 1)], ALU.subtract, ALU.mult)
                    dve.tensor_copy(rows[:, p, D:2 * D], xt)
                    dve.tensor_copy(rows[:, p, 2 * D:].bitcast(I32), token_i[:, ds(t, 1)])
                    dve.tensor_copy(slot_now[:, p:p + 1], slot_i[:, ds(t, 1)]).then_inc(S("row_ready"), 1)

            def keep_xs(n, p):
                dve.wait_ge(S("xs_turned"), n + 1)
                dve.tensor_copy(xsT[:, p, :, :], bank[6][:, 0:D].rearrange("p (k n) -> p k n", k=KD)).then_inc(S("xsT_ready"), 1)

            def relu_and_add(n, p, nxt=True):
                e = dve.value_load(expert_i[0:1, ds(n, 1)], min_val=0, max_val=NE - 1)
                dve.wait_ge(S("h_turned"), 2 * n + 1)
                dve.wait_ge(S("down_mm"), n)
                for f in range(4):
                    i = dve.tensor_scalar(hidT[:, f, :], bank[2][:, f * P:(f + 1) * P], b1_cols[:, ds(e * NFF + f, 1)], 0.0, ALU.add, ALU.max)
                i.then_inc(S("hT_half_a"), 1)
                dve.wait_ge(S(f"rest_loaded{p}"), 8 * (n - p) + 16)
                dve.wait_ge(S(f"out_stored{p}"), 8 * (n - p))
                dve.tensor_tensor(yo[:, p, :], rest[:, p, 0:D], b2_rows[:, ds(e, 1), :].rearrange("p a d -> p (a d)"), ALU.add
                                  ).then_inc(S("yo_part"), 1)
                if nxt:
                    keep_xs(n + 2, p)
                dve.wait_ge(S("yo_part"), n + 1)
                dve.wait_ge(S("down_mm"), n + 1)
                dve.tensor_tensor(yo[:, p, :], yo[:, p, :], bank[4][:, 0:D], ALU.add).then_inc(S("yo_ready"), 1)

            dve.wait_ge(S("w2_loaded"), 16 * 2 * NE)
            keep_xs(0, 0)
            keep_xs(1, 1)
            with dve.Fori(0, NB // 2 - 1) as i:
                relu_and_add(2 * i, 0)
                relu_and_add(2 * i + 1, 1)
            relu_and_add(NB - 3, 0)
            relu_and_add(NB - 2, 1, False)
            relu_and_add(NB - 1, 0, False)

        @block.tensor
        def _(pe):
            pe.wait_ge(pool_once, at("masks_set_3"))

            def turn_group(j):
                for q in range(GT):
                    t = GT * j + q
                    pe.wait_ge(S("xn_ready"), t + 1)
                    if t % 2 == 0 and t >= 2 * 4:
                        pe.wait_ge(S("xnT_ready"), t // 2 - 3)
                    for k in range(KD):
                        m = pe.transpose(bank[(t // 2) % 4][:, (t % 2) * D + k * P:(t % 2) * D + (k + 1) * P],
                                         xn[:, q, k * P:(k + 1) * P], ident[:, :])
                    if t % 2:
                        m.then_inc(S("xn_turned"), 1)

            def dt_group(j):
                pe.wait_ge(S("xnT_ready"), 2 * (j + 1))
                pe.wait_ge(S("weights_ready"), KD)
                for t in range(GT * j, GT * (j + 1)):
                    for k in range(KD):
                        m = pe.matmul(bank[4][:, t * H:(t + 1) * H], featT[:, k, t * P:(t + 1) * P], w_in[:, k, IN_W - H:],
                                      start=(k == 0), stop=(k == KD - 1))
                if j == NT // GT - 1:
                    m.then_inc(pe_once, reached("dt_mm"))
            turn_group(0)
            turn_group(1)
            for j in range(2, NT // GT):
                dt_group(j - 2)
                turn_group(j)
            dt_group(NT // GT - 2)
            dt_group(NT // GT - 1)
            pe.wait_ge(S("weights_ready"), 3 * KD)
            pe.wait_ge(S("dt_kept"), 1)

            def project(blk, first=False):
                for f in range(NZ + NX):
                    if f >= 5 + NZ:
                        pe.wait_ge(S("raw_ready"), NX * blk + f - 4 - NZ)
                    elif f >= 5:
                        pe.wait_ge(S("zs_ready"), NZ * blk + f - 4)
                    elif not first:
                        pe.wait_ge(S("raw_ready"), NX * blk - 4 + f)
                    for k in range(KD):
                        m = pe.matmul(bank[f % 5][:, :], w_in[:, k, f * P:(f + 1) * P], featT[:, k, ds(blk * BLK, BLK)],
                                      start=(k == 0), stop=(k == KD - 1))
                    m.then_inc(S("proj_mm"), 1)
            project(0, True)
            with pe.Fori(1, NBLK) as blk:
                project(blk)
            pe.wait_ge(dve_once, at("dt_ready"))
            pe.wait_ge(S("raw_ready"), NX * NBLK)
            pe.wait_ge(S("zs_ready"), NZ * NBLK)
            pe.matmul(bank[0][:, 0:NT * H], tri_le[:, :], dta, start=True, stop=True).then_inc(pe_once, reached("cum_mm_1"))
            pe.matmul(bank[1][:, 0:NT * H], ones[:, :], dta, start=True, stop=True).then_inc(pe_once, reached("cum_mm_2"))
            pe.wait_ge(dve_once, at("decay_ready"))

            def turn(t, p, wait):
                pe.wait_ge(S(f"chunk_loaded{p}"), 8 * (t - p) + 16)
                if wait:
                    pe.wait_ge(S("sides_ready"), t)
                for k in range(NZ):
                    pe.transpose(bank[0][:, k * P:(k + 1) * P], xbc[:, p, k, :], ident[:, :])
                pe.transpose(bank[1][:, 0:P], xbc[:, p, NZ, :], ident[:, :])
                pe.matmul(bank[1][:, P:2 * P], xbc[:, p, NZ, :], xbc[:, p, NZ + 1, :], start=True, stop=True
                          ).then_inc(S("g_mm"), 1)

            def segments(t, p, wait):
                pe.wait_ge(S("seg_ready"), t + 1)
                if wait:
                    pe.wait_ge(S("decay_mat"), t)
                for q in range(2):
                    m = pe.matmul(bank[2 + q][:, :], tri_gt[:, :], seg[:, p, 4 * q:4 * q + 4, :], start=True, stop=True)
                m.then_inc(S("seg_mm"), 1)

            def transpose_y(t, p, wait):
                pe.wait_ge(S("y_ready"), t + 1)
                if wait:
                    pe.wait_ge(S("out_kept"), t)
                for k in range(NZ):
                    m = pe.transpose(bank[7][:, k * P:(k + 1) * P], y_in[:, p, k * P:(k + 1) * P], ident[:, :])
                m.then_inc(S("y_transposed"), 1)

            def mix(t, p, wait):
                pe.wait_ge(S("sides_ready"), t + 1)
                pe.wait_ge(S("state_added"), t) if wait else pe.wait_ge(pool_once, at("state_set"))
                pe.matmul(bank[4][:, :], xbc[:, p, NZ + 1, :], state, start=True, stop=True).then_inc(S("inter_mm"), 1)
                pe.wait_ge(S("m_ready"), t + 1)
                for h in range(H):
                    m = pe.matmul(bank[5][:, h * HP:(h + 1) * HP], lmat[:, p, h, :], xdt[:, p, h * HP:(h + 1) * HP],
                                  start=True, stop=True)
                m.then_inc(S("intra_mm"), 1)
                pe.matmul(bank[6][:, :], b_tok[:, p, :], xend[:, p, :], start=True, stop=True).then_inc(S("state_mm"), 1)

            def total_square(t, p):
                pe.wait_ge(S("sq_summed"), t + 1)
                pe.matmul(bank[7][:, D:D + 1], sq[:, p, 0, :], ones[:, 0:1], start=True, stop=True).then_inc(S("out_mm"), 1)

            def project_out(t, p, first=False):
                pe.wait_ge(S("gated_ready"), t + 1)
                for k in range(NZ):
                    m = pe.matmul(bank[7][:, 0:D], gated[:, p, k, :], w_out[:, k, :], start=(k == 0), stop=(k == NZ - 1))
                if first:
                    m.then_inc(S("out_mm"), 1)
                else:
                    total_square(t - 1, 1 - p)

            turn(0, 0, False)
            segments(0, 0, False)
            turn(1, 1, True)
            segments(1, 1, True)
            mix(0, 0, False)

            def pe_step(t, p, wait=True):
                turn(t + 1, 1 - p, True)
                segments(t + 1, 1 - p, True)
                transpose_y(t - 1, 1 - p, wait)
                mix(t, p, True)
                project_out(t - 1, 1 - p, not wait)
            pe_step(1, 1, False)
            pe_step(2, 0)
            with pe.Fori(1, NT // 2 - 1) as i:
                pe_step(2 * i + 1, 1)
                pe_step(2 * i + 2, 0)
            transpose_y(NT - 2, 0, True)
            mix(NT - 1, 1, True)
            project_out(NT - 2, 0)
            transpose_y(NT - 1, 1, True)
            project_out(NT - 1, 1)
            pe.wait_ge(S("out_kept"), NT)
            total_square(NT - 1, 1)
            def turn_y(j):
                for t in range(GT * j, GT * (j + 1)):
                    pe.wait_ge(S("y_tok_ready"), t + 1)
                    if t % 2 == 0 and t >= 2 * 4:
                        pe.wait_ge(S("yT_ready"), t // 2 - 3)
                    for k in range(KD):
                        m = pe.transpose(bank[(t // 2) % 4][:, (t % 2) * D + k * P:(t % 2) * D + (k + 1) * P],
                                         y_tok[:, t, k * P:(k + 1) * P], ident[:, :])
                    if t % 2:
                        m.then_inc(S("y_turned"), 1)

            def score_hidden(blk):
                pe.wait_ge(S("yT_ready"), 2 * (blk + 1))
                pe.wait_ge(dve_once, at("w2b_ready"))
                if blk >= 2:
                    pe.wait_ge(S("hid_ready"), blk - 1)
                for k in range(KD):
                    m = pe.matmul(bank[4 + blk % 2][0:SD, :], scorer_w1[:, k, :], featT[:, k, blk * BLK:(blk + 1) * BLK],
                                  start=(k == 0), stop=(k == KD - 1))
                m.then_inc(S("hid_mm"), 1)

            def score_row(blk):
                pe.wait_ge(S("hid_ready"), blk + 1)
                if blk >= 2:
                    pe.wait_ge(S("score_tanh"), blk - 1)
                pe.matmul(bank[6 + blk % 2][:, :], scorer_w2b[:, :], hid[0:SD, blk % 2, :], start=True, stop=True).then_inc(S("score_mm"), 1)
            turn_y(0)
            for j in range(1, NBLK):
                turn_y(j)
                score_hidden(j - 1)
                if j >= 2:
                    score_row(j - 2)
            score_hidden(NBLK - 1)
            score_row(NBLK - 2)
            score_row(NBLK - 1)
            pe.wait_ge(S("yT_ready"), NT // 2)
            pe.wait_ge(S("mem_w_loaded"), 16 * 7)
            for n in range(NBLK):
                for k in range(KD):
                    m = pe.matmul(bank[n][0:SD, :], mem_q_w[:, k, :], featT[:, k, n * BLK:(n + 1) * BLK], start=(k == 0), stop=(k == KD - 1))
                m.then_inc(S("q_mem_mm"), 1)
            pe.wait_ge(S("s_col_ready"), B)
            pe.wait_ge(dve_once, at("cols_set"))
            for b in range(B):
                for k in range(TB - 1):
                    pe.wait_ge(S("rank_counted"), 2 * (b * TB + k) + 1)
                    for j in range(k + 1, TB):
                        m = pe.matmul(bank[7][:, b * TB + j:b * TB + j + 1], greater[:, k % 2, j * P:(j + 1) * P], ones_bf[:, 0:1],
                                      start=(k == 0 and j == 1), stop=(k == j - 1), skip_group_check=True)
                    m.then_inc(S("rank_cols"), 1)
            pe.matmul(bank[6][:, 0:NT], ones[:, :], s_col, start=True, stop=True).then_inc(pe_once, reached("mean_mm"))
            pe.wait_ge(S("y_tok_ready"), NT)
            pe.wait_ge(dve_once, at("mean_ready_1"))
            pe.wait_ge(S("q_mem_ready"), NBLK)
            for b in range(B):
                pe.wait_ge(S("onehot_ready"), b + 1)
                for k in range(TB):
                    pe.matmul(mem_bank[b][1][0:POOL, 0:D], onehot[:, b * TB + k, :], y_tok[:, b * TB + k, :], start=(k == 0), stop=(k == TB - 1))
                for k in range(TB):
                    m = pe.matmul(mem_bank[b][2][:, 0:POOL], ones[:, :], onehot[:, b * TB + k, :], start=(k == 0), stop=(k == TB - 1))
                m.then_inc(S("select_mm"), 1)
            pe.wait_ge(pool_once, at("masks_set_3"))
            pe.wait_ge(S("mem_w_loaded"), 16 * 7)
            for b in range(B):
                pe.wait_ge(S("pool_tok_ready"), b + 1)
                for k in range(KD):
                    m = pe.transpose(mem_bank[b][0][:, k * POOL:(k + 1) * POOL], pool_tok[0:POOL, b, k * P:(k + 1) * P], ident[0:POOL, 0:POOL])
                m.then_inc(S("pool_tok_turned"), 1)
            for b in range(B):
                pe.wait_ge(S("pool_tokT_ready"), b + 1)
                for k in range(KD):
                    m = pe.matmul(mem_bank[b][1][0:SD, 0:POOL], summ_w[:, k, :], pool_tokT[:, b, k, :], start=(k == 0), stop=(k == KD - 1))
                m.then_inc(S("pool_mm"), 1)
            for b in range(B):
                pe.wait_ge(S("poolT_ready"), b + 1)
                pe.matmul(mem_bank[b][0][0:SD, 0:POOL], mem_k_w[:, :], poolT[0:SD, b, :], start=True, stop=True).then_inc(S("key_mm"), 1)
                pe.wait_ge(S("vbias_ready"), b + 1)
                pe.matmul(mem_bank[b][2][0:POOL, 0:D], poolT[0:SD, b, :], mem_v_w[:, :], start=True, stop=True).then_inc(S("val_mm"), 1)

            def logits_of(n):
                b = n // (T // BLK)
                pe.wait_ge(S("q_now_ready"), n + 1)
                for i in range(4):
                    m = pe.matmul(bank[1][:, i * 64:i * 64 + POOL], q_now[0:SD, i * P:(i + 1) * P],
                                  keyT[0:SD, ds(b, 1), :].rearrange("p a n -> p (a n)"), start=True, stop=True)
                m.then_inc(S("logit_mm"), 1)

            def gate(n, m_, ks):
                for k in ks:
                    side = featT[:, k, ds(n * BLK, BLK)] if k < KD else retT[:, k - KD, :]
                    m = pe.matmul(bank[5 + m_][:, :], gate_w[:, k, m_ * P:(m_ + 1) * P], side, start=(k == 0), stop=(k == 2 * KD - 1))
                return m

            def retrieve(n, nxt=True):
                pe.wait_ge(S("attn_ready"), n + 1)
                gate(n, 0, range(KD))
                for i in range(4):
                    m = pe.transpose(bank[2][0:POOL, i * P:(i + 1) * P], logit[:, i, :], ident[:, :])
                m.then_inc(S("attn_turned"), 1)
                pe.wait_ge(S("attnT_ready"), n + 1)
                pe.wait_ge(S("val_now_ready"), n + 1)
                for m_ in range(KD):
                    pe.matmul(bank[3 + m_][:, :], val_now[0:POOL, m_ * P:(m_ + 1) * P], attnT[0:POOL, :], start=True, stop=True
                              ).then_inc(S("ret_mm"), 1)
                if nxt:
                    logits_of(n + 1)
                pe.wait_ge(S("retT_ready"), KD * n + KD)
                gate(n, 0, range(KD, 2 * KD)).then_inc(S("gate_mm"), 1)
                gate(n, 1, range(2 * KD)).then_inc(S("gate_mm"), 1)
                pe.wait_ge(S("x1_ready"), 2 * n)
                for m_ in range(2):
                    pe.wait_ge(S("upd_ready"), KD * n + KD)
                    for i in range(2):
                        for k in range(KD):
                            m = pe.transpose(bank[7 * (1 - m_)][:, (2 * i + k) * P:(2 * i + k + 1) * P],
                                             upd[:, k, (2 * m_ + i) * P:(2 * m_ + i + 1) * P], ident[:, :])
                    m.then_inc(S("upd_turned"), 1)

            pe.wait_ge(S("keyT_ready"), B)
            pe.wait_ge(S("val_ready"), B)
            logits_of(0)
            with pe.Fori(0, NBLK - 1) as n:
                retrieve(n)
            retrieve(NBLK - 1, False)

            pe.wait_ge(S("x_w_loaded"), 16 * 9)
            pe.wait_ge(pool_once, at("bias_rows_cleared_2"))
            for n in range(2):
                m = pe.transpose(bank[2][:, n * NG:(n + 1) * NG], bias_rows[:, n, :, :].rearrange("g h c -> g (h c)"), ident[0:NG, 0:NG])
            m.then_inc(pe_once, reached("bias_turned"))
            pe.wait_ge(S("pads_ready"), 4)
            pe.wait_ge(dve_once, at("mask_row_ready"))
            for b in range(B):
                for g in range(NG):
                    n = NG * b + g
                    if n >= 2:
                        pe.wait_ge(S("keys_ready"), n - 1)
                    for k in range(KD):
                        pe.matmul(bank[3 + n % 2][:, 0:LK], wk_pad[:, k, g * P:(g + 1) * P], ctxT[:, b, k, :], start=(k == 0), stop=False)
                    pe.matmul(bank[3 + n % 2][:, 0:LK], mask_sel[:, :], mask_row[:, b * LK:(b + 1) * LK], start=False, stop=True
                              ).then_inc(S("keys_mm"), 1)
                if b:
                    pe.wait_ge(S("v_main_ready"), b)
                    pe.wait_ge(S("v_tail_ready"), b)
                for dst, lhs, rows, done in ((bank[5], ctxT[:, b, :, 0:KM], KM, "val_main_mm"), (bank[6], tail_ctx[:, b, :, :], P, "val_tail_mm")):
                    for k in range(KD):
                        pe.matmul(dst[0:rows, 0:D], lhs[:, k, :], wv[:, k, :], start=(k == 0), stop=False)
                    pe.matmul(dst[0:rows, 0:D], ones[0:1, 0:rows], vb_row[:, :], start=False, stop=True).then_inc(S(done), 1)
            for t in range(NT):
                pe.wait_ge(S("ln2_ready"), t + 1)
                if t % 2 == 0 and t >= 4:
                    pe.wait_ge(S("hT_ready"), t // 2 - 1)
                for k in range(KD):
                    m = pe.transpose(bank[(t // 2) % 2][:, (t % 2) * D + k * P:(t % 2) * D + (k + 1) * P],
                                     st4[:, t % GT, k * P:(k + 1) * P], ident[:, :])
                if t % 2:
                    m.then_inc(S("ln2_turned"), 1)
            pe.wait_ge(S("hT_ready"), NT // 2)
            pe.wait_ge(S("keys_ready"), B * NG)
            pe.wait_ge(S("v_main_ready"), B)
            pe.wait_ge(S("v_tail_ready"), B)

            keys_of = keys.rearrange("p b g n -> p (b g) n")
            vt_of = v_tail.rearrange("p b g n -> p (b g) n")
            vm_of = v_main.rearrange("p b h n -> p (b h) n")
            W = HD + 1

            def queries(t):
                for g in range(NG):
                    for k in range(KD):
                        m = pe.matmul(bank[5][:, g * P:(g + 1) * P], wq_pad[:, k, g * P:(g + 1) * P], featT[:, k, ds(t * P, P)],
                                      start=(k == 0), stop=(k == KD - 1))
                m.then_inc(S("q_mm"), 1)

            def scores(t, p, g, waits):
                if waits:
                    pe.wait_ge(S("shifted"), NG * t + g - 1)
                if g == 0:
                    pe.wait_ge(S("qT_ready"), t + 1)
                for j in range(2):
                    m = pe.matmul(pair[g % 2][:, j, 0:2 * LK], qT[:, p, g, :],
                                  keys_of[:, :, 2 * j * LK:(2 * j + 2) * LK][:, ds((t // TB) * NG + g, 1), :].rearrange("p a n -> p (a n)"),
                                  start=True, stop=True)
                m.then_inc(S("score_x_mm"), 1)

            def turn_probs(t, p, g, waits):
                if g < NG:
                    pe.wait_ge(S("prob_ready"), NG * t + g + 1)
                if waits or g >= 1:
                    pe.wait_ge(S("probT_ready"), (NG + 1) * t + (-1, 1, 0, 2, 3)[g])
                for h in range(GH):
                    if g < NG:
                        m = pe.transpose(bank[TURN_BANK[g]][0:KM, h * P:(h + 1) * P], prob_m[p][:, GH * g + h, :], ident[:, :])
                    else:
                        m = pe.transpose(bank[TURN_BANK[g]][:, h * P:(h + 1) * P],
                                         prob_t[p][:, GH * h:GH * (h + 1), :].rearrange("p h n -> p (h n)"), ident[:, :])
                m.then_inc(S("prob_turned"), 1)

            def weigh_main(t, p, g, waits):
                pe.wait_ge(S("probT_ready"), (NG + 1) * t + g + 1)
                if g == 0 and waits:
                    pe.wait_ge(S("head_o_ready"), t - 1)
                for h in range(GH):
                    hh = GH * g + h
                    m = pe.matmul(bank[6 + p][:, hh * W:(hh + 1) * W], probT[0:KM, hh, :],
                                  vm_of[0:KM, ds((t // TB) * XH + hh, 1), :].rearrange("p a n -> p (a n)"), start=(hh == 0), stop=False,
                                  skip_group_check=True)
                m.then_inc(S("pv_mm"), 1)

            def weigh_tail(t, p):
                pe.wait_ge(S("probT_ready"), (NG + 1) * (t + 1))
                for g in range(NG):
                    m = pe.matmul(bank[6 + p][:, g * GH * W:(g + 1) * GH * W], probT[:, XH + g, :],
                                  vt_of[:, ds((t // TB) * NG + g, 1), :].rearrange("p a n -> p (a n)"), start=False, stop=True,
                                  skip_group_check=True)
                m.then_inc(S("pv_mm"), 1)

            def tile_step(t, p, now=True, before=True, before2=True, score_waits=True, turn_waits=True, pv_waits=True, nxt=True):
                for g in range(NG):
                    if now:
                        scores(t, p, g, score_waits or g > 1)
                    if nxt and g == 1:
                        if before and turn_waits:
                            pe.wait_ge(S("probT_ready"), (NG + 1) * (t - 1))
                        queries(t + 1)
                    if before:
                        if nxt and g == 2:
                            pe.wait_ge(S("qT_ready"), t + 2)
                        turn_probs(t - 1, 1 - p, g, turn_waits)
                    if before2 and g == 0:
                        weigh_main(t - 2, p, NG - 1, pv_waits)
                        weigh_tail(t - 2, p)
                    if before and g:
                        weigh_main(t - 1, 1 - p, g - 1, pv_waits)
                if before:
                    turn_probs(t - 1, 1 - p, NG, turn_waits)
            queries(0)
            pe.wait_ge(S("qT_ready"), 1)
            tile_step(0, 0, before=False, before2=False, score_waits=False)
            pe.wait_ge(S("qT_ready"), 2)
            tile_step(1, 1, before2=False, turn_waits=False, pv_waits=False)
            tile_step(2, 0, pv_waits=False)
            tile_step(3, 1)
            with pe.Fori(2, NT // 2 - 1) as i:
                for p in range(2):
                    tile_step(2 * i + p, p)
            tile_step(NT - 2, 0)
            tile_step(NT - 1, 1, nxt=False)
            tile_step(NT, 0, now=False, nxt=False)
            weigh_main(NT - 1, 1, NG - 1, True)
            weigh_tail(NT - 1, 1)

            pe.wait_ge(S("head_o_ready"), NT)
            pe.wait_ge(S("route_w_loaded"), 16 * 3)

            def turn_group(j):
                for q in range(GT):
                    pe.wait_ge(S("x3_ready"), GT * j + q + 1)
                    if j >= 2 and q == 0:
                        pe.wait_ge(S("x3T_ready"), 2 * (j - 1))
                    for k in range(KD):
                        m = pe.transpose(bank[2 * (j % 2) + q // 2][:, (q % 2) * D + k * P:(q % 2) * D + (k + 1) * P],
                                         st4[:, q, k * P:(k + 1) * P], ident[:, :])
                    if q % 2:
                        m.then_inc(S("x3_turned"), 1)

            def route_group(j):
                pe.wait_ge(S("x3T_ready"), 2 * j + 2)
                if j >= 2:
                    pe.wait_ge(S("logits_ready"), j - 1)
                for q in range(GT):
                    for k in range(KD):
                        m = pe.matmul(bank[4 + j % 2][:, q * NE:(q + 1) * NE], x3T[j % 2][:, q, k, :], w_route[:, k, :],
                                      start=(k == 0), stop=(k == KD - 1))
                m.then_inc(S("route_mm"), 1)
            turn_group(0)
            for j in range(1, NT // GT):
                turn_group(j)
                route_group(j - 1)
            route_group(NT // GT - 1)
            pe.wait_ge(S("hot_ready"), 1)
            hot_flat = hot.rearrange("p t e -> p (t e)")
            pe.matmul(bank[4][:, 0:NT * NE], tri_le[:, :], hot_flat, start=True, stop=True).then_inc(pe_once, reached("count_mm_1"))
            pe.matmul(bank[5][:, 0:NT * NE], ones[:, :], hot_flat, start=True, stop=True).then_inc(pe_once, reached("count_mm_2"))
            pe.wait_ge(dve_once, at("block_expert_ready"))

            def turn_rows(n, p):
                pe.wait_ge(S(f"xs_loaded{p}"), 8 * (n - p) + 16)
                pe.wait_ge(S("xsT_ready"), n)
                for k in range(KD):
                    m = pe.transpose(bank[6][:, k * P:(k + 1) * P], xs[:, p, k * P:(k + 1) * P], ident[:, :])
                m.then_inc(S("xs_turned"), 1)

            def up(n, p):
                e = pe.value_load(expert_i[0:1, ds(n, 1)], min_val=0, max_val=NE - 1)
                pe.wait_ge(S("xsT_ready"), n + 1)
                pe.wait_ge(S("h_kept"), 2 * n)
                for f in range(2):
                    for k in range(KD):
                        m = pe.matmul(bank[f][:, :], xsT[:, p, k, :], w1_of[:, ds(e * KD + k, 1), f * 512:(f + 1) * 512].rearrange("p a n -> p (a n)"),
                                      start=(k == 0), stop=(k == KD - 1))
                    m.then_inc(S("up_mm"), 1)

            def turn_hidden(n):
                for half in range(2):
                    pe.wait_ge(S("h_kept"), 2 * n + half + 1)
                    pe.wait_ge(S("hT_half_a" if half == 0 else "hT_half_b"), n)
                    for f in range(4):
                        m = pe.transpose(bank[2 + half][:, f * P:(f + 1) * P], hid_e[:, (4 * half + f) * P:(4 * half + f + 1) * P], ident[:, :])
                    m.then_inc(S("h_turned"), 1)

            def down(n):
                e = pe.value_load(expert_i[0:1, ds(n, 1)], min_val=0, max_val=NE - 1)
                pe.wait_ge(S("yo_ready"), n)
                for f in range(NFF):
                    if f % 4 == 0:
                        pe.wait_ge(S("hT_half_a" if f == 0 else "hT_half_b"), n + 1)
                    m = pe.matmul(bank[4][:, 0:D], hidT[:, f, :], w2_of[:, ds(e * NFF + f, 1), :].rearrange("p a n -> p (a n)"),
                                  start=(f == 0), stop=(f == NFF - 1))
                m.then_inc(S("down_mm"), 1)

            w1_of = w1.rearrange("p e k f -> p (e k) f")
            w2_of = w2.rearrange("p e f d -> p (e f) d")
            pe.wait_ge(S("w1_loaded"), 16 * NE)
            turn_rows(0, 0)
            up(0, 0)
            pe.wait_ge(S("w2_loaded"), 16 * 2 * NE)
            turn_rows(1, 1)

            def step(n, p):
                turn_hidden(n)
                up(n + 1, 1 - p)
                turn_rows(n + 2, p)
                down(n)
            with pe.Fori(0, NB // 2 - 1) as i:
                step(2 * i, 0)
                step(2 * i + 1, 1)
            step(NB - 3, 0)
            turn_hidden(NB - 2)
            up(NB - 1, 0)
            down(NB - 2)
            turn_hidden(NB - 1)
            down(NB - 1)


def layouts(inputs):
    g = {k: np.asarray(v) for k, v in inputs.items()}

    def c(v, *axes):
        return np.ascontiguousarray(v.transpose(*axes) if axes else v)

    def cols(v, *shape):
        return c(v.reshape(-1, P, *shape), 1, 0, *range(2, 2 + len(shape)))
    return {
        "x": c(g["x"]), "ctxT": c(g["ctx_1024"], 0, 2, 1), "mask": c(g["mask_BxS2_ik0"]),
        "attn_norm_w": cols(g["L0_attn_norm_w"]), "attn_in_wT": c(g["L0_attn_in_w"], 1, 0),
        "attn_conv_w": cols(g["L0_attn_conv_w"], TAPS), "attn_conv_b": cols(g["L0_attn_conv_b"]),
        "attn_dt_bias": c(g["L0_attn_dt_bias"]), "attn_A_log": c(g["L0_attn_A_log"]),
        "attn_D_param": c(g["L0_attn_D_param"]), "attn_gnorm_w": cols(g["L0_attn_gnorm_w"]),
        "attn_out_wT": c(g["L0_attn_out_w"], 1, 0), "scorer_w1T": c(g["L0_attn_scorer_w1"], 1, 0),
        "scorer_w2T": c(g["L0_attn_scorer_w2"], 1, 0), "summ_wT": c(g["L0_attn_summ_w"], 1, 0),
        "mem_q_wT": c(g["L0_attn_q_w"], 1, 0), "mem_k_wT": c(g["L0_attn_k_w"], 1, 0),
        "mem_v_wT": c(g["L0_attn_v_w"], 1, 0), "gate_wT": c(g["L0_attn_gate_w"], 1, 0),
        "q_w": c(g["L0_xattn_q_w"], 1, 0), "q_b": c(g["L0_xattn_q_b"]), "k_w": c(g["L0_xattn_k_w"], 1, 0),
        "k_b": c(g["L0_xattn_k_b"]), "v_w": c(g["L0_xattn_v_w"], 1, 0), "v_b": c(g["L0_xattn_v_b"]),
        "WrT": c(g["L0_ffn_Wr"], 1, 0), "br": c(g["L0_ffn_br"]),
        "W1T": c(g["L0_ffn_W1"], 0, 2, 1), "b1": c(g["L0_ffn_b1"].reshape(NE * NFF, P), 1, 0),
        "W2T": c(g["L0_ffn_W2"], 0, 2, 1), "b2": c(g["L0_ffn_b2"]),
    }


def kernel(**inputs):
    import concourse.bacc as bacc
    from concourse.bass_utils import run_bass_kernel_spmd

    nc = bacc.Bacc("TRN2", target_bir_lowering=False, num_devices=1)
    arrays = layouts(inputs)
    dram = {n: nc.dram_tensor(n, v.shape, mybir.dt.from_np(v.dtype), kind="ExternalInput").ap() for n, v in arrays.items()}
    out = nc.dram_tensor("out", (B, T, D), F32, kind="ExternalOutput").ap()
    build(nc, dram, out)
    return run_bass_kernel_spmd(nc, [arrays], core_ids=[0]).results[0]["out"]
```
